# Optimizing a Trainium2 kernel written in Bass

```python
import numpy as np
import jax
import jax.numpy as jnp

def _softmax(x, axis=-1):
    return jax.nn.softmax(x, axis=axis)
def _gelu(x):
    return jax.nn.gelu(x, approximate=True)
def _silu(x):
    return jax.nn.silu(x)
def _sigmoid(x):
    return jax.nn.sigmoid(x)
def _layernorm(x, axis=-1, eps=1e-5):
    m = jnp.mean(x, axis=axis, keepdims=True)
    v = jnp.var(x, axis=axis, keepdims=True)
    return (x - m) / jnp.sqrt(v + eps)
def _scatter_add(tgt, idx, src, axis=0):
    return tgt.at[idx].add(src)
def _segment_sum(src, seg, n):
    return jax.ops.segment_sum(src, seg, n)

kernel_name = 'mk_conv_attn_hybrid_d4_conv_nhwc128_f929b4'

def setup_inputs(seed: int = 0):
    np.random.seed(seed)
    _w = jnp.asarray
    def _rec_inputs():
        import jax
        import jax.numpy as jnp
        _gk = jax.random.key(seed)
        x = -0.0009896 + 1 * jax.random.normal(jax.random.fold_in(_gk, 1), (4, 56, 56, 128), jnp.float32)
        return x
    x = _rec_inputs()
    def _L0_conv_setup():
        import jax, jax.numpy as jnp
        import numpy as np
        DIM = 128
        NUM_HEADS = 4
        HEAD_DIM = DIM // NUM_HEADS
        KSIZE = 7
        DILATION = 1
        SCALE = HEAD_DIM ** (-0.5)

        def _rpb_bias(rpb):
            coords = np.stack(np.meshgrid(np.arange(KSIZE), np.arange(KSIZE), indexing='ij'))
            coords = coords.reshape(2, -1).T
            rel = coords - KSIZE // 2 + (KSIZE - 1)
            return rpb[:, rel[:, 0], rel[:, 1]]
        key = jax.random.key(seed)
        ks = jax.random.split(key, 6)
        B, H, W = (4, 56, 56)
        x = jax.random.normal(ks[0], (B, H, W, DIM), dtype=jnp.float32)
        qkv_w = jax.random.normal(ks[1], (3 * DIM, DIM), dtype=jnp.float32) * 0.02
        qkv_b = jnp.zeros((3 * DIM,), dtype=jnp.float32)
        rpb = jax.random.normal(ks[2], (NUM_HEADS, 2 * KSIZE - 1, 2 * KSIZE - 1), dtype=jnp.float32) * 0.02
        proj_w = jax.random.normal(ks[3], (DIM, DIM), dtype=jnp.float32) * 0.02
        proj_b = jnp.zeros((DIM,), dtype=jnp.float32)
        return {'x': x, 'qkv_w': qkv_w, 'qkv_b': qkv_b, 'rpb': rpb, 'proj_w': proj_w, 'proj_b': proj_b}
    _L0_conv_all = _L0_conv_setup()
    _L0_conv_in = {k: v for k, v in _L0_conv_all.items() if k in ('qkv_w', 'qkv_b', 'rpb', 'proj_w', 'proj_b', )}
    del _L0_conv_all

    def _L1_conv_setup():
        import jax, jax.numpy as jnp
        import numpy as np
        import math
        D_MODEL = 128
        D_STATE = 16
        D_CONV = 3
        EXPAND = 2
        D_INNER = EXPAND * D_MODEL
        DT_RANK = math.ceil(D_MODEL / 16)
        B, H, W = (2, 64, 64)
        LN_EPS = 1e-05

        def _local_scan(x, Hh, Ww, w_h, w_w, flip=False, column_first=False):
            Bb, C = (x.shape[0], x.shape[1])
            Hg, Wg = (Hh // w_h, Ww // w_w)
            x = x.reshape(Bb, C, Hg, w_h, Wg, w_w)
            if column_first:
                x = x.transpose(0, 1, 4, 2, 5, 3)
            else:
                x = x.transpose(0, 1, 2, 4, 3, 5)
            x = x.reshape(Bb, C, -1)
            if flip:
                x = x[:, :, ::-1]
            return x

        def _selective_scan(u, delta, A, Bm, Cm, D, delta_bias):
            Bsz, Dch, L = u.shape
            K, N = (Bm.shape[1], A.shape[1])
            d = Dch // K
            delta = jax.nn.softplus(delta + delta_bias[None, :, None])
            A4 = A.reshape(K, d, N)
            u4 = u.reshape(Bsz, K, d, L)
            dt4 = delta.reshape(Bsz, K, d, L)

            def step(h, inp):
                ut, dt, bt, ct = inp
                dA = jnp.exp(dt[..., None] * A4)
                h = dA * h + (dt * ut)[..., None] * bt[:, :, None, :]
                y = jnp.einsum('bkdn,bkn->bkd', h, ct)
                return (h, y)
            xs_t = (u4.transpose(3, 0, 1, 2), dt4.transpose(3, 0, 1, 2), Bm.transpose(3, 0, 1, 2), Cm.transpose(3, 0, 1, 2))
            h0 = jnp.zeros((Bsz, K, d, N), u.dtype)
            _, ys = jax.lax.scan(step, h0, xs_t)
            y = ys.transpose(1, 2, 3, 0).reshape(Bsz, Dch, L)
            return y + u * D[None, :, None]
        key = jax.random.key(seed)
        ks = jax.random.split(key, 8)
        x = jax.random.normal(ks[0], (B, H, W, D_MODEL), jnp.float32)
        W_in = jax.random.normal(ks[1], (2 * D_INNER, D_MODEL), jnp.float32) * D_MODEL ** (-0.5)
        conv_w = jax.random.normal(ks[2], (D_INNER, 1, D_CONV, D_CONV), jnp.float32) * (1.0 / D_CONV)
        conv_b = jnp.zeros((D_INNER,), jnp.float32)
        x_proj_w = jax.random.normal(ks[3], (4, DT_RANK + 2 * D_STATE, D_INNER), jnp.float32) * D_INNER ** (-0.5)
        std = DT_RANK ** (-0.5)
        dt_proj_w = jax.random.uniform(ks[4], (4, D_INNER, DT_RANK), jnp.float32, -std, std)
        dt = jnp.exp(jax.random.uniform(ks[5], (4, D_INNER), jnp.float32) * (math.log(0.1) - math.log(0.001)) + math.log(0.001))
        dt = jnp.maximum(dt, 0.0001)
        dt_proj_b = dt + jnp.log(-jnp.expm1(-dt))
        A_logs = jnp.log(jnp.tile(jnp.arange(1, D_STATE + 1, dtype=jnp.float32)[None, :], (4 * D_INNER, 1)))
        Ds = jnp.ones((4 * D_INNER,), jnp.float32)
        ln_w = jnp.ones((D_INNER,), jnp.float32)
        ln_b = jnp.zeros((D_INNER,), jnp.float32)
        W_out = jax.random.normal(ks[6], (D_MODEL, D_INNER), jnp.float32) * D_INNER ** (-0.5)
        return dict(x=x, W_in=W_in, conv_w=conv_w, conv_b=conv_b, x_proj_w=x_proj_w, dt_proj_w=dt_proj_w, dt_proj_b=dt_proj_b, A_logs=A_logs, Ds=Ds, ln_w=ln_w, ln_b=ln_b, W_out=W_out)
    _L1_conv_all = _L1_conv_setup()
    _L1_conv_in = {k: v for k, v in _L1_conv_all.items() if k in ('W_in', 'conv_w', 'conv_b', 'x_proj_w', 'dt_proj_w', 'dt_proj_b', 'A_logs', 'Ds', 'ln_w', 'ln_b', 'W_out', )}
    del _L1_conv_all

    def _L2_attn_setup():
        import jax, jax.numpy as jnp
        import numpy as np
        NEG = -1000000000000.0
        key = jax.random.key(seed)
        k1, k2, k3, k4 = jax.random.split(key, 4)
        B, T, D, U = (4, 4096, 128, 128)
        query = jax.random.normal(k1, (B, T, D), dtype=jnp.float32)
        s = 1.0 / np.sqrt(D)
        Wq = jax.random.normal(k2, (D, U), dtype=jnp.float32) * s
        Wk = jax.random.normal(k3, (D, U), dtype=jnp.float32) * s
        Wv = jax.random.normal(k4, (D, U), dtype=jnp.float32) * s
        return {'query': query, 'Wq': Wq, 'Wk': Wk, 'Wv': Wv}
    _L2_attn_all = _L2_attn_setup()
    _L2_attn_in = {k: v for k, v in _L2_attn_all.items() if k in ('Wq', 'Wk', 'Wv', )}
    del _L2_attn_all

    def _L2_ffn_setup():
        import jax, jax.numpy as jnp
        import numpy as np
        B, N, D, C, E, K = (8, 8192, 128, 128, 8, 2)
        key = jax.random.key(seed)
        k0, k1, k2 = jax.random.split(key, 3)
        x = jax.random.normal(k0, (B, N, D), dtype=jnp.float32)
        router_w = jax.random.normal(k1, (D, E), dtype=jnp.float32) * 0.05
        router_b = jnp.zeros((E,), dtype=jnp.float32)
        expert_w = jax.random.normal(k2, (E, D, C), dtype=jnp.float32) * (1.0 / np.sqrt(D))
        expert_b = jnp.zeros((E, C), dtype=jnp.float32)
        return {'x': x, 'router_w': router_w, 'router_b': router_b, 'expert_w': expert_w, 'expert_b': expert_b}
    _L2_ffn_all = _L2_ffn_setup()
    _L2_ffn_in = {k: v for k, v in _L2_ffn_all.items() if k in ('router_w', 'router_b', 'expert_w', 'expert_b', )}
    del _L2_ffn_all

    def _L3_attn_setup():
        import jax, jax.numpy as jnp
        import numpy as np
        B, T, C = (4096, 64, 128)
        N_HEAD = 8
        D_HEAD = C // N_HEAD
        key = jax.random.key(seed)
        k1, k2, k3 = jax.random.split(key, 3)
        x = jax.random.normal(k1, (B, T, C), dtype=jnp.float32)
        w_attn = jax.random.normal(k2, (C, 3 * C), dtype=jnp.float32) * 0.02
        w_proj = jax.random.normal(k3, (C, C), dtype=jnp.float32) * 0.02
        return {'x': x, 'w_attn': w_attn, 'w_proj': w_proj}
    _L3_attn_all = _L3_attn_setup()
    _L3_attn_in = {k: v for k, v in _L3_attn_all.items() if k in ('w_attn', 'w_proj', )}
    del _L3_attn_all

    def _L3_ffn_setup():
        import jax, jax.numpy as jnp
        import numpy as np
        BN_EPS = 1e-05
        key = jax.random.key(seed)
        k1, k2, k3 = jax.random.split(key, 3)
        B, T, I, H = (64, 2048, 128, 128)
        x = jax.random.normal(k1, (B, T, I), dtype=jnp.float32)
        W = jax.random.normal(k2, (H, I), dtype=jnp.float32) * (1.0 / np.sqrt(I))
        V = jnp.linalg.qr(jax.random.normal(k3, (H, H), dtype=jnp.float32))[0]
        gamma = jnp.ones((H,), dtype=jnp.float32)
        beta = jnp.zeros((H,), dtype=jnp.float32)
        return {'x': x, 'W': W, 'V': V, 'gamma': gamma, 'beta': beta}
    _L3_ffn_all = _L3_ffn_setup()
    _L3_ffn_in = {k: v for k, v in _L3_ffn_all.items() if k in ('W', 'V', 'gamma', 'beta', )}
    del _L3_ffn_all

    return {
        "x": x,
        "L0_conv_qkv_w": _L0_conv_in["qkv_w"],
        "L0_conv_qkv_b": _L0_conv_in["qkv_b"],
        "L0_conv_rpb": _L0_conv_in["rpb"],
        "L0_conv_proj_w": _L0_conv_in["proj_w"],
        "L0_conv_proj_b": _L0_conv_in["proj_b"],
        "L1_conv_W_in": _L1_conv_in["W_in"],
        "L1_conv_conv_w": _L1_conv_in["conv_w"],
        "L1_conv_conv_b": _L1_conv_in["conv_b"],
        "L1_conv_x_proj_w": _L1_conv_in["x_proj_w"],
        "L1_conv_dt_proj_w": _L1_conv_in["dt_proj_w"],
        "L1_conv_dt_proj_b": _L1_conv_in["dt_proj_b"],
        "L1_conv_A_logs": _L1_conv_in["A_logs"],
        "L1_conv_Ds": _L1_conv_in["Ds"],
        "L1_conv_ln_w": _L1_conv_in["ln_w"],
        "L1_conv_ln_b": _L1_conv_in["ln_b"],
        "L1_conv_W_out": _L1_conv_in["W_out"],
        "L2_attn_Wq": _L2_attn_in["Wq"],
        "L2_attn_Wk": _L2_attn_in["Wk"],
        "L2_attn_Wv": _L2_attn_in["Wv"],
        "L2_ffn_router_w": _L2_ffn_in["router_w"],
        "L2_ffn_router_b": _L2_ffn_in["router_b"],
        "L2_ffn_expert_w": _L2_ffn_in["expert_w"],
        "L2_ffn_expert_b": _L2_ffn_in["expert_b"],
        "L3_attn_w_attn": _L3_attn_in["w_attn"],
        "L3_attn_w_proj": _L3_attn_in["w_proj"],
        "L3_ffn_W": _L3_ffn_in["W"],
        "L3_ffn_V": _L3_ffn_in["V"],
        "L3_ffn_gamma": _L3_ffn_in["gamma"],
        "L3_ffn_beta": _L3_ffn_in["beta"],
    }

def reference(x, L0_conv_qkv_w, L0_conv_qkv_b, L0_conv_rpb, L0_conv_proj_w, L0_conv_proj_b, L1_conv_W_in, L1_conv_conv_w, L1_conv_conv_b, L1_conv_x_proj_w, L1_conv_dt_proj_w, L1_conv_dt_proj_b, L1_conv_A_logs, L1_conv_Ds, L1_conv_ln_w, L1_conv_ln_b, L1_conv_W_out, L2_attn_Wq, L2_attn_Wk, L2_attn_Wv, L2_ffn_router_w, L2_ffn_router_b, L2_ffn_expert_w, L2_ffn_expert_b, L3_attn_w_attn, L3_attn_w_proj, L3_ffn_W, L3_ffn_V, L3_ffn_gamma, L3_ffn_beta):
    import jax
    import jax.numpy as jnp
    def _L0_conv_ref(x, qkv_w, qkv_b, rpb, proj_w, proj_b):
        import jax, jax.numpy as jnp
        import numpy as np
        DIM = 128
        NUM_HEADS = 4
        HEAD_DIM = DIM // NUM_HEADS
        KSIZE = 7
        DILATION = 1
        SCALE = HEAD_DIM ** (-0.5)

        def _rpb_bias(rpb):
            coords = np.stack(np.meshgrid(np.arange(KSIZE), np.arange(KSIZE), indexing='ij'))
            coords = coords.reshape(2, -1).T
            rel = coords - KSIZE // 2 + (KSIZE - 1)
            return rpb[:, rel[:, 0], rel[:, 1]]
        B, H, W, C = x.shape
        qkv = x @ qkv_w.T + qkv_b
        qkv = qkv.reshape(B, H, W, 3, NUM_HEADS, HEAD_DIM).transpose(3, 0, 4, 1, 2, 5)
        q, k, v = (qkv[0], qkv[1], qkv[2])
        pad = KSIZE // 2 * DILATION
        kp = jnp.pad(k, ((0, 0), (0, 0), (pad, pad), (pad, pad), (0, 0)))
        vp = jnp.pad(v, ((0, 0), (0, 0), (pad, pad), (pad, pad), (0, 0)))
        off = jnp.arange(0, KSIZE * DILATION, DILATION)
        idx_i = jnp.arange(H)[:, None] + off[None, :]
        idx_j = jnp.arange(W)[:, None] + off[None, :]
        Ai = idx_i[:, None, :, None]
        Aj = idx_j[None, :, None, :]
        k_win = kp[:, :, Ai, Aj, :].reshape(B, NUM_HEADS, H, W, KSIZE * KSIZE, HEAD_DIM)
        v_win = vp[:, :, Ai, Aj, :].reshape(B, NUM_HEADS, H, W, KSIZE * KSIZE, HEAD_DIM)
        bias = _rpb_bias(rpb)
        attn = jnp.einsum('bnhwd,bnhwkd->bnhwk', q, k_win) * SCALE
        attn = attn + bias[None, :, None, None, :]
        attn = jax.nn.softmax(attn, axis=-1)
        out = jnp.einsum('bnhwk,bnhwkd->bnhwd', attn, v_win)
        out = out.transpose(0, 2, 3, 1, 4).reshape(B, H, W, C)
        return out @ proj_w.T + proj_b

    def _L1_conv_ref(x, W_in, conv_w, conv_b, x_proj_w, dt_proj_w, dt_proj_b, A_logs, Ds, ln_w, ln_b, W_out):
        import jax, jax.numpy as jnp
        import numpy as np
        import math
        D_MODEL = 128
        D_STATE = 16
        D_CONV = 3
        EXPAND = 2
        D_INNER = EXPAND * D_MODEL
        DT_RANK = math.ceil(D_MODEL / 16)
        B, H, W = (2, 64, 64)
        LN_EPS = 1e-05

        def _local_scan(x, Hh, Ww, w_h, w_w, flip=False, column_first=False):
            Bb, C = (x.shape[0], x.shape[1])
            Hg, Wg = (Hh // w_h, Ww // w_w)
            x = x.reshape(Bb, C, Hg, w_h, Wg, w_w)
            if column_first:
                x = x.transpose(0, 1, 4, 2, 5, 3)
            else:
                x = x.transpose(0, 1, 2, 4, 3, 5)
            x = x.reshape(Bb, C, -1)
            if flip:
                x = x[:, :, ::-1]
            return x

        def _selective_scan(u, delta, A, Bm, Cm, D, delta_bias):
            Bsz, Dch, L = u.shape
            K, N = (Bm.shape[1], A.shape[1])
            d = Dch // K
            delta = jax.nn.softplus(delta + delta_bias[None, :, None])
            A4 = A.reshape(K, d, N)
            u4 = u.reshape(Bsz, K, d, L)
            dt4 = delta.reshape(Bsz, K, d, L)

            def step(h, inp):
                ut, dt, bt, ct = inp
                dA = jnp.exp(dt[..., None] * A4)
                h = dA * h + (dt * ut)[..., None] * bt[:, :, None, :]
                y = jnp.einsum('bkdn,bkn->bkd', h, ct)
                return (h, y)
            xs_t = (u4.transpose(3, 0, 1, 2), dt4.transpose(3, 0, 1, 2), Bm.transpose(3, 0, 1, 2), Cm.transpose(3, 0, 1, 2))
            h0 = jnp.zeros((Bsz, K, d, N), u.dtype)
            _, ys = jax.lax.scan(step, h0, xs_t)
            y = ys.transpose(1, 2, 3, 0).reshape(Bsz, Dch, L)
            return y + u * D[None, :, None]
        Bb, Hh, Ww, _ = x.shape
        L = Hh * Ww
        d_inner = conv_b.shape[0]
        dt_rank = dt_proj_w.shape[2]
        N = A_logs.shape[1]
        xz = x @ W_in.T
        xc, z = jnp.split(xz, 2, axis=-1)
        xc = xc.transpose(0, 3, 1, 2)
        xc = jax.lax.conv_general_dilated(xc, conv_w, (1, 1), ((1, 1), (1, 1)), dimension_numbers=('NCHW', 'OIHW', 'NCHW'), feature_group_count=d_inner) + conv_b[None, :, None, None]
        xc = jax.nn.silu(xc)
        w_h, w_w = (Hh // 4, Ww // 4)
        x1 = _local_scan(xc, Hh, Ww, w_h, w_w)
        x2 = _local_scan(xc, Hh, Ww, w_h, w_w, column_first=True)
        x3 = _local_scan(xc, Hh, Ww, w_h, w_w, flip=True)
        x4 = _local_scan(xc, Hh, Ww, w_h, w_w, column_first=True, flip=True)
        xs = jnp.stack([x1, x2, x3, x4], axis=1)
        x_dbl = jnp.einsum('bkdl,kcd->bkcl', xs, x_proj_w)
        dts, Bs, Cs = jnp.split(x_dbl, [dt_rank, dt_rank + N], axis=2)
        dts = jnp.einsum('bkrl,kdr->bkdl', dts, dt_proj_w)
        u = xs.reshape(Bb, -1, L)
        delta = dts.reshape(Bb, -1, L)
        As = -jnp.exp(A_logs)
        out_y = _selective_scan(u, delta, As, Bs, Cs, Ds, dt_proj_b.reshape(-1)).reshape(Bb, 4, -1, L)
        inv_y = out_y[:, 2:4, :, ::-1]
        wh_y = out_y[:, 1].reshape(Bb, -1, Ww, Hh).transpose(0, 1, 3, 2).reshape(Bb, -1, L)
        invwh_y = inv_y[:, 1].reshape(Bb, -1, Ww, Hh).transpose(0, 1, 3, 2).reshape(Bb, -1, L)
        y = out_y[:, 0] + inv_y[:, 0] + wh_y + invwh_y
        y = y.transpose(0, 2, 1).reshape(Bb, Hh, Ww, -1)
        mu = jnp.mean(y, axis=-1, keepdims=True)
        var = jnp.mean(jnp.square(y - mu), axis=-1, keepdims=True)
        y = (y - mu) * jax.lax.rsqrt(var + LN_EPS) * ln_w + ln_b
        y = y * jax.nn.silu(z)
        return y @ W_out.T

    def _L2_attn_ref(query, Wq, Wk, Wv):
        import jax, jax.numpy as jnp
        import numpy as np
        NEG = -1000000000000.0
        q = jnp.einsum('btd,du->btu', query, Wq)
        k = jnp.einsum('btd,du->btu', query, Wk)
        v = jnp.einsum('btd,du->btu', query, Wv)
        T = v.shape[1]
        scores = jnp.einsum('bqu,bku->bqk', q, k) / jnp.sqrt(jnp.asarray(T, jnp.float32))
        causal = jnp.tril(jnp.ones((T, T), dtype=jnp.float32))
        scores = scores + NEG * (1.0 - causal)
        attn = jax.nn.softmax(scores, axis=-1)
        context = jnp.einsum('bqk,bku->bqu', attn, v)
        return context

    def _L2_ffn_ref(x, router_w, router_b, expert_w, expert_b):
        import jax, jax.numpy as jnp
        import numpy as np
        B, N, D, C, E, K = (8, 8192, 128, 128, 8, 2)
        router_probs = jax.nn.softmax(x @ router_w + router_b, axis=-1)
        top_p, top_i = jax.lax.top_k(router_probs, K)
        top_p = top_p / jnp.sum(top_p, axis=-1, keepdims=True)
        expert_out = jnp.einsum('bnd,edc->bnec', x, expert_w) + expert_b
        gathered = jnp.take_along_axis(expert_out, top_i[..., None], axis=2)
        return jnp.einsum('bnk,bnkc->bnc', top_p, gathered)

    def _L3_attn_ref(x, w_attn, w_proj):
        import jax, jax.numpy as jnp
        import numpy as np
        B, T, C = (4096, 64, 128)
        N_HEAD = 8
        D_HEAD = C // N_HEAD
        Bt, Tt, Ct = x.shape
        qkv = x @ w_attn
        q, k, v = jnp.split(qkv, 3, axis=-1)
        q = q.reshape(Bt, Tt, N_HEAD, D_HEAD)
        k = k.reshape(Bt, Tt, N_HEAD, D_HEAD)
        v = v.reshape(Bt, Tt, N_HEAD, D_HEAD)
        scale = 1.0 / jnp.sqrt(jnp.float32(D_HEAD))
        att = jnp.einsum('bqhd,bkhd->bhqk', q, k) * scale
        causal = jnp.tril(jnp.ones((Tt, Tt), dtype=bool))
        att = jnp.where(causal[None, None, :, :], att, -jnp.inf)
        att = jax.nn.softmax(att, axis=-1)
        out = jnp.einsum('bhqk,bkhd->bqhd', att, v).reshape(Bt, Tt, Ct)
        return out @ w_proj

    def _L3_ffn_ref(x, W, V, gamma, beta):
        import jax, jax.numpy as jnp
        import numpy as np
        BN_EPS = 1e-05
        B, T, H = (x.shape[0], x.shape[1], W.shape[0])
        Wx = jnp.einsum('bti,hi->bth', x, W)
        flat = Wx.reshape(B * T, H)
        mean = jnp.mean(flat, axis=0)
        var = jnp.var(flat, axis=0)
        Wx = ((flat - mean) * jax.lax.rsqrt(var + BN_EPS) * gamma + beta).reshape(B, T, H)
        Vt = V.T

        def step(yt, wx_t):
            yt = jax.nn.sigmoid(wx_t + yt @ Vt)
            return (yt, yt)
        y0 = jnp.zeros((B, H), dtype=Wx.dtype)
        _, ys = jax.lax.scan(step, y0, jnp.swapaxes(Wx, 0, 1))
        return jnp.swapaxes(ys, 0, 1)

    def _gn(v, G=32, eps=1e-5):
        B_, H_, W_, C_ = v.shape
        g = v.reshape(B_, H_, W_, G, C_ // G)
        m = jnp.mean(g, axis=(1, 2, 4), keepdims=True)
        s = jnp.var(g, axis=(1, 2, 4), keepdims=True)
        return ((g - m) / jnp.sqrt(s + eps)).reshape(v.shape)

    def _ln_c(v, eps=1e-6):
        m = jnp.mean(v, axis=-1, keepdims=True)
        s = jnp.var(v, axis=-1, keepdims=True)
        return (v - m) / jnp.sqrt(s + eps)

    def _ln_t(v, eps=1e-5):
        m = jnp.mean(v, axis=-1, keepdims=True)
        s = jnp.var(v, axis=-1, keepdims=True)
        return (v - m) / jnp.sqrt(s + eps)

    def _to_tokens(v):
        B_, H_, W_, C_ = v.shape
        return v.reshape(B_, H_ * W_, C_)
    def _from_tokens(t, like):
        return t.reshape(like.shape)

    x = x + _L0_conv_ref(_gn(x), L0_conv_qkv_w, L0_conv_qkv_b, L0_conv_rpb, L0_conv_proj_w, L0_conv_proj_b)
    x = x + _L1_conv_ref(_gn(x), L1_conv_W_in, L1_conv_conv_w, L1_conv_conv_b, L1_conv_x_proj_w, L1_conv_dt_proj_w, L1_conv_dt_proj_b, L1_conv_A_logs, L1_conv_Ds, L1_conv_ln_w, L1_conv_ln_b, L1_conv_W_out)
    t = _to_tokens(x)
    t = t + _L2_attn_ref(_ln_t(t), L2_attn_Wq, L2_attn_Wk, L2_attn_Wv)
    t = t + _L2_ffn_ref(_ln_t(t), L2_ffn_router_w, L2_ffn_router_b, L2_ffn_expert_w, L2_ffn_expert_b)
    t = t + _L3_attn_ref(_ln_t(t), L3_attn_w_attn, L3_attn_w_proj)
    t = t + _L3_ffn_ref(_ln_t(t), L3_ffn_W, L3_ffn_V, L3_ffn_gamma, L3_ffn_beta)
    x = _from_tokens(t, x)
    return x


_drawn_inputs = setup_inputs


def setup_inputs(seed=0):
    import zlib

    import numpy as np

    out = dict(_drawn_inputs(seed))
    spreads = {'L0_conv_qkv_b': (0.0, 0.1),
     'L0_conv_proj_b': (0.0, 0.1),
     'L1_conv_conv_b': (0.0, 0.1),
     'L1_conv_Ds': (1.0, 0.2),
     'L1_conv_ln_w': (1.0, 0.2),
     'L1_conv_ln_b': (0.0, 0.1),
     'L2_ffn_router_b': (0.0, 0.1),
     'L2_ffn_expert_b': (0.0, 0.1),
     'L3_ffn_gamma': (1.0, 0.6),
     'L3_ffn_beta': (0.0, 0.63)}
    factors = {'L0_conv_rpb': 8.0, 'L3_attn_w_attn': 8.0, 'L3_attn_w_proj': 8.0}
    for name, (base, spread) in spreads.items():
        noise = np.random.default_rng([zlib.crc32(name.encode()), seed]).standard_normal(out[name].shape)
        drawn = base * np.exp(spread * noise) if base else spread * noise
        out[name] = jnp.asarray(drawn.astype(out[name].dtype))
    for name, factor in factors.items():
        out[name] = (out[name] * factor).astype(out[name].dtype)
    return out
```

```python
from contextlib import ExitStack

import concourse.bass as bass
from concourse import mybir

ALU = mybir.AluOpType
ACT = mybir.ActivationFunctionType
AX = mybir.AxisListType
F32 = mybir.dt.float32
BF16 = mybir.dt.bfloat16

C = 128
B = 4
HW = 56
L = HW * HW
T = B * L
TILE = 2 * HW
TPC = 4
CH = TPC * TILE
NCH = T // CH
CPB = L // CH
TPB = L // TILE

NH0, HD0, KS = 4, 32, 7
PAD = KS // 2
WP = HW + 2 * PAD
LP = WP * WP
PAIR = 2 * WP
NPAIR = WP // 2
WIN = 8 * WP
NWIN = WIN // PAIR
NEG = -1.0e30

DI, NS, DTR, ND = 256, 16, 8, 4
CT = DI // C
WS = HW // 4
CS = 2 * WS * WS
NCS = L // CS
RC = CS // HW

NE = 8
NH3, HD3 = 8, 16


def ds(start, size):
    return bass.ds(start, size)


class Chain:

    def __init__(self, eng, sem, base=0):
        self.eng, self.sem, self.base, self.n = eng, sem, base, 0

    def link(self, ins):
        self.n += 1
        ins.then_inc(self.sem, 1)
        self.eng.wait_ge(self.sem, self.base + self.n)


class Sem:

    def __init__(self, s, credit):
        self.s, self.credit = s, credit

    def at(self, n):
        return n + self.credit


class Core:

    def __init__(self, nc, ctx, dram):
        self.nc, self.ctx, self.dram = nc, ctx, dram
        self.handles = []
        self.X, self.N = self.sb("X", [C, T]), None
        self.ident = self.sb("ident", [C, C])
        self.mean_mat = self.sb("mean_mat", [C, C])
        self.gn_nmean, self.gn_rstd = self.sb("gn_nmean", [C, B]), self.sb("gn_rstd", [C, B])
        self.ps = ctx.enter_context(nc.psum_tensor("ps", [128, 8, 512], F32))

    def normed(self):
        if self.N is None:
            self.N = self.sb("N", [C, T + CH])
        return self.N

    def sb(self, name, shape, dt=F32, ctx=None):
        return (ctx or self.ctx).enter_context(self.nc.sbuf_tensor(name, shape, dt))

    def sem(self, name, credit=0):
        handle = self.nc.alloc_semaphore(name=name)
        self.handles.append(handle)
        return Sem(handle, credit)

    def end_phase(self):
        self.nc.clear_and_free_semaphores(self.handles)
        self.nc.all_engine_barrier()
        self.handles = []

    def weights(self, block_sync, pairs, sem):
        for dst, src in pairs:
            block_sync.dma_start(dst, src).then_inc(sem, 16)
        return 16 * len(pairs)


def load_x(k):
    nc, X, ps = k.nc, k.X, k.ps
    src = k.dram["x"].rearrange("(t p) c -> p t c", p=TILE)
    with ExitStack() as ctx:
        xin = k.sb("ld_xin", [TILE, 2, TPC, C], ctx=ctx)
        consts_in, landed = k.sem("ld_consts").s, [k.sem("ld_landed0").s, k.sem("ld_landed1").s]
        turned, copied = [k.sem("ld_turned0").s, k.sem("ld_turned1").s], [k.sem("ld_copied0").s, k.sem("ld_copied1").s]
        with nc.Block() as block:
            @block.sync
            def _(sp):
                sp.dma_start(k.ident[:], k.dram["ident"]).then_inc(consts_in, 16)
                sp.dma_start(k.mean_mat[:], k.dram["mean_mat"]).then_inc(consts_in, 16)
                for s in range(2):
                    sp.dma_start(xin[:, s], src[:, s * TPC:(s + 1) * TPC, :]).then_inc(landed[s], 16)
                with sp.Fori(1, NCH // 2) as i:
                    for s in range(2):
                        sp.wait_ge(turned[s], i)
                        sp.dma_start(xin[:, s], src[:, ds(i * (2 * TPC) + s * TPC, TPC), :]).then_inc(landed[s], 16)

            @block.tensor
            def _(pe):
                pe.wait_ge(consts_in, 32)
                with pe.Fori(0, NCH // 2) as i:
                    for s in range(2):
                        pe.wait_ge(landed[s], i * 16 + 16)
                        pe.wait_ge(copied[s], i + 1)
                        for j in range(TPC):
                            last = nc.tensor.transpose(ps[:, s, j * TILE:(j + 1) * TILE], xin[:, s, j, :],
                                                       k.ident[0:TILE, 0:TILE])
                        last.then_inc(turned[s], 1)

            @block.vector
            def _(dve):
                for s in range(2):
                    dve.sem_inc(copied[s], 1)
                with dve.Fori(0, NCH // 2) as i:
                    for s in range(2):
                        dve.wait_ge(turned[s], i + 1)
                        nc.vector.tensor_copy(X[:, ds(i * (2 * CH) + s * CH, CH)], ps[:, s, 0:CH]).then_inc(copied[s], 1)


def store_x(k):
    nc, X, ps = k.nc, k.X, k.ps
    dst = k.dram["out"].rearrange("(t p) c -> p t c", p=TILE)
    with ExitStack() as ctx:
        xst = k.sb("st_in", [C, 2, CH], ctx=ctx)
        xout = k.sb("st_out", [TILE, 2, TPC, C], ctx=ctx)
        staged, turned, copied, stored = ([k.sem(f"st_{n}{s}").s for s in range(2)]
                                          for n in ("staged", "turned", "copied", "stored"))
        with nc.Block() as block:
            @block.scalar
            def _(act):
                for s in range(2):
                    act.sem_inc(turned[s], 1)
                with act.Fori(0, NCH // 2) as i:
                    for s in range(2):
                        act.wait_ge(turned[s], i + 1)
                        nc.scalar.activation(xst[:, s], X[:, ds(i * (2 * CH) + s * CH, CH)], ACT.Copy).then_inc(staged[s], 1)

            @block.tensor
            def _(pe):
                with pe.Fori(0, NCH // 2) as i:
                    for s in range(2):
                        pe.wait_ge(staged[s], i + 1)
                        pe.wait_ge(copied[s], i + 1)
                        for j in range(TPC):
                            last = nc.tensor.transpose(ps[0:TILE, s, j * C:(j + 1) * C], xst[:, s, j * TILE:(j + 1) * TILE],
                                                       k.ident[:])
                        last.then_inc(turned[s], 1)

            @block.vector
            def _(dve):
                for s in range(2):
                    dve.sem_inc(copied[s], 1)
                    dve.sem_inc(stored[s], 16)
                with dve.Fori(0, NCH // 2) as i:
                    for s in range(2):
                        dve.wait_ge(turned[s], i + 2)
                        dve.wait_ge(stored[s], i * 16 + 16)
                        nc.vector.tensor_copy(xout[:, s], ps[0:TILE, s, :]).then_inc(copied[s], 1)

            @block.sync
            def _(sp):
                with sp.Fori(0, NCH // 2) as i:
                    for s in range(2):
                        sp.wait_ge(copied[s], i + 2)
                        sp.dma_start(dst[:, ds(i * (2 * TPC) + s * TPC, TPC), :], xout[:, s]).then_inc(stored[s], 16)
                for s in range(2):
                    sp.wait_ge(stored[s], 16 * (NCH // 2) + 16)


def gn_stats(k, tag):
    nc, X, ps = k.nc, k.X, k.ps
    with ExitStack() as ctx:
        sb = lambda n, s, dt=F32: k.sb(f"{tag}_{n}", s, dt, ctx)
        sem = lambda n: k.sem(f"{tag}_{n}").s
        stats, mv = sb("stats", [C, NCH * 6]), sb("mv", [C, B, 2])
        moments, grp, gsq, gstd = sb("moments", [C, 2, B]), sb("grp", [C, 2, B]), sb("gsq", [C, B]), sb("gstd", [C, B])
        group_mat = sb("group_mat", [C, C])
        eps = sb("eps", [C, 1])
        mat_in, own, moments_ready, grouped, var_ready, std_ready = (
            sem(n) for n in ("mat_in", "own", "moments_ready", "grouped", "var_ready", "std_ready"))
        with nc.Block() as block:
            @block.sync
            def _(sp):
                sp.dma_start(group_mat[:], k.dram["group_mat"]).then_inc(mat_in, 16)

            @block.vector
            def _(dve):
                with dve.Fori(0, NCH) as i:
                    nc.vector.bn_stats(stats[:, ds(i * 6, 6)], X[:, ds(i * CH, CH)]).then_inc(own, 1)
                dve.wait_ge(own, NCH)
                c = Chain(dve, own, NCH)
                for b in range(B):
                    ins = nc.vector.bn_aggr(mv[:, b, :], stats[:, b * CPB * 6:(b + 1) * CPB * 6])
                    if b < B - 1:
                        ins.then_inc(own, 1)
                        c.n += 1
                c.link(ins)
                c.link(nc.vector.tensor_copy(moments[:, 0, :], mv[:, :, 0]))
                c.link(nc.vector.tensor_tensor(moments[:, 1, :], mv[:, :, 0], mv[:, :, 0], ALU.mult))
                nc.vector.tensor_tensor(moments[:, 1, :], moments[:, 1, :], mv[:, :, 1], ALU.add).then_inc(moments_ready, 1)
                dve.wait_ge(grouped, 1)
                c.link(nc.vector.tensor_copy(grp[:], ps[:, 0, 0:2 * B].rearrange("p (a b) -> p a b", a=2)))
                c.link(nc.vector.tensor_tensor(gsq[:], grp[:, 0, :], grp[:, 0, :], ALU.mult))
                c.link(nc.vector.tensor_tensor(gsq[:], grp[:, 1, :], gsq[:], ALU.subtract))
                nc.vector.tensor_scalar(gsq[:], gsq[:], 1e-5, None, ALU.add).then_inc(var_ready, 1)
                nc.vector.tensor_scalar(k.gn_nmean[:], grp[:, 0, :], -1.0, None, ALU.mult)
                dve.wait_ge(std_ready, 1)
                nc.vector.reciprocal(k.gn_rstd[:], gstd[:])

            @block.tensor
            def _(pe):
                pe.wait_ge(mat_in, 16)
                pe.wait_ge(moments_ready, 1)
                nc.tensor.matmul(ps[:, 0, 0:2 * B], group_mat[:], moments[:].rearrange("p a b -> p (a b)"),
                                 start=True, stop=True).then_inc(grouped, 1)

            @block.scalar
            def _(act):
                act.wait_ge(var_ready, 1)
                nc.scalar.activation(gstd[:], gsq[:], ACT.Sqrt).then_inc(std_ready, 1)


def layer0(k):
    nc, X, ps = k.nc, k.X, k.ps
    with ExitStack() as ctx:
        sb = lambda n, s, dt=F32: k.sb(f"a0_{n}", s, dt, ctx)
        sem = lambda n, credit=0: k.sem(f"a0_{n}", credit)
        wqkv, bqkv = sb("wqkv", [C, 3 * C]), sb("bqkv", [C, 3])
        wproj, bproj = sb("wproj", [C, C]), sb("bproj", [C, 1])
        head_scale = sb("head_scale", [C, NH0])
        bias, wmask = sb("bias", [TILE, NH0, WIN]), sb("wmask", [TILE, WIN])
        xn = sb("xn", [C, CH])
        Q, Kp, Vp = sb("Q", [C, L]), sb("Kp", [C, LP]), sb("Vp", [C, LP])
        vst, V = sb("vst", [C, PAIR]), sb("V", [PAIR, NPAIR, C])
        qh = sb("qh", [C, NH0, TILE])
        scored, P = sb("scored", [TILE, 2, WIN]), sb("P", [TILE, 2, WIN])
        PT = sb("PT", [PAIR, 2, NWIN * TILE])
        rmax, nmax = sb("rmax", [TILE, NH0]), sb("nmax", [TILE, NH0])
        rsum, rinv = sb("rsum", [TILE, NH0]), sb("rinv", [TILE, NH0])
        o, oT = sb("o", [TILE, C]), sb("oT", [C, TILE])
        junk = sb("junk", [1, 1])
        w_in, own = sem("w_in"), sem("own")
        xn_ready, qkv_done, q_out, kv_out = sem("xn_ready"), sem("qkv_done", 1), sem("q_out", 1), sem("kv_out")
        v_staged, v_turned, v_out = sem("v_staged"), sem("v_turned"), sem("v_out", 1)
        qh_ready, s_done, s_read, mx_ready = sem("qh_ready"), sem("s_done", 1), sem("s_read", 2), sem("mx_ready")
        p_ready, p_turned, pt_ready, pv_done = sem("p_ready", 2), sem("p_turned", 2), sem("pt_ready", 2), sem("pv_done", 2)
        o_ready, o_turned, ot_ready, proj_done, x_done = (
            sem(n) for n in ("o_ready", "o_turned", "ot_ready", "proj_done", "x_done"))
        loads = [(wqkv[:], "w0_qkv"), (bqkv[:], "b0_qkv"), (wproj[:], "w0_proj"), (bproj[:], "b0_proj"),
                 (head_scale[:], "head_scale0"), (bias[:], "rpb_laid"), (wmask[:], "wmask")]
        rows = lambda t: t[:].rearrange("p (r w) -> p r w", w=WP)

        with nc.Block() as block:
            @block.sync
            def _(sp):
                for dst, name in loads:
                    sp.dma_start(dst, k.dram[name]).then_inc(w_in.s, 16)

            @block.vector
            def _(dve):
                for q in (s_read, v_out):
                    dve.sem_inc(q.s, q.credit)
                nc.vector.memset(Kp[:], 0.0)
                nc.vector.memset(Vp[:], 0.0)
                dve.wait_ge(w_in.s, 16 * len(loads))
                for h in range(NH0):
                    ins = nc.vector.tensor_tensor(bias[:, h, :], bias[:, h, :], wmask[:], ALU.add)
                ins.then_inc(own.s, 1)
                dve.wait_ge(own.s, 1)
                with dve.Fori(0, B) as b:
                    with dve.Fori(0, CPB) as i:
                        it = b * CPB + i
                        dve.wait_ge(qkv_done.s, qkv_done.at(it * 3))
                        nc.vector.tensor_scalar(xn[:], X[:, ds(b * L + i * CH, CH)], k.gn_nmean[:, ds(b, 1)],
                                                k.gn_rstd[:, ds(b, 1)], ALU.add, ALU.mult).then_inc(xn_ready.s, 1)
                        for j, buf in ((1, Kp), (2, Vp)):
                            dve.wait_ge(qkv_done.s, qkv_done.at(it * 3 + j + 1))
                            nc.vector.tensor_scalar(rows(buf)[:, ds(i * 8 + PAD, 8), PAD:PAD + HW],
                                                    ps[:, j, 0:CH].rearrange("p (r w) -> p r w", w=HW),
                                                    bqkv[:, j:j + 1], None, ALU.add).then_inc(kv_out.s, 1)
                    with dve.Fori(0, NPAIR) as i:
                        dve.wait_ge(v_turned.s, b * NPAIR + i + 1)
                        nc.vector.tensor_copy(V[:, ds(i, 1), :].rearrange("p a c -> p (a c)"), ps[0:PAIR, 3, 0:C]).then_inc(v_out.s, 1)
                    with dve.Fori(0, TPB) as r:
                        it = b * TPB + r
                        n0 = it * NH0
                        dve.wait_ge(q_out.s, q_out.at((b + 1) * CPB))
                        dve.wait_ge(s_done.s, s_done.at(n0))
                        nc.vector.tensor_tensor(qh[:], Q[:, ds(r * TILE, TILE)].unsqueeze(1).to_broadcast([C, NH0, TILE]),
                                                head_scale[:].unsqueeze(2).to_broadcast([C, NH0, TILE]),
                                                ALU.mult).then_inc(qh_ready.s, 1)
                        for h in range(NH0):
                            s, n = h % 2, n0 + h
                            dve.wait_ge(s_done.s, s_done.at(n + 1))
                            dve.wait_ge(p_ready.s, p_ready.at(n - 1))
                            nc.vector.memset(junk[:], 0.0)
                            nc.vector.tensor_tensor_reduce(out=scored[:, s, :], in0=ps[0:TILE, s, 0:WIN], in1=bias[:, h, :],
                                                           scale=1.0, scalar=-3.0e38, op0=ALU.add, op1=ALU.max,
                                                           accum_out=rmax[:, h:h + 1]).then_inc(s_read.s, 1)
                            dve.wait_ge(s_read.s, s_read.at(n + 1))
                            nc.vector.tensor_scalar(nmax[:, h:h + 1], rmax[:, h:h + 1], -1.0, None, ALU.mult).then_inc(mx_ready.s, 1)
                        dve.wait_ge(p_ready.s, p_ready.at(n0 + NH0))
                        nc.vector.reciprocal(rinv[:], rsum[:]).then_inc(own.s, 1)
                        dve.wait_ge(own.s, it + 2)
                        dve.wait_ge(pv_done.s, pv_done.at(n0 + NH0))
                        nc.vector.tensor_tensor(o[:].rearrange("p (h d) -> p h d", h=NH0),
                                                ps[0:TILE, 4, 0:C].rearrange("p (h d) -> p h d", h=NH0),
                                                rinv[:].unsqueeze(2).to_broadcast([TILE, NH0, HD0]), ALU.mult).then_inc(o_ready.s, 1)
                        dve.wait_ge(proj_done.s, it + 1)
                        xs = X[:, ds(b * L + r * TILE, TILE)]
                        nc.vector.scalar_tensor_tensor(xs, ps[:, 6, 0:TILE], bproj[:, 0:1], xs, ALU.add, ALU.add)

            @block.scalar
            def _(act):
                for q in (p_ready, pt_ready, q_out):
                    act.sem_inc(q.s, q.credit)
                act.wait_ge(w_in.s, 16 * len(loads))

                def turned_out(n, s):
                    act.wait_ge(p_turned.s, p_turned.at(n + 1))
                    act.wait_ge(pv_done.s, pv_done.at(n - 1))
                    nc.scalar.activation(PT[:, s, :], ps[0:PAIR, 2 + s, 0:NWIN * TILE], ACT.Copy).then_inc(pt_ready.s, 1)

                with act.Fori(0, B) as b:
                    with act.Fori(0, CPB) as i:
                        act.wait_ge(qkv_done.s, qkv_done.at((b * CPB + i) * 3 + 1))
                        nc.scalar.activation(Q[:, ds(i * CH, CH)], ps[:, 0, 0:CH], ACT.Identity, bias=bqkv[:, 0:1]).then_inc(q_out.s, 1)
                    act.wait_ge(kv_out.s, (b + 1) * (2 * CPB))
                    with act.Fori(0, NPAIR) as i:
                        act.wait_ge(v_out.s, v_out.at(b * NPAIR + i))
                        nc.scalar.activation(vst[:], Vp[:, ds(i * PAIR, PAIR)], ACT.Copy).then_inc(v_staged.s, 1)
                    with act.Fori(0, TPB) as r:
                        it = b * TPB + r
                        for h in range(NH0):
                            s, n = h % 2, it * NH0 + h
                            act.wait_ge(mx_ready.s, n + 1)
                            act.wait_ge(p_turned.s, p_turned.at(n - 1))
                            nc.scalar.activation(P[:, s, :], scored[:, s, :], ACT.Exp, bias=nmax[:, h:h + 1],
                                                 accum_out=rsum[:, h:h + 1]).then_inc(p_ready.s, 1)
                            if h > 0:
                                turned_out(n - 1, 1 - s)
                        turned_out(it * NH0 + NH0 - 1, 1)
                        act.wait_ge(o_turned.s, it + 1)
                        nc.scalar.activation(oT[:], ps[:, 5, 0:TILE], ACT.Copy).then_inc(ot_ready.s, 1)

            @block.tensor
            def _(pe):
                for q in (qkv_done, s_done, p_turned, pv_done):
                    pe.sem_inc(q.s, q.credit)
                pe.wait_ge(w_in.s, 16 * len(loads))

                def scores(it, r, h):
                    n = it * NH0 + h
                    pe.wait_ge(s_read.s, s_read.at(n - 1))
                    nc.tensor.matmul(ps[0:TILE, h % 2, 0:WIN], qh[:, h, :], Kp[:, ds(r * PAIR, WIN)],
                                     start=True, stop=True).then_inc(s_done.s, 1)

                def turn(it, h):
                    s, n = h % 2, it * NH0 + h
                    pe.wait_ge(p_ready.s, p_ready.at(n + 1))
                    pe.wait_ge(pt_ready.s, pt_ready.at(n - 1))
                    for j in range(NWIN):
                        ins = nc.tensor.transpose(ps[0:PAIR, 2 + s, j * TILE:(j + 1) * TILE],
                                                  P[:, s, j * PAIR:(j + 1) * PAIR], k.ident[0:TILE, 0:TILE])
                    ins.then_inc(p_turned.s, 1)

                def weigh(it, r, h):
                    s, n = h % 2, it * NH0 + h
                    pe.wait_ge(pt_ready.s, pt_ready.at(n + 1))
                    for j in range(NWIN):
                        ins = nc.tensor.matmul(ps[0:TILE, 4, h * HD0:(h + 1) * HD0], PT[:, s, j * TILE:(j + 1) * TILE],
                                               V[:, ds(r + j, 1), h * HD0:(h + 1) * HD0].rearrange("p a c -> p (a c)"),
                                               start=(j == 0), stop=(j == NWIN - 1))
                    ins.then_inc(pv_done.s, 1)

                with pe.Fori(0, B) as b:
                    with pe.Fori(0, CPB) as i:
                        it = b * CPB + i
                        pe.wait_ge(xn_ready.s, it + 1)
                        pe.wait_ge(q_out.s, q_out.at(it))
                        for j in range(3):
                            nc.tensor.matmul(ps[:, j, 0:CH], wqkv[:, j * C:(j + 1) * C], xn[:],
                                             start=True, stop=True).then_inc(qkv_done.s, 1)
                    with pe.Fori(0, NPAIR) as i:
                        pe.wait_ge(v_staged.s, b * NPAIR + i + 1)
                        nc.tensor.transpose(ps[0:PAIR, 3, 0:C], vst[:], k.ident[:]).then_inc(v_turned.s, 1)
                    with pe.Fori(0, TPB) as r:
                        it = b * TPB + r
                        pe.wait_ge(v_out.s, v_out.at((b + 1) * NPAIR))
                        pe.wait_ge(qh_ready.s, it + 1)
                        scores(it, r, 0)
                        scores(it, r, 1)
                        turn(it, 0)
                        for h in range(2, NH0):
                            scores(it, r, h)
                            weigh(it, r, h - 2)
                            turn(it, h - 1)
                        weigh(it, r, NH0 - 2)
                        turn(it, NH0 - 1)
                        weigh(it, r, NH0 - 1)
                        pe.wait_ge(o_ready.s, it + 1)
                        nc.tensor.transpose(ps[:, 5, 0:TILE], o[:], k.ident[0:TILE, 0:TILE]).then_inc(o_turned.s, 1)
                        pe.wait_ge(ot_ready.s, it + 1)
                        nc.tensor.matmul(ps[:, 6, 0:TILE], wproj[:], oT[:], start=True, stop=True).then_inc(proj_done.s, 1)


def layer_norm(k, tag, eps_value):
    nc, X, N, ps = k.nc, k.X, k.normed(), k.ps
    with ExitStack() as ctx:
        sb = lambda n, s, dt=F32: k.sb(f"{tag}_{n}", s, dt, ctx)
        sem = lambda n, credit=0: k.sem(f"{tag}_{n}", credit)
        xc, sq, std = sb("xc", [C, 2, CH]), sb("sq", [C, 2, CH]), sb("std", [C, 2, CH])
        eps = sb("eps", [C, 1])
        two = lambda n, credit=0: [sem(f"{n}{i}", credit) for i in range(2)]
        eps_set, mean_done, centred, squared, var_done, std_ready, inverted, done = (
            sem("eps_set"), two("mean_done"), two("centred", 1), two("squared", 1), two("var_done", 1),
            two("std_ready", 1), two("inverted", 1), two("done", 1))
        with nc.Block() as block:
            @block.tensor
            def _(pe):
                for s in range(2):
                    pe.sem_inc(var_done[s].s, 1)
                with pe.Fori(0, NCH // 2) as i:
                    for s in range(2):
                        pe.wait_ge(centred[s].s, centred[s].at(i))
                        nc.tensor.matmul(ps[:, s, 0:CH], k.mean_mat[:], X[:, ds(i * (2 * CH) + s * CH, CH)],
                                         start=True, stop=True).then_inc(mean_done[s].s, 1)
                    for s in range(2):
                        pe.wait_ge(squared[s].s, squared[s].at(i + 1))
                        pe.wait_ge(std_ready[s].s, std_ready[s].at(i))
                        nc.tensor.matmul(ps[:, 2 + s, 0:CH], k.mean_mat[:], sq[:, s, :],
                                         start=True, stop=True).then_inc(var_done[s].s, 1)

            @block.scalar
            def _(act):
                for s in range(2):
                    act.sem_inc(squared[s].s, 1)
                    act.sem_inc(std_ready[s].s, 1)
                act.wait_ge(eps_set.s, 1)
                with act.Fori(0, NCH // 2) as i:
                    for s in range(2):
                        act.wait_ge(centred[s].s, centred[s].at(i + 1))
                        act.wait_ge(var_done[s].s, var_done[s].at(i))
                        nc.scalar.activation(sq[:, s, :], xc[:, s, :], ACT.Square).then_inc(squared[s].s, 1)
                    for s in range(2):
                        act.wait_ge(var_done[s].s, var_done[s].at(i + 1))
                        act.wait_ge(inverted[s].s, inverted[s].at(i))
                        nc.scalar.activation(std[:, s, :], ps[:, 2 + s, 0:CH], ACT.Sqrt, bias=eps[:]).then_inc(std_ready[s].s, 1)

            @block.vector
            def _(dve):
                nc.vector.memset(eps[:], eps_value).then_inc(eps_set.s, 1)
                for s in range(2):
                    dve.sem_inc(centred[s].s, 1)
                    dve.sem_inc(inverted[s].s, 1)
                    dve.sem_inc(done[s].s, 1)
                with dve.Fori(0, NCH // 2) as i:
                    for s in range(2):
                        dve.wait_ge(mean_done[s].s, i + 1)
                        dve.wait_ge(done[s].s, done[s].at(i))
                        nc.vector.tensor_tensor(xc[:, s, :], X[:, ds(i * (2 * CH) + s * CH, CH)], ps[:, s, 0:CH],
                                                ALU.subtract).then_inc(centred[s].s, 1)
                    for s in range(2):
                        dve.wait_ge(std_ready[s].s, std_ready[s].at(i + 1))
                        dve.wait_ge(done[s].s, done[s].at(i))
                        nc.vector.reciprocal(std[:, s, :], std[:, s, :]).then_inc(inverted[s].s, 1)
                        dve.wait_ge(inverted[s].s, inverted[s].at(i + 1))
                        nc.vector.tensor_tensor(N[:, ds(i * (2 * CH) + s * CH, CH)], xc[:, s, :], std[:, s, :],
                                                ALU.mult).then_inc(done[s].s, 1)


def attention(k, tag, heads, wqkv_name, wproj_name):
    nc, X, N, ps = k.nc, k.X, k.normed(), k.ps
    H, hd = heads, C // heads
    HP = max(1, H // 2)
    with ExitStack() as ctx:
        sb = lambda n, s, dt=F32: k.sb(f"{tag}_{n}", s, dt, ctx)
        sem = lambda n, credit=0: k.sem(f"{tag}_{n}", credit)
        wqkv = sb("wqkv", [C, 3 * C])
        wproj = sb("wproj", [C, C]) if wproj_name else None
        head_scale, masks = sb("head_scale", [C, H]), sb("masks", [TILE, TPC, CH])
        Q, K, V = sb("Q", [C, L]), sb("K", [C, L]), sb("V", [TILE, TPB, C])
        ncs = sb("ncs", [C, CH])
        qh, row = sb("qh", [C, 2, TILE]), sb("row", [TILE, 2, L])
        PT = sb("PT", [TILE, 2, CH])
        rmax, nmax, rsum, rinv = (sb(n, [TILE, 2]) for n in ("rmax", "nmax", "rsum", "rinv"))
        o, oT = sb("o", [TILE, 2, C]), sb("oT", [C, TILE])
        w_in, own, n_copied, qkv_done, q_out, kv_out = (
            sem("w_in"), sem("own"), sem("n_copied"), sem("qkv_done", 1), sem("q_out", 1), sem("kv_out", 1))
        qh_ready, s_done, s_read, row_max, neg_max = sem("qh_ready"), sem("s_done"), sem("s_read", 2), sem("row_max"), sem("neg_max")
        p_ready, pt_ready, pv_blk = sem("p_ready"), sem("pt_ready", 2), sem("pv_blk", 2)
        inverted, o_ready, o_turned, ot_ready, proj_done, x_done = (
            sem("inverted"), sem("o_ready"), sem("o_turned"), sem("ot_ready"), sem("proj_done"), sem("x_done", 2))
        blk_turned = sem("blk_turned")
        loads = [(wqkv[:], wqkv_name), (head_scale[:], f"head_scale_{tag}"), (masks[:], "causal_masks")]
        if wproj_name:
            loads.append((wproj[:], wproj_name))

        def steps(eng, b, body):
            for I in range(TPB // TPC):
                nb = b * (TPB * H) + I * TPC * H
                gb = b * (TPC * H * sum(range(1, TPB // TPC + 1))) + TPC * H * (I * (I + 1) // 2)
                if H == 1:
                    with eng.Fori(0, TPC // 2) as jp:
                        body(I, [(jp * 2 + s, None, s, nb + jp * 2 + s, gb + (jp * 2 + s) * (I + 1)) for s in range(2)], None)
                else:
                    with eng.Fori(0, TPC) as j:
                        with eng.Fori(0, HP) as hp:
                            body(I, [(j, hp * 2 + s, s, nb + j * H + hp * 2 + s, gb + (j * H + hp * 2 + s) * (I + 1))
                                     for s in range(2)], None)
                        body(I, [], (j, b * TPB + I * TPC + j))

        with nc.Block() as block:
            @block.sync
            def _(sp):
                for dst, name in loads:
                    sp.dma_start(dst, k.dram[name]).then_inc(w_in.s, 16)

            @block.vector
            def _(dve):
                for q in (s_read, kv_out, x_done):
                    dve.sem_inc(q.s, q.credit)
                dve.wait_ge(w_in.s, 16 * len(loads))
                with dve.Fori(0, B) as b:
                    with dve.Fori(0, CPB) as i:
                        it = b * CPB + i
                        dve.wait_ge(qkv_done.s, qkv_done.at(it * 3))
                        nc.vector.tensor_copy(ncs[:], N[:, ds(b * L + i * CH, CH)]).then_inc(n_copied.s, 1)
                        dve.wait_ge(qkv_done.s, qkv_done.at(it * 3 + 2))
                        nc.vector.tensor_copy(K[:, ds(i * CH, CH)], ps[:, 1, 0:CH]).then_inc(kv_out.s, 1)
                        dve.wait_ge(qkv_done.s, qkv_done.at(it * 3 + 3))
                        nc.vector.tensor_copy(V[:, ds(i * TPC, TPC), :], ps[0:TILE, 2, :].rearrange("p (t c) -> p t c", c=C)).then_inc(kv_out.s, 1)

                    def body(I, items, tile):
                        for j, h, s, n, g in items:
                            dve.wait_ge(q_out.s, q_out.at((b + 1) * CPB))
                            nc.vector.tensor_scalar(qh[:, s, :], Q[:, ds((j + I * TPC) * TILE, TILE)],
                                                    head_scale[:, 0:1] if h is None else head_scale[:, ds(h, 1)],
                                                    None, ALU.mult).then_inc(qh_ready.s, 1)
                            for c in range(I + 1):
                                dve.wait_ge(s_done.s, g + c + 1)
                                dst, src = row[:, s, c * CH:(c + 1) * CH], ps[0:TILE, 2 * s + c % 2, 0:CH]
                                if c < I:
                                    nc.vector.tensor_copy(dst, src).then_inc(s_read.s, 1)
                                else:
                                    nc.vector.tensor_tensor(dst, src, masks[:, ds(j, 1), :].rearrange("p a k -> p (a k)"),
                                                            ALU.add).then_inc(s_read.s, 1)
                            dve.wait_ge(s_read.s, s_read.at(g + I + 1))
                            nc.vector.tensor_reduce(rmax[:, s:s + 1], row[:, s, 0:(I + 1) * CH], AX.X, ALU.max).then_inc(row_max.s, 1)
                            dve.wait_ge(row_max.s, n + 1)
                            nc.vector.tensor_scalar(nmax[:, s:s + 1], rmax[:, s:s + 1], -1.0, None, ALU.mult).then_inc(neg_max.s, 1)
                        for j, h, s, n, g in items:
                            dve.wait_ge(p_ready.s, n + 1)
                            nc.vector.reciprocal(rinv[:, s:s + 1], rsum[:, s:s + 1]).then_inc(inverted.s, 1)
                            dve.wait_ge(inverted.s, n + 1)
                            dve.wait_ge(pv_blk.s, pv_blk.at(g + I + 1))
                            dst = o[:, s, :] if h is None else o[:, 0, ds(h * hd, hd)]
                            nc.vector.tensor_scalar(dst, ps[0:TILE, 6 + s, 0:hd], rinv[:, s:s + 1], None, ALU.mult).then_inc(o_ready.s, 1)
                        if H == 1:
                            for j, h, s, n, g in items:
                                dve.wait_ge(o_turned.s, n + 1)
                                xs = X[:, ds(b * L + (j + I * TPC) * TILE, TILE)]
                                nc.vector.tensor_tensor(xs, xs, ps[:, 6 + s, C:C + TILE], ALU.add).then_inc(x_done.s, 1)
                        elif tile:
                            j, t = tile
                            dve.wait_ge(proj_done.s, t + 1)
                            xs = X[:, ds(b * L + (j + I * TPC) * TILE, TILE)]
                            nc.vector.tensor_tensor(xs, xs, ps[:, 7, C:C + TILE], ALU.add).then_inc(x_done.s, 1)

                    steps(dve, b, body)

            @block.scalar
            def _(act):
                for q in (pt_ready, q_out):
                    act.sem_inc(q.s, q.credit)
                with act.Fori(0, B) as b:
                    with act.Fori(0, CPB) as i:
                        act.wait_ge(qkv_done.s, qkv_done.at((b * CPB + i) * 3 + 1))
                        nc.scalar.activation(Q[:, ds(i * CH, CH)], ps[:, 0, 0:CH], ACT.Copy).then_inc(q_out.s, 1)

                    def body(I, items, tile):
                        for j, h, s, n, g in items:
                            act.wait_ge(neg_max.s, n + 1)
                            p = row[:, s, 0:(I + 1) * CH]
                            nc.scalar.activation(p, p, ACT.Exp, bias=nmax[:, s:s + 1], accum_out=rsum[:, s:s + 1]).then_inc(p_ready.s, 1)
                            for c in range(I + 1):
                                act.wait_ge(blk_turned.s, g + c + 1)
                                act.wait_ge(pv_blk.s, pv_blk.at(g + c - (1 if c else 0)))
                                nc.scalar.activation(PT[:, c % 2, :], ps[0:TILE, 4 + c % 2, 0:CH], ACT.Copy).then_inc(pt_ready.s, 1)
                        if tile:
                            act.wait_ge(o_turned.s, tile[1] + 1)
                            nc.scalar.activation(oT[:], ps[:, 6, C:C + TILE], ACT.Copy).then_inc(ot_ready.s, 1)

                    steps(act, b, body)

            @block.tensor
            def _(pe):
                for q in (qkv_done, pv_blk):
                    pe.sem_inc(q.s, q.credit)
                pe.wait_ge(w_in.s, 16 * len(loads))
                with pe.Fori(0, B) as b:
                    with pe.Fori(0, CPB) as i:
                        it = b * CPB + i
                        pe.wait_ge(n_copied.s, it + 1)
                        pe.wait_ge(q_out.s, q_out.at(it))
                        for j in range(2):
                            nc.tensor.matmul(ps[:, j, 0:CH], wqkv[:, j * C:(j + 1) * C], ncs[:],
                                             start=True, stop=True).then_inc(qkv_done.s, 1)
                        for t in range(TPC):
                            ins = nc.tensor.matmul(ps[0:TILE, 2, t * C:(t + 1) * C], ncs[:, t * TILE:(t + 1) * TILE],
                                                   wqkv[:, 2 * C:3 * C], start=True, stop=True)
                        ins.then_inc(qkv_done.s, 1)

                    def body(I, items, tile):
                        for j, h, s, n, g in items:
                            pe.wait_ge(kv_out.s, kv_out.at((b + 1) * (2 * CPB)))
                            pe.wait_ge(qh_ready.s, n + 1)
                            for c in range(I + 1):
                                pe.wait_ge(s_read.s, s_read.at(g + c - 1))
                                nc.tensor.matmul(ps[0:TILE, 2 * s + c % 2, 0:CH], qh[:, s, :], K[:, c * CH:(c + 1) * CH],
                                                 start=True, stop=True).then_inc(s_done.s, 1)
                        for j, h, s, n, g in items:
                            pe.wait_ge(p_ready.s, n + 1)
                            if H == 1:
                                pe.wait_ge(x_done.s, x_done.at(n - 1))
                            for c in range(I + 1):
                                pe.wait_ge(pt_ready.s, pt_ready.at(g + c - (1 if c else 0)))
                                for t in range(TPC):
                                    ins = nc.tensor.transpose(ps[0:TILE, 4 + c % 2, t * TILE:(t + 1) * TILE],
                                                              row[:, s, c * CH + t * TILE:c * CH + (t + 1) * TILE],
                                                              k.ident[0:TILE, 0:TILE])
                                ins.then_inc(blk_turned.s, 1)
                                if c > 0:
                                    weigh(I, c - 1, h, s, n, g)
                            weigh(I, I, h, s, n, g)
                        if H == 1:
                            for j, h, s, n, g in items:
                                pe.wait_ge(o_ready.s, n + 1)
                                nc.tensor.transpose(ps[:, 6 + s, C:C + TILE], o[:, s, :], k.ident[0:TILE, 0:TILE]).then_inc(o_turned.s, 1)
                        elif tile:
                            t = tile[1]
                            pe.wait_ge(o_ready.s, (t + 1) * H)
                            nc.tensor.transpose(ps[:, 6, C:C + TILE], o[:, 0, :], k.ident[0:TILE, 0:TILE]).then_inc(o_turned.s, 1)
                            pe.wait_ge(ot_ready.s, t + 1)
                            nc.tensor.matmul(ps[:, 7, C:C + TILE], wproj[:], oT[:], start=True, stop=True).then_inc(proj_done.s, 1)
                            pe.wait_ge(x_done.s, x_done.at(t + 1))

                    def weigh(I, c, h, s, n, g):
                        pe.wait_ge(pt_ready.s, pt_ready.at(g + c + 1))
                        for t in range(TPC):
                            v = V[:, c * TPC + t, :] if h is None else V[:, c * TPC + t, ds(h * hd, hd)]
                            first, last = c == 0 and t == 0, c == I and t == TPC - 1
                            ins = nc.tensor.matmul(ps[0:TILE, 6 + s, 0:hd], PT[:, c % 2, t * TILE:(t + 1) * TILE], v,
                                                   start=first, stop=last)
                        ins.then_inc(pv_blk.s, 1)

                    steps(pe, b, body)


def experts(k):
    nc, X, N, ps = k.nc, k.X, k.normed(), k.ps
    NT = T // TILE
    with ExitStack() as ctx:
        sb = lambda n, s, dt=F32: k.sb(f"moe_{n}", s, dt, ctx)
        sem = lambda n, credit=0: k.sem(f"moe_{n}", credit)
        wr, br = sb("wr", [C, NE]), sb("br", [NE, 1])
        we, be, spread = sb("we", [C, NE, C]), sb("be", [NE, C]), sb("spread", [NE, NE, C])
        rank = sb("rank", [TILE, NE])
        lt = sb("lt", [NE, CH])
        logit, prob, left, pick = (sb(n, [TILE, NT, NE]) for n in ("logit", "prob", "left", "pick"))
        best, top1, top2 = (sb(n, [TILE, NT]) for n in ("best", "top1", "top2"))
        gst, gT = sb("gst", [TILE, TPC * NE]), sb("gT", [NE, CH])
        xg = sb("xg", [C, 2, CH])
        w_in, own = sem("w_in"), sem("own")
        logit_done, lt_ready, lt_turned, l_out = sem("logit_done"), sem("lt_ready"), sem("lt_turned"), sem("l_out")
        shifted, exped = sem("shifted"), sem("exped")
        g_staged, g_turned, gt_ready, spread_done, xg_ready, xg_used, y_done, x_done = (
            sem("g_staged"), sem("g_turned"), sem("gt_ready"), sem("spread_done"), sem("xg_ready", 2), sem("xg_used", 2),
            sem("y_done"), sem("x_done", 1))
        loads = [(wr[:], "w2_router"), (br[:], "b2_router"), (we[:], "w2_expert"), (be[:], "b2_expert"),
                 (spread[:], "spread8"), (rank[:], "rank8")]
        over = lambda t: t[:].unsqueeze(2).to_broadcast([TILE, NT, NE])
        with nc.Block() as block:
            @block.sync
            def _(sp):
                for dst, name in loads:
                    sp.dma_start(dst, k.dram[name]).then_inc(w_in.s, 16)

            @block.tensor
            def _(pe):
                pe.sem_inc(xg_used.s, xg_used.credit)
                pe.wait_ge(w_in.s, 16 * len(loads))
                with pe.Fori(0, NCH) as i:
                    nc.tensor.matmul(ps[0:NE, 0, 0:CH], wr[:], N[:, ds(i * CH, CH)], start=True, stop=True).then_inc(logit_done.s, 1)
                    pe.wait_ge(lt_ready.s, i + 1)
                    for t in range(TPC):
                        ins = nc.tensor.matmul(ps[0:TILE, 1, t * NE:(t + 1) * NE], lt[:, t * TILE:(t + 1) * TILE],
                                               k.ident[0:NE, 0:NE], start=True, stop=True)
                    ins.then_inc(lt_turned.s, 1)
                    pe.wait_ge(l_out.s, i + 1)
                with pe.Fori(0, NCH) as i:
                    pe.wait_ge(g_staged.s, i + 1)
                    for t in range(TPC):
                        ins = nc.tensor.transpose(ps[0:NE, 2, t * TILE:(t + 1) * TILE], gst[:, t * NE:(t + 1) * NE],
                                                  k.ident[0:TILE, 0:TILE])
                    ins.then_inc(g_turned.s, 1)
                    pe.wait_ge(gt_ready.s, i + 1)
                    pe.wait_ge(x_done.s, x_done.at(i))
                    nc.tensor.matmul(ps[:, 3, 0:CH], be[:], gT[:], start=True, stop=False)

                    def spread_gate(e):
                        pe.wait_ge(xg_ready.s, xg_ready.at(i * NE + e - 1))
                        nc.tensor.matmul(ps[:, 4 + e % 2, 0:CH], spread[:, e, :], gT[:], start=True, stop=True).then_inc(spread_done.s, 1)

                    spread_gate(0)
                    for e in range(NE):
                        if e + 1 < NE:
                            spread_gate(e + 1)
                        pe.wait_ge(xg_ready.s, xg_ready.at(i * NE + e + 1))
                        ins = nc.tensor.matmul(ps[:, 3, 0:CH], we[:, e, :], xg[:, e % 2, :], start=False, stop=(e == NE - 1))
                        ins.then_inc(xg_used.s, 1)

            @block.scalar
            def _(act):
                act.wait_ge(w_in.s, 16 * len(loads))
                with act.Fori(0, NCH) as i:
                    act.wait_ge(logit_done.s, i + 1)
                    nc.scalar.activation(lt[:], ps[0:NE, 0, 0:CH], ACT.Identity, bias=br[:]).then_inc(lt_ready.s, 1)
                act.wait_ge(shifted.s, 1)
                nc.scalar.activation(prob[:], prob[:], ACT.Exp).then_inc(exped.s, 1)
                with act.Fori(0, NCH) as i:
                    act.wait_ge(g_turned.s, i + 1)
                    nc.scalar.activation(gT[:], ps[0:NE, 2, 0:CH], ACT.Copy).then_inc(gt_ready.s, 1)

            @block.vector
            def _(dve):
                dve.sem_inc(xg_ready.s, xg_ready.credit)
                dve.sem_inc(x_done.s, x_done.credit)
                dve.wait_ge(w_in.s, 16 * len(loads))
                with dve.Fori(0, NCH) as i:
                    dve.wait_ge(lt_turned.s, i + 1)
                    nc.vector.tensor_copy(logit[:, ds(i * TPC, TPC), :], ps[0:TILE, 1, 0:TPC * NE].rearrange("p (t e) -> p t e", e=NE)).then_inc(l_out.s, 1)
                dve.wait_ge(l_out.s, NCH)
                link = Chain(dve, own.s).link
                v = nc.vector
                link(v.tensor_reduce(best[:], logit[:], AX.X, ALU.max))
                v.tensor_tensor(prob[:], logit[:], over(best), ALU.subtract).then_inc(shifted.s, 1)
                dve.wait_ge(exped.s, 1)
                link(v.tensor_reduce(best[:], prob[:], AX.X, ALU.add))
                link(v.reciprocal(best[:], best[:]))
                link(v.tensor_tensor(prob[:], prob[:], over(best), ALU.mult))
                ranks = rank[:].unsqueeze(1).to_broadcast([TILE, NT, NE])

                def choose(chosen, p, top):
                    link(v.tensor_reduce(top[:], p[:], AX.X, ALU.max))
                    link(v.tensor_tensor(chosen[:], p[:], over(top), ALU.is_equal))
                    link(v.tensor_tensor(chosen[:], chosen[:], ranks, ALU.mult))
                    link(v.tensor_reduce(best[:], chosen[:], AX.X, ALU.max))
                    link(v.tensor_tensor(chosen[:], chosen[:], over(best), ALU.is_equal))

                choose(pick, prob, top1)
                link(v.scalar_tensor_tensor(left[:], pick[:], -2.0, prob[:], ALU.mult, ALU.add))
                choose(logit, left, top2)
                link(v.tensor_tensor(pick[:], pick[:], logit[:], ALU.add))
                link(v.tensor_tensor(top1[:], top1[:], top2[:], ALU.add))
                link(v.reciprocal(top1[:], top1[:]))
                link(v.tensor_tensor(prob[:], prob[:], pick[:], ALU.mult))
                link(v.tensor_tensor(prob[:], prob[:], over(top1), ALU.mult))
                with dve.Fori(0, NCH) as i:
                    nc.vector.tensor_copy(gst[:].rearrange("p (t e) -> p t e", e=NE), prob[:, ds(i * TPC, TPC), :]).then_inc(g_staged.s, 1)
                    for e in range(NE):
                        dve.wait_ge(spread_done.s, i * NE + e + 1)
                        dve.wait_ge(xg_used.s, xg_used.at(i * NE + e - 1))
                        nc.vector.tensor_tensor(xg[:, e % 2, :], N[:, ds(i * CH, CH)], ps[:, 4 + e % 2, 0:CH], ALU.mult).then_inc(xg_ready.s, 1)
                    dve.wait_ge(xg_used.s, xg_used.at(i * NE + NE))
                    xs = X[:, ds(i * CH, CH)]
                    nc.vector.tensor_tensor(xs, xs, ps[:, 3, 0:CH], ALU.add).then_inc(x_done.s, 1)


def recurrence(k):
    nc, X, N, ps = k.nc, k.X, k.normed(), k.ps
    G = CH // B
    NG = L // G
    with ExitStack() as ctx:
        sb = lambda n, s, dt=F32: k.sb(f"rnn_{n}", s, dt, ctx)
        sem = lambda n, credit=0: k.sem(f"rnn_{n}", credit)
        wx, w, v = sb("wx", [C, T]), sb("w", [C, C]), sb("v", [C, C])
        gamma, beta = sb("gamma", [C, 1]), sb("beta", [C, 1])
        stats, mv, std, a, c = sb("stats", [C, NCH * 6]), sb("mv", [C, 2]), sb("std", [C, 1]), sb("a", [C, 1]), sb("c", [C, 1])
        y = sb("y", [C, 2, CH])
        w_in, own, zeroed = sem("w_in"), sem("own"), sem("zeroed")
        wx_done, wx_out, stat_done, var_ready, std_ready, wn_ready, added, stepped, y_ready, banks = (
            sem(n, cr) for n, cr in (("wx_done", 0), ("wx_out", 2), ("stat_done", 0), ("var_ready", 0), ("std_ready", 0),
                                     ("wn_ready", 0), ("added", 2), ("stepped", 0), ("y_ready", 1), ("banks", 0)))
        loads = [(w[:], "w3_in"), (v[:], "w3_v"), (gamma[:], "gamma3"), (beta[:], "beta3")]
        steps_major = N[:, 0:T].rearrange("p (t b) -> p t b", b=B)
        with nc.Block() as block:
            @block.sync
            def _(sp):
                for dst, name in loads:
                    sp.dma_start(dst, k.dram[name]).then_inc(w_in.s, 16)

            @block.vector
            def _(dve):
                nc.vector.memset(y[:], 0.0).then_inc(zeroed.s, 1)
                nc.vector.memset(N[:, T:T + CH], 0.0).then_inc(zeroed.s, 1)
                dve.wait_ge(w_in.s, 16 * len(loads))
                with dve.Fori(0, NCH) as i:
                    dve.wait_ge(wx_out.s, wx_out.at(i + 1))
                    nc.vector.bn_stats(stats[:, ds(i * 6, 6)], wx[:, ds(i * CH, CH)]).then_inc(stat_done.s, 1)
                dve.wait_ge(stat_done.s, NCH)
                chain = Chain(dve, own.s)
                link = chain.link
                link(nc.vector.bn_aggr(mv[:], stats[:]))
                nc.vector.tensor_scalar(std[:], mv[:, 1:2], 1e-5, None, ALU.add).then_inc(var_ready.s, 1)
                dve.wait_ge(std_ready.s, 1)
                link(nc.vector.reciprocal(a[:], std[:]))
                link(nc.vector.tensor_tensor(a[:], a[:], gamma[:], ALU.mult))
                link(nc.vector.tensor_tensor(c[:], mv[:, 0:1], a[:], ALU.mult))
                link(nc.vector.tensor_tensor(c[:], beta[:], c[:], ALU.subtract))
                for b in range(B):
                    nc.vector.tensor_scalar(steps_major[:, :, b], wx[:, b * L:(b + 1) * L], a[:, 0:1], c[:, 0:1],
                                            ALU.mult, ALU.add).then_inc(wn_ready.s, 1)

            @block.gpsimd
            def _(pool):
                pool.sem_inc(added.s, added.credit)
                with pool.Fori(0, NG // 2) as i:
                    for s in range(2):
                        pool.wait_ge(y_ready.s, y_ready.at((i * 2 + s + 1) * G))
                        xs = X[:].rearrange("p (b t) -> p b t", b=B)[:, :, ds((i * 2 + s) * G, G)]
                        nc.gpsimd.tensor_tensor(xs, xs, y[:, s, :].rearrange("p (t b) -> p b t", b=B), ALU.add).then_inc(added.s, 1)

            @block.scalar
            def _(act):
                act.sem_inc(wx_out.s, wx_out.credit)
                act.sem_inc(y_ready.s, y_ready.credit)
                with act.Fori(0, NCH // 2) as i:
                    for s in range(2):
                        act.wait_ge(wx_done.s, i * 2 + s + 1)
                        nc.scalar.activation(wx[:, ds(i * (2 * CH) + s * CH, CH)], ps[:, s, 0:CH], ACT.Copy).then_inc(wx_out.s, 1)
                act.wait_ge(var_ready.s, 1)
                nc.scalar.activation(std[:], std[:], ACT.Sqrt).then_inc(std_ready.s, 1)
                with act.Fori(0, NG // 2) as i:
                    for s in range(2):
                        act.wait_ge(added.s, added.at(i * 2 + s - 1))
                        for t in range(G):
                            act.wait_ge(stepped.s, (i * 2 + s) * G + t + 1)
                            nc.scalar.activation(y[:, s, t * B:(t + 1) * B], ps[:, 2 + s, t * B:(t + 1) * B],
                                                 ACT.Sigmoid).then_inc(y_ready.s, 1)

            @block.tensor
            def _(pe):
                pe.wait_ge(w_in.s, 16 * len(loads))
                with pe.Fori(0, NCH // 2) as i:
                    for s in range(2):
                        pe.wait_ge(wx_out.s, wx_out.at(i * 2 + s - 1))
                        nc.tensor.matmul(ps[:, s, 0:CH], w[:], N[:, ds(i * (2 * CH) + s * CH, CH)], start=True, stop=True).then_inc(wx_done.s, 1)
                pe.wait_ge(wn_ready.s, B)
                nc.tensor.matmul(ps[:, 2, 0:CH], k.ident[:], N[:, 0:CH], start=True, stop=True)
                pe.wait_ge(zeroed.s, 2)
                with pe.Fori(0, NG // 2) as i:
                    for s in range(2):
                        for t in range(G):
                            pe.wait_ge(y_ready.s, y_ready.at((i * 2 + s) * G + t))
                            prev = y[:, s, (t - 1) * B:t * B] if t else y[:, 1 - s, CH - B:CH]
                            nc.tensor.matmul(ps[:, 2 + s, t * B:(t + 1) * B], v[:], prev, start=False, stop=True,
                                             skip_group_check=True).then_inc(stepped.s, 1)
                            if t == G // 2:
                                nxt = (i * 2 + 1) * CH if s == 0 else i * (2 * CH) + 2 * CH
                                nc.tensor.matmul(ps[:, 3 - s, 0:CH], k.ident[:], N[:, ds(nxt, CH)], start=True, stop=True)


def layer1(k):
    nc, X, ps = k.nc, k.X, k.ps
    WPD = HW + 2
    v = nc.vector
    with ExitStack() as ctx:
        sb = lambda n, s, dt=F32: k.sb(f"l1_{n}", s, dt, ctx)
        sem = lambda n, credit=0: k.sem(f"l1_{n}", credit)
        w_in_proj = sb("w_in_proj", [C, 2 * DI])
        w_taps, b_conv = sb("w_taps", [C, CT, 9]), sb("b_conv", [C, CT])
        w_bc, w_dt_in, w_dt = sb("w_bc", [C, ND, CT, 96]), sb("w_dt_in", [C, ND, CT, DTR]), sb("w_dt", [DTR, ND, DI])
        b_dt, A, D = sb("b_dt", [C, ND, CT]), sb("A", [C, ND, CT, NS]), sb("D", [C, ND, CT])
        ln_w, ln_b, w_out = sb("ln_w", [C, CT]), sb("ln_b", [C, CT]), sb("w_out", [C, CT, C])
        mean256, eps = sb("mean256", [C, C]), sb("eps", [C, 1])
        spread = sb("spread", [96, 2 * NS, C], BF16)
        d_mat = sb("d_mat", [C, ND, CT, C])
        xn, u, Y = sb("xn", [C, L]), sb("u", [C, CT, L]), sb("Y", [C, CT, L])
        xpad = sb("xpad", [C, WPD, WPD])
        bc, rest = sb("bc", [96, 2, CS], BF16), sb("rest", [96, CS])
        dtr, xb, e, w = sb("dtr", [DTR, CS]), sb("xb", [C, CT, CS]), sb("e", [C, CT, CS]), sb("w", [C, CT, CS])
        dt, dtu = sb("dt", [C, 2, CT, CS]), sb("dtu", [C, 2, CT, CS])
        dA, dBu, h, hC = (sb(n, [C, 2, CT, CS]) for n in ("dA", "dBu", "h", "hC"))
        Cs, mid, state = sb("Cs", [C, 2, CS]), sb("mid", [96, CS], BF16), sb("state", [C, CT, NS])
        flat = lambda t, n, w: t[:].rearrange("p a b c -> p (a b c)")[:, 0:n * w].rearrange("p (a c) -> p a c", a=n)
        yc, sq, std, sz = flat(dA, CT, CH), flat(dBu, CT, CH), flat(h, 1, CH), flat(hC, CT, CH)

        w_loaded, own, conv_own, end_own, a_negated, d_ready = (
            sem(n) for n in ("w_loaded", "own", "conv_own", "end_own", "a_negated", "d_ready"))
        xn_ready, xc_done, xc_out, conv_done, sg_ready, u_ready = (
            sem("xn_ready"), sem("xc_done"), sem("xc_out", 1), sem("conv_done", 1), sem("sg_ready"), sem("u_ready"))
        proj_done, split_done, dtr_ready, delta_done, delta_out, abs_ready, e_ready, w_ready, ln_ready, dt_ready = (
            sem("proj_done"), sem("split_done"), sem("dtr_ready"), sem("delta_done"), sem("delta_out", 1),
            sem("abs_ready"), sem("e_ready"), sem("w_ready"), sem("ln_ready"), sem("dt_ready"))
        bc_done, dbu_ready, a_ready, c_copied, scan_done, hc_ready, y_done, y_out = (
            sem("bc_done"), sem("dbu_ready", 2), sem("a_ready"), sem("c_copied", 2), sem("scan_done", 2),
            sem("hc_ready", 2), sem("y_done", 2), sem("y_out", 1))
        m_done, yc_ready, sq_ready, var_done, std_ready, z_done, sz_ready, g_ready, out_done, x_done = (
            sem("m_done"), sem("yc_ready"), sem("sq_ready"), sem("var_done"), sem("std_ready"), sem("z_done"),
            sem("sz_ready"), sem("g_ready"), sem("out_done"), sem("x_done", 1))
        loads = [(w_in_proj[:], "w1_in"), (w_taps[:], "w1_taps"), (b_conv[:], "b1_conv"), (w_bc[:], "w1_bc"),
                 (w_dt_in[:], "w1_dt_in"), (w_dt[:], "w1_dt"), (b_dt[:], "b1_dt"), (A[:], "A_logs"), (D[:], "D1"),
                 (ln_w[:], "ln1_w"), (ln_b[:], "ln1_b"), (w_out[:], "w1_out"), (mean256[:], "mean256"),
                 (spread[:].bitcast(mybir.dt.uint16), "spread_bc")]

        def forward(eng, kk, o):
            return o if kk < 2 else o * -1 + (NCS // 2 - 1)

        def u_view(ct, kk, o, p):
            p = p if kk < 2 else 1 - p
            win = u[:, ct, :].rearrange("p (hg wh wg ww) -> p hg wh wg ww", hg=4, wh=WS, wg=4)
            if kk % 2 == 0:
                return win[:, ds(o, 1), :, 2 * p:2 * p + 2, :].rearrange("p a wh wg ww -> p (a wg) wh ww")
            return win[:, 2 * p:2 * p + 2, :, ds(o, 1), :].rearrange("p hg wh a ww -> p (a hg) ww wh")

        def y_view(ct, kk, o, p):
            p = p if kk < 2 else 1 - p
            pos = "p (i j) -> p i j" if kk % 2 == 0 else "p (i j) -> p j i"
            return Y[:, ct, :].rearrange(pos, i=HW)[:, ds((o * 2 + p) * RC, RC), :]

        windows = lambda t: t.rearrange("p (g a b) -> p g a b", g=2, a=WS)
        lines = lambda t: t.rearrange("p (r c) -> p r c", c=HW)
        order = lambda t, kk: t if kk < 2 else t[:, ::-1]

        with nc.Block() as block:
            @block.sync
            def _(sp):
                for dst, name in loads:
                    sp.dma_start(dst, k.dram[name]).then_inc(w_loaded.s, 16)

            @block.tensor
            def _(pe):
                for q in (y_done,):
                    pe.sem_inc(q.s, q.credit)
                pe.wait_ge(w_loaded.s, 16 * len(loads))
                with pe.Fori(0, B) as b:
                    for ct in range(CT):
                        with pe.Fori(0, CPB) as i:
                            pe.wait_ge(xn_ready.s, b + 1)
                            pe.wait_ge(xc_out.s, xc_out.at((b * CT + ct) * CPB + i))
                            nc.tensor.matmul(ps[:, 0, 0:CH], w_in_proj[:, ct * C:(ct + 1) * C], xn[:, ds(i * CH, CH)],
                                             start=True, stop=True).then_inc(xc_done.s, 1)
                    for kk in range(ND):
                        with pe.Fori(0, NCS // 2) as o:
                            f = forward(nc.tensor, kk, o)
                            q0 = (b * ND + kk) * NCS + o * 2
                            for p in range(2):
                                q = q0 + p
                                pe.wait_ge(u_ready.s, (b + 1) * CT)
                                pe.wait_ge(delta_out.s, delta_out.at(q))
                                for ct in range(CT):
                                    nc.tensor.matmul(ps[0:96, 6, 0:CS], w_bc[:, kk, ct, :], u_view(ct, kk, f, p),
                                                     start=(ct == 0), stop=(ct == CT - 1))
                                for ct in range(CT):
                                    ins = nc.tensor.matmul(ps[0:DTR, 7, 0:CS], w_dt_in[:, kk, ct, :], u_view(ct, kk, f, p),
                                                           start=(ct == 0), stop=(ct == CT - 1))
                                ins.then_inc(proj_done.s, 1)
                                pe.wait_ge(dtr_ready.s, q + 1)
                                for ct in range(CT):
                                    ins = nc.tensor.matmul(ps[:, 6 + ct, 0:CS], w_dt[:, kk, ct * C:(ct + 1) * C], dtr[:],
                                                           start=True, stop=True)
                                ins.then_inc(delta_done.s, 1)

                            def spread_bc(i):
                                p, n, m = i // NS, i % NS, q0 * NS + i
                                pe.wait_ge(split_done.s, q0 + p + 1)
                                pe.wait_ge(dbu_ready.s, dbu_ready.at(m - 1))
                                pe.wait_ge(c_copied.s, c_copied.at(m - 1))
                                nc.tensor.matmul(ps[:, n % 2, 0:CS], spread[:, n, :], bc[:, p, :], start=True, stop=True)
                                nc.tensor.matmul(ps[:, 2 + n % 2, 0:CS], spread[:, NS + n, :], bc[:, p, :],
                                                 start=True, stop=True).then_inc(bc_done.s, 1)

                            spread_bc(0)
                            spread_bc(1)
                            for i in range(2 * NS):
                                p, n, m = i // NS, i % NS, q0 * NS + i
                                if i + 2 < 2 * NS:
                                    spread_bc(i + 2)
                                if n == 0:
                                    pe.wait_ge(d_ready.s, 1)
                                    pe.wait_ge(y_out.s, y_out.at(q0 + p))
                                    for ct in range(CT):
                                        nc.tensor.matmul(ps[:, 4 + ct, 0:CS], d_mat[:, kk, ct, :], u_view(ct, kk, f, p),
                                                         start=True, stop=False)
                                pe.wait_ge(hc_ready.s, hc_ready.at(m + 1))
                                for ct in range(CT):
                                    ins = nc.tensor.matmul(ps[:, 4 + ct, 0:CS], k.ident[:], hC[:, n % 2, ct, :],
                                                           start=False, stop=(n == NS - 1))
                                ins.then_inc(y_done.s, 1)
                    with pe.Fori(0, CPB) as i:
                        it = b * CPB + i
                        pe.wait_ge(y_out.s, y_out.at((b + 1) * (ND * NCS)))
                        pe.wait_ge(x_done.s, x_done.at(it))
                        for ct in range(CT):
                            ins = nc.tensor.matmul(ps[:, 0, 0:CH], mean256[:], Y[:, ct, ds(i * CH, CH)],
                                                   start=(ct == 0), stop=(ct == CT - 1))
                        ins.then_inc(m_done.s, 1)
                        for ct in range(CT):
                            ins = nc.tensor.matmul(ps[:, 2 + ct, 0:CH], w_in_proj[:, DI + ct * C:DI + (ct + 1) * C],
                                                   xn[:, ds(i * CH, CH)], start=True, stop=True)
                        ins.then_inc(z_done.s, 1)
                        pe.wait_ge(sq_ready.s, it + 1)
                        for ct in range(CT):
                            ins = nc.tensor.matmul(ps[:, 1, 0:CH], mean256[:], sq[:, ct, :], start=(ct == 0), stop=(ct == CT - 1))
                        ins.then_inc(var_done.s, 1)
                        pe.wait_ge(g_ready.s, it + 1)
                        for ct in range(CT):
                            ins = nc.tensor.matmul(ps[:, 4, 0:CH], w_out[:, ct, :], sz[:, ct, :], start=(ct == 0), stop=(ct == CT - 1))
                        ins.then_inc(out_done.s, 1)

            @block.scalar
            def _(act):
                for q in (xc_out, c_copied):
                    act.sem_inc(q.s, q.credit)
                act.wait_ge(w_loaded.s, 16 * len(loads))
                nc.scalar.activation(A[:], A[:], ACT.Exp).then_inc(a_negated.s, 1)
                with act.Fori(0, B) as b:
                    for ct in range(CT):
                        with act.Fori(0, CPB) as i:
                            act.wait_ge(xc_done.s, (b * CT + ct) * CPB + i + 1)
                            act.wait_ge(conv_done.s, conv_done.at(b * CT + ct))
                            nc.scalar.activation(xpad[:, ds(i * 8 + 1, 8), 1:1 + HW], ps[:, 0, 0:CH].rearrange("p (r w) -> p r w", w=HW),
                                                 ACT.Copy).then_inc(xc_out.s, 1)
                        act.wait_ge(conv_done.s, conv_done.at(b * CT + ct + 1))
                        nc.scalar.activation(Y[:, ct, :], u[:, ct, :], ACT.Sigmoid, bias=b_conv[:, ct:ct + 1]).then_inc(sg_ready.s, 1)
                    for kk in range(ND):
                        with act.Fori(0, NCS // 2) as o:
                            q0 = (b * ND + kk) * NCS + o * 2
                            for p in range(2):
                                q = q0 + p
                                act.wait_ge(abs_ready.s, q + 1)
                                nc.scalar.activation(e[:], e[:], ACT.Exp).then_inc(e_ready.s, 1)
                                act.wait_ge(w_ready.s, q + 1)
                                nc.scalar.activation(dt[:, p], w[:], ACT.Ln).then_inc(ln_ready.s, 1)
                            for i in range(2 * NS):
                                p, n, m = i // NS, i % NS, q0 * NS + i
                                act.wait_ge(a_negated.s, 2)
                                act.wait_ge(dt_ready.s, q0 + p + 1)
                                act.wait_ge(scan_done.s, scan_done.at(m - 1))
                                for ct in range(CT):
                                    ins = nc.scalar.activation(dA[:, n % 2, ct, :], dt[:, p, ct, :], ACT.Exp,
                                                               scale=A[:, kk, ct, n:n + 1])
                                ins.then_inc(a_ready.s, 1)
                                act.wait_ge(bc_done.s, m + 1)
                                act.wait_ge(hc_ready.s, hc_ready.at(m - 1))
                                nc.scalar.activation(Cs[:, n % 2, :], ps[:, 2 + n % 2, 0:CS], ACT.Copy).then_inc(c_copied.s, 1)
                    with act.Fori(0, CPB) as i:
                        it = b * CPB + i
                        act.wait_ge(z_done.s, it + 1)
                        act.wait_ge(x_done.s, x_done.at(it))
                        nc.scalar.activation(sz, ps[:, 2:4, 0:CH], ACT.Sigmoid).then_inc(sz_ready.s, 1)
                        act.wait_ge(yc_ready.s, it + 1)
                        nc.scalar.activation(sq, yc, ACT.Square).then_inc(sq_ready.s, 1)
                        act.wait_ge(var_done.s, it + 1)
                        nc.scalar.activation(std[:, 0, :], ps[:, 1, 0:CH], ACT.Sqrt, bias=eps[:]).then_inc(std_ready.s, 1)

            @block.gpsimd
            def _(pool):
                pool.sem_inc(hc_ready.s, hc_ready.credit)
                with pool.Fori(0, B) as b:
                    for kk in range(ND):
                        last = CS - 1 if kk < 2 else 0
                        with pool.Fori(0, NCS // 2) as o:
                            q0 = (b * ND + kk) * NCS + o * 2
                            for i in range(2 * NS):
                                n, m = i % NS, q0 * NS + i
                                pool.wait_ge(scan_done.s, scan_done.at(m + 1))
                                pool.wait_ge(c_copied.s, c_copied.at(m + 1))
                                pool.wait_ge(y_done.s, y_done.at(m - 1))
                                nc.gpsimd.tensor_tensor(hC[:, n % 2], h[:, n % 2], Cs[:, n % 2, :].unsqueeze(1).to_broadcast([C, CT, CS]),
                                                        ALU.mult)
                                nc.gpsimd.tensor_copy(state[:, :, n:n + 1], h[:, n % 2, :, last:last + 1]).then_inc(hc_ready.s, 1)

            @block.vector
            def _(dve):
                for q in (conv_done, delta_out, dbu_ready, scan_done, y_out, x_done):
                    dve.sem_inc(q.s, q.credit)
                v.memset(xpad[:], 0.0)
                v.memset(eps[:], 1e-5)
                dve.wait_ge(a_negated.s, 1)
                v.tensor_scalar(A[:], A[:], -1.0, None, ALU.mult).then_inc(a_negated.s, 1)
                for kk in range(ND):
                    for ct in range(CT):
                        ins = v.tensor_scalar(d_mat[:, kk, ct, :], k.ident[:], D[:, kk, ct:ct + 1], None, ALU.mult)
                ins.then_inc(d_ready.s, 1)
                PER_B = 1 + CT * 10
                PER_Q = 11
                with dve.Fori(0, B) as b:
                    chain = Chain(dve, conv_own.s, b * PER_B)
                    chain.link(v.tensor_scalar(xn[:], X[:, ds(b * L, L)], k.gn_nmean[:, ds(b, 1)], k.gn_rstd[:, ds(b, 1)],
                                               ALU.add, ALU.mult))
                    dve.sem_inc(xn_ready.s, 1)
                    for ct in range(CT):
                        dve.wait_ge(xc_out.s, xc_out.at((b * CT + ct + 1) * CPB))
                        image = u[:, ct, :].rearrange("p (r c) -> p r c", c=HW)
                        for tap in range(9):
                            src = xpad[:, tap // 3:tap // 3 + HW, tap % 3:tap % 3 + HW]
                            if tap == 0:
                                ins = v.tensor_scalar(image, src, w_taps[:, ct, 0:1], None, ALU.mult)
                            else:
                                ins = v.scalar_tensor_tensor(image, src, w_taps[:, ct, tap:tap + 1], image, ALU.mult, ALU.add)
                            chain.link(ins)
                        dve.sem_inc(conv_done.s, 1)
                        dve.wait_ge(sg_ready.s, b * CT + ct + 1)
                        chain.link(v.scalar_tensor_tensor(u[:, ct, :], u[:, ct, :], b_conv[:, ct:ct + 1], Y[:, ct, :],
                                                          ALU.add, ALU.mult))
                        dve.sem_inc(u_ready.s, 1)
                    assert chain.n == PER_B
                    for kk in range(ND):
                        dve.wait_ge(hc_ready.s, hc_ready.at((b * ND + kk) * (NCS * NS)))
                        v.memset(state[:], 0.0)
                        with dve.Fori(0, NCS // 2) as o:
                            f = forward(nc.vector, kk, o)
                            q0 = (b * ND + kk) * NCS + o * 2
                            chain = Chain(dve, own.s, q0 * PER_Q)
                            link = chain.link
                            for p in range(2):
                                q = q0 + p
                                dve.wait_ge(proj_done.s, q + 1)
                                link(v.tensor_copy(bc[:, p, :], ps[0:96, 6, 0:CS]))
                                link(v.tensor_tensor(rest[:], ps[0:96, 6, 0:CS], bc[:, p, :], ALU.subtract))
                                link(v.tensor_copy(mid[:], rest[:]))
                                v.tensor_copy(bc[32:64, p, :], mid[32:64, :])
                                v.tensor_tensor(bc[64:96, p, :], rest[64:96, :], mid[64:96, :], ALU.subtract).then_inc(split_done.s, 1)
                                v.tensor_copy(dtr[:], ps[0:DTR, 7, 0:CS]).then_inc(dtr_ready.s, 1)
                                dve.wait_ge(delta_done.s, q + 1)
                                for ct in range(CT):
                                    ins = v.tensor_scalar(xb[:, ct, :], ps[:, 6 + ct, 0:CS], b_dt[:, kk, ct:ct + 1], None, ALU.add)
                                    link(ins)
                                dve.sem_inc(delta_out.s, 1)
                                v.scalar_tensor_tensor(e[:], xb[:], -1.0, xb[:], ALU.mult, ALU.min).then_inc(abs_ready.s, 1)
                                dve.wait_ge(e_ready.s, q + 1)
                                link(v.tensor_scalar(w[:], e[:], 1.0, None, ALU.add))
                                dve.sem_inc(w_ready.s, 1)
                                link(v.scalar_tensor_tensor(e[:], w[:], -1.0, e[:], ALU.add, ALU.subtract))
                                dve.wait_ge(ln_ready.s, q + 1)
                                link(v.tensor_tensor(dt[:, p], dt[:, p], e[:], ALU.subtract))
                                link(v.scalar_tensor_tensor(dt[:, p], xb[:], 0.0, dt[:, p], ALU.max, ALU.add))
                                dve.sem_inc(dt_ready.s, 1)
                                for ct in range(CT):
                                    link(v.tensor_tensor(windows(dtu[:, p, ct, :]), windows(dt[:, p, ct, :]), u_view(ct, kk, f, p), ALU.mult))
                            assert chain.n == 2 * PER_Q
                            for p in range(2):
                                q = q0 + p
                                for n in range(NS):
                                    m, s = q * NS + n, n % 2
                                    dve.wait_ge(bc_done.s, m + 1)
                                    v.tensor_tensor(dBu[:, s], dtu[:, p], ps[:, s, 0:CS].unsqueeze(1).to_broadcast([C, CT, CS]),
                                                    ALU.mult).then_inc(dbu_ready.s, 1)
                                    dve.wait_ge(dbu_ready.s, dbu_ready.at(m + 1))
                                    dve.wait_ge(a_ready.s, m + 1)
                                    dve.wait_ge(hc_ready.s, hc_ready.at(m - 1))
                                    for ct in range(CT):
                                        ins = v.tensor_tensor_scan(order(h[:, s, ct, :], kk), order(dA[:, s, ct, :], kk),
                                                                   order(dBu[:, s, ct, :], kk), state[:, ct, n:n + 1],
                                                                   ALU.mult, ALU.add)
                                    ins.then_inc(scan_done.s, 1)
                                dve.wait_ge(y_done.s, y_done.at(q * NS + NS))
                                for ct in range(CT):
                                    dst, src = y_view(ct, kk, f, p), lines(ps[:, 4 + ct, 0:CS])
                                    if kk == 0:
                                        ins = v.tensor_copy(dst, src)
                                    else:
                                        ins = v.tensor_tensor(dst, dst, src, ALU.add)
                                ins.then_inc(y_out.s, 1)
                        dve.wait_ge(y_out.s, y_out.at((b * ND + kk + 1) * NCS))
                        v.memset(eps[:], 1e-5)
                    PER_I = 5
                    with dve.Fori(0, CPB) as i:
                        it = b * CPB + i
                        chain = Chain(dve, end_own.s, it * PER_I)
                        over = lambda t: t.unsqueeze(1).to_broadcast([C, CT, CH])
                        dve.wait_ge(m_done.s, it + 1)
                        v.tensor_tensor(yc, Y[:, :, ds(i * CH, CH)], over(ps[:, 0, 0:CH]), ALU.subtract).then_inc(yc_ready.s, 1)
                        dve.wait_ge(std_ready.s, it + 1)
                        chain.link(v.reciprocal(std[:, 0, :], std[:, 0, :]))
                        chain.link(v.tensor_tensor(yc, yc, over(std[:, 0, :]), ALU.mult))
                        for ct in range(CT):
                            chain.link(v.tensor_scalar(yc[:, ct, :], yc[:, ct, :], ln_w[:, ct:ct + 1], ln_b[:, ct:ct + 1], ALU.mult, ALU.add))
                        dve.wait_ge(sz_ready.s, it + 1)
                        chain.link(v.tensor_tensor(sz, sz, ps[:, 2:4, 0:CH], ALU.mult))
                        v.tensor_tensor(sz, sz, yc, ALU.mult).then_inc(g_ready.s, 1)
                        assert chain.n == PER_I
                        dve.wait_ge(out_done.s, it + 1)
                        xs = X[:, ds(b * L + i * CH, CH)]
                        v.tensor_tensor(xs, xs, ps[:, 4, 0:CH], ALU.add).then_inc(x_done.s, 1)


PHASES = {"load": load_x, "store": store_x, "gn0": lambda k: gn_stats(k, "gn0"), "l0": layer0,
          "ln2a": lambda k: layer_norm(k, "ln2a", 1e-5), "a2": lambda k: attention(k, "a2", 1, "w2_qkv", None),
          "gn1": lambda k: gn_stats(k, "gn1"), "l1": layer1,
          "ln2f": lambda k: layer_norm(k, "ln2f", 1e-5), "moe": experts,
          "ln3f": lambda k: layer_norm(k, "ln3f", 1e-5), "rnn": recurrence,
          "ln3a": lambda k: layer_norm(k, "ln3a", 1e-5), "a3": lambda k: attention(k, "a3", NH3, "w3_qkv", "w3_proj")}
ORDER = ["load", "gn0", "l0", "gn1", "l1", "ln2a", "a2", "ln2f", "moe", "ln3a", "a3", "ln3f", "rnn", "store"]


def build(nc, dram):
    with ExitStack() as ctx:
        k = Core(nc, ctx, dram)
        for name in ORDER:
            PHASES[name](k)
            k.end_phase()


def arrange(inputs):
    import numpy as np
    f = {n: np.ascontiguousarray(v) for n, v in inputs.items()}
    t = np.ascontiguousarray
    a = {"x": f["x"].reshape(T, C)}
    a["ident"] = np.eye(C, dtype=np.float32)
    a["mean_mat"] = np.full((C, C), 1.0 / C, np.float32)
    a["group_mat"] = np.kron(np.eye(C // 4), np.full((4, 4), 0.25)).astype(np.float32)
    a["w0_qkv"], a["b0_qkv"] = t(f["L0_conv_qkv_w"].T), t(f["L0_conv_qkv_b"].reshape(3, C).T)
    a["w0_proj"], a["b0_proj"] = t(f["L0_conv_proj_w"].T), f["L0_conv_proj_b"].reshape(C, 1)
    a["head_scale0"] = np.kron(np.eye(NH0), np.full((HD0, 1), HD0 ** -0.5)).astype(np.float32)
    ki = np.arange(8)[None, None, :, None] - np.arange(2)[:, None, None, None]
    kj = np.arange(WP)[None, None, None, :] - np.arange(HW)[None, :, None, None]
    ki, kj = (np.broadcast_to(v, (2, HW, 8, WP)).reshape(TILE, WIN) for v in (ki, kj))
    inside = (ki >= 0) & (ki < KS) & (kj >= 0) & (kj < KS)
    a["wmask"] = np.where(inside, 0.0, NEG).astype(np.float32)
    laid = f["L0_conv_rpb"][:, np.clip(ki, 0, KS - 1) + PAD, np.clip(kj, 0, KS - 1) + PAD]
    a["rpb_laid"] = t(laid.transpose(1, 0, 2))
    a["w1_in"] = t(f["L1_conv_W_in"].T)
    a["w1_taps"] = t(f["L1_conv_conv_w"].reshape(CT, C, 9).transpose(1, 0, 2))
    a["b1_conv"] = t(f["L1_conv_conv_b"].reshape(CT, C).T)
    xp = f["L1_conv_x_proj_w"].reshape(ND, DTR + 2 * NS, CT, C).transpose(3, 0, 2, 1)
    a["w1_dt_in"] = t(xp[..., :DTR])
    a["w1_bc"] = t(np.concatenate([xp[..., DTR:]] * 3, axis=-1))
    a["w1_dt"] = t(f["L1_conv_dt_proj_w"].transpose(2, 0, 1))
    a["b1_dt"] = t(f["L1_conv_dt_proj_b"].reshape(ND, CT, C).transpose(2, 0, 1))
    a["A_logs"] = t(f["L1_conv_A_logs"].reshape(ND, CT, C, NS).transpose(2, 0, 1, 3))
    a["D1"] = t(f["L1_conv_Ds"].reshape(ND, CT, C).transpose(2, 0, 1))
    a["ln1_w"], a["ln1_b"] = t(f["L1_conv_ln_w"].reshape(CT, C).T), t(f["L1_conv_ln_b"].reshape(CT, C).T)
    a["w1_out"] = t(f["L1_conv_W_out"].reshape(C, CT, C).transpose(2, 1, 0))
    a["mean256"] = np.full((C, C), 1.0 / DI, np.float32)
    one = np.tile(np.eye(2 * NS, dtype=np.float32), (3, 1))
    a["spread_bc"] = np.repeat(one[:, :, None], C, axis=2).astype(np.uint16) * np.uint16(0x3F80)
    key = np.arange(CH)[None, None, :]
    query = np.arange(TILE)[:, None, None] + TILE * np.arange(TPC)[None, :, None]
    a["causal_masks"] = np.where(key <= query, 0.0, NEG).astype(np.float32)
    a["w2_qkv"] = np.concatenate([f["L2_attn_Wq"], f["L2_attn_Wk"], f["L2_attn_Wv"]], axis=1)
    a["head_scale_a2"] = np.full((C, 1), L ** -0.5, np.float32)
    a["w3_qkv"], a["w3_proj"] = f["L3_attn_w_attn"], f["L3_attn_w_proj"]
    a["head_scale_a3"] = np.kron(np.eye(NH3), np.full((HD3, 1), HD3 ** -0.5)).astype(np.float32)
    a["w2_router"], a["b2_router"] = f["L2_ffn_router_w"], f["L2_ffn_router_b"].reshape(NE, 1)
    a["w2_expert"], a["b2_expert"] = t(f["L2_ffn_expert_w"].transpose(1, 0, 2)), f["L2_ffn_expert_b"]
    a["spread8"] = np.repeat(np.eye(NE, dtype=np.float32)[:, :, None], C, axis=2)
    a["rank8"] = np.broadcast_to(np.arange(NE, 0, -1).astype(np.float32), (TILE, NE)).copy()
    a["w3_in"], a["w3_v"] = t(f["L3_ffn_W"].T), t(f["L3_ffn_V"].T)
    a["gamma3"], a["beta3"] = f["L3_ffn_gamma"].reshape(C, 1), f["L3_ffn_beta"].reshape(C, 1)
    return a


def kernel(**inputs):
    import concourse.bacc as _bacc
    from concourse import mybir as _mybir
    from concourse.bass_utils import run_bass_kernel_spmd as _run

    nc = _bacc.Bacc("TRN2", target_bir_lowering=False, num_devices=1)
    arrays, dram = {}, {}
    for name, a in arrange(inputs).items():
        arrays[f"in_{name}_dram"] = a
        dram[name] = nc.dram_tensor(f"in_{name}_dram", a.shape, _mybir.dt.from_np(a.dtype), kind="ExternalInput").ap()
    dram["out"] = nc.dram_tensor("out_0_dram", (T, C), _mybir.dt.float32, kind="ExternalOutput").ap()
    build(nc, dram)
    r = _run(nc, [arrays], core_ids=[0])
    return r.results[0]["out_0_dram"].reshape(B, HW, HW, C)
```

```python
from contextlib import ExitStack

import concourse.bass as bass
from concourse import mybir

ALU = mybir.AluOpType
ACT = mybir.ActivationFunctionType
AX = mybir.AxisListType
F32 = mybir.dt.float32
BF16 = mybir.dt.bfloat16

C = 128
B = 4
HW = 56
L = HW * HW
T = B * L
TILE = 2 * HW
TPC = 4
CH = TPC * TILE
NCH = T // CH
CPB = L // CH
TPB = L // TILE

NH0, HD0, KS = 4, 32, 7
PAD = KS // 2
WP = HW + 2 * PAD
LP = WP * WP
PAIR = 2 * WP
NPAIR = WP // 2
WIN = 8 * WP
NWIN = WIN // PAIR
NEG = -1.0e30

DI, NS, DTR, ND = 256, 16, 8, 4
CT = DI // C
WS = HW // 4
CS = 2 * WS * WS
NCS = L // CS
RC = CS // HW

NE = 8
NH3, HD3 = 8, 16


def ds(start, size):
    return bass.ds(start, size)


class Chain:

    def __init__(self, eng, sem, base=0):
        self.eng, self.sem, self.base, self.n = eng, sem, base, 0

    def link(self, ins):
        self.n += 1
        ins.then_inc(self.sem, 1)
        self.eng.wait_ge(self.sem, self.base + self.n)


class Sem:

    def __init__(self, s, credit):
        self.s, self.credit = s, credit

    def at(self, n):
        return n + self.credit


class Core:

    def __init__(self, nc, ctx, dram):
        self.nc, self.ctx, self.dram = nc, ctx, dram
        self.handles = []
        self.X, self.N = self.sb("X", [C, T]), None
        self.ident = self.sb("ident", [C, C])
        self.mean_mat = self.sb("mean_mat", [C, C])
        self.gn_nmean, self.gn_rstd = self.sb("gn_nmean", [C, B]), self.sb("gn_rstd", [C, B])
        self.ps = ctx.enter_context(nc.psum_tensor("ps", [128, 8, 512], F32))

    def normed(self):
        if self.N is None:
            self.N = self.sb("N", [C, T])
        return self.N

    def sb(self, name, shape, dt=F32, ctx=None):
        return (ctx or self.ctx).enter_context(self.nc.sbuf_tensor(name, shape, dt))

    def sem(self, name, credit=0):
        handle = self.nc.alloc_semaphore(name=name)
        self.handles.append(handle)
        return Sem(handle, credit)

    def end_phase(self):
        self.nc.clear_and_free_semaphores(self.handles)
        self.nc.all_engine_barrier()
        self.handles = []

    def weights(self, block_sync, pairs, sem):
        for dst, src in pairs:
            block_sync.dma_start(dst, src).then_inc(sem, 16)
        return 16 * len(pairs)


def load_x(k):
    nc, X, ps = k.nc, k.X, k.ps
    src = k.dram["x"].rearrange("(t p) c -> p t c", p=TILE)
    with ExitStack() as ctx:
        xin = k.sb("ld_xin", [TILE, 2, TPC, C], ctx=ctx)
        consts_in, landed = k.sem("ld_consts").s, [k.sem("ld_landed0").s, k.sem("ld_landed1").s]
        turned, copied = [k.sem("ld_turned0").s, k.sem("ld_turned1").s], [k.sem("ld_copied0").s, k.sem("ld_copied1").s]
        with nc.Block() as block:
            @block.sync
            def _(sp):
                sp.dma_start(k.ident[:], k.dram["ident"]).then_inc(consts_in, 16)
                sp.dma_start(k.mean_mat[:], k.dram["mean_mat"]).then_inc(consts_in, 16)
                for s in range(2):
                    sp.dma_start(xin[:, s], src[:, s * TPC:(s + 1) * TPC, :]).then_inc(landed[s], 16)
                with sp.Fori(1, NCH // 2) as i:
                    for s in range(2):
                        sp.wait_ge(turned[s], i)
                        sp.dma_start(xin[:, s], src[:, ds(i * (2 * TPC) + s * TPC, TPC), :]).then_inc(landed[s], 16)

            @block.tensor
            def _(pe):
                pe.wait_ge(consts_in, 32)
                with pe.Fori(0, NCH // 2) as i:
                    for s in range(2):
                        pe.wait_ge(landed[s], i * 16 + 16)
                        pe.wait_ge(copied[s], i + 1)
                        for j in range(TPC):
                            last = nc.tensor.transpose(ps[:, s, j * TILE:(j + 1) * TILE], xin[:, s, j, :],
                                                       k.ident[0:TILE, 0:TILE])
                        last.then_inc(turned[s], 1)

            @block.vector
            def _(dve):
                for s in range(2):
                    dve.sem_inc(copied[s], 1)
                with dve.Fori(0, NCH // 2) as i:
                    for s in range(2):
                        dve.wait_ge(turned[s], i + 1)
                        nc.vector.tensor_copy(X[:, ds(i * (2 * CH) + s * CH, CH)], ps[:, s, 0:CH]).then_inc(copied[s], 1)


def store_x(k):
    nc, X, ps = k.nc, k.X, k.ps
    dst = k.dram["out"].rearrange("(t p) c -> p t c", p=TILE)
    with ExitStack() as ctx:
        xst = k.sb("st_in", [C, 2, CH], ctx=ctx)
        xout = k.sb("st_out", [TILE, 2, TPC, C], ctx=ctx)
        staged, turned, copied, stored = ([k.sem(f"st_{n}{s}").s for s in range(2)]
                                          for n in ("staged", "turned", "copied", "stored"))
        with nc.Block() as block:
            @block.scalar
            def _(act):
                for s in range(2):
                    act.sem_inc(turned[s], 1)
                with act.Fori(0, NCH // 2) as i:
                    for s in range(2):
                        act.wait_ge(turned[s], i + 1)
                        nc.scalar.activation(xst[:, s], X[:, ds(i * (2 * CH) + s * CH, CH)], ACT.Copy).then_inc(staged[s], 1)

            @block.tensor
            def _(pe):
                with pe.Fori(0, NCH // 2) as i:
                    for s in range(2):
                        pe.wait_ge(staged[s], i + 1)
                        pe.wait_ge(copied[s], i + 1)
                        for j in range(TPC):
                            last = nc.tensor.transpose(ps[0:TILE, s, j * C:(j + 1) * C], xst[:, s, j * TILE:(j + 1) * TILE],
                                                       k.ident[:])
                        last.then_inc(turned[s], 1)

            @block.vector
            def _(dve):
                for s in range(2):
                    dve.sem_inc(copied[s], 1)
                    dve.sem_inc(stored[s], 16)
                with dve.Fori(0, NCH // 2) as i:
                    for s in range(2):
                        dve.wait_ge(turned[s], i + 2)
                        dve.wait_ge(stored[s], i * 16 + 16)
                        nc.vector.tensor_copy(xout[:, s], ps[0:TILE, s, :]).then_inc(copied[s], 1)

            @block.sync
            def _(sp):
                with sp.Fori(0, NCH // 2) as i:
                    for s in range(2):
                        sp.wait_ge(copied[s], i + 2)
                        sp.dma_start(dst[:, ds(i * (2 * TPC) + s * TPC, TPC), :], xout[:, s]).then_inc(stored[s], 16)
                for s in range(2):
                    sp.wait_ge(stored[s], 16 * (NCH // 2) + 16)


def gn_stats(k, tag):
    nc, X, ps = k.nc, k.X, k.ps
    with ExitStack() as ctx:
        sb = lambda n, s, dt=F32: k.sb(f"{tag}_{n}", s, dt, ctx)
        sem = lambda n: k.sem(f"{tag}_{n}").s
        stats, mv = sb("stats", [C, NCH * 6]), sb("mv", [C, B, 2])
        moments, grp, gsq, gstd = sb("moments", [C, 2, B]), sb("grp", [C, 2, B]), sb("gsq", [C, B]), sb("gstd", [C, B])
        group_mat = sb("group_mat", [C, C])
        eps = sb("eps", [C, 1])
        mat_in, own, moments_ready, grouped, var_ready, std_ready = (
            sem(n) for n in ("mat_in", "own", "moments_ready", "grouped", "var_ready", "std_ready"))
        with nc.Block() as block:
            @block.sync
            def _(sp):
                sp.dma_start(group_mat[:], k.dram["group_mat"]).then_inc(mat_in, 16)

            @block.vector
            def _(dve):
                with dve.Fori(0, NCH) as i:
                    nc.vector.bn_stats(stats[:, ds(i * 6, 6)], X[:, ds(i * CH, CH)]).then_inc(own, 1)
                dve.wait_ge(own, NCH)
                c = Chain(dve, own, NCH)
                for b in range(B):
                    ins = nc.vector.bn_aggr(mv[:, b, :], stats[:, b * CPB * 6:(b + 1) * CPB * 6])
                    if b < B - 1:
                        ins.then_inc(own, 1)
                        c.n += 1
                c.link(ins)
                c.link(nc.vector.tensor_copy(moments[:, 0, :], mv[:, :, 0]))
                c.link(nc.vector.tensor_tensor(moments[:, 1, :], mv[:, :, 0], mv[:, :, 0], ALU.mult))
                nc.vector.tensor_tensor(moments[:, 1, :], moments[:, 1, :], mv[:, :, 1], ALU.add).then_inc(moments_ready, 1)
                dve.wait_ge(grouped, 1)
                c.link(nc.vector.tensor_copy(grp[:], ps[:, 0, 0:2 * B].rearrange("p (a b) -> p a b", a=2)))
                c.link(nc.vector.tensor_tensor(gsq[:], grp[:, 0, :], grp[:, 0, :], ALU.mult))
                c.link(nc.vector.tensor_tensor(gsq[:], grp[:, 1, :], gsq[:], ALU.subtract))
                nc.vector.tensor_scalar(gsq[:], gsq[:], 1e-5, None, ALU.add).then_inc(var_ready, 1)
                nc.vector.tensor_scalar(k.gn_nmean[:], grp[:, 0, :], -1.0, None, ALU.mult)
                dve.wait_ge(std_ready, 1)
                nc.vector.reciprocal(k.gn_rstd[:], gstd[:])

            @block.tensor
            def _(pe):
                pe.wait_ge(mat_in, 16)
                pe.wait_ge(moments_ready, 1)
                nc.tensor.matmul(ps[:, 0, 0:2 * B], group_mat[:], moments[:].rearrange("p a b -> p (a b)"),
                                 start=True, stop=True).then_inc(grouped, 1)

            @block.scalar
            def _(act):
                act.wait_ge(var_ready, 1)
                nc.scalar.activation(gstd[:], gsq[:], ACT.Sqrt).then_inc(std_ready, 1)


def layer0(k):
    nc, X, ps = k.nc, k.X, k.ps
    with ExitStack() as ctx:
        sb = lambda n, s, dt=F32: k.sb(f"a0_{n}", s, dt, ctx)
        sem = lambda n, credit=0: k.sem(f"a0_{n}", credit)
        wqkv, bqkv = sb("wqkv", [C, 3 * C]), sb("bqkv", [C, 3])
        wproj, bproj = sb("wproj", [C, C]), sb("bproj", [C, 1])
        head_scale = sb("head_scale", [C, NH0])
        bias, wmask = sb("bias", [TILE, NH0, WIN]), sb("wmask", [TILE, WIN])
        xn = sb("xn", [C, CH])
        Q, Kp, Vp = sb("Q", [C, L]), sb("Kp", [C, LP]), sb("Vp", [C, LP])
        vst, V = sb("vst", [C, PAIR]), sb("V", [PAIR, NPAIR, C])
        qh = sb("qh", [C, NH0, TILE])
        scored, P = sb("scored", [TILE, 2, WIN]), sb("P", [TILE, 2, WIN])
        PT = sb("PT", [PAIR, 2, NWIN * TILE])
        rmax, nmax = sb("rmax", [TILE, NH0]), sb("nmax", [TILE, NH0])
        rsum, rinv = sb("rsum", [TILE, NH0]), sb("rinv", [TILE, NH0])
        o, oT = sb("o", [TILE, C]), sb("oT", [C, TILE])
        junk = sb("junk", [1, 1])
        w_in, own = sem("w_in"), sem("own")
        xn_ready, qkv_done, q_out, kv_out = sem("xn_ready"), sem("qkv_done", 1), sem("q_out", 1), sem("kv_out")
        v_staged, v_turned, v_out = sem("v_staged"), sem("v_turned"), sem("v_out", 1)
        qh_ready, s_done, s_read, mx_ready = sem("qh_ready"), sem("s_done", 1), sem("s_read", 2), sem("mx_ready")
        p_ready, p_turned, pt_ready, pv_done = sem("p_ready", 2), sem("p_turned", 2), sem("pt_ready", 2), sem("pv_done", 2)
        o_ready, o_turned, ot_ready, proj_done, x_done = (
            sem(n) for n in ("o_ready", "o_turned", "ot_ready", "proj_done", "x_done"))
        loads = [(wqkv[:], "w0_qkv"), (bqkv[:], "b0_qkv"), (wproj[:], "w0_proj"), (bproj[:], "b0_proj"),
                 (head_scale[:], "head_scale0"), (bias[:], "rpb_laid"), (wmask[:], "wmask")]
        rows = lambda t: t[:].rearrange("p (r w) -> p r w", w=WP)

        with nc.Block() as block:
            @block.sync
            def _(sp):
                for dst, name in loads:
                    sp.dma_start(dst, k.dram[name]).then_inc(w_in.s, 16)

            @block.vector
            def _(dve):
                for q in (s_read, v_out):
                    dve.sem_inc(q.s, q.credit)
                nc.vector.memset(Kp[:], 0.0)
                nc.vector.memset(Vp[:], 0.0)
                dve.wait_ge(w_in.s, 16 * len(loads))
                for h in range(NH0):
                    ins = nc.vector.tensor_tensor(bias[:, h, :], bias[:, h, :], wmask[:], ALU.add)
                ins.then_inc(own.s, 1)
                dve.wait_ge(own.s, 1)
                with dve.Fori(0, B) as b:
                    with dve.Fori(0, CPB) as i:
                        it = b * CPB + i
                        dve.wait_ge(qkv_done.s, qkv_done.at(it * 3))
                        nc.vector.tensor_scalar(xn[:], X[:, ds(b * L + i * CH, CH)], k.gn_nmean[:, ds(b, 1)],
                                                k.gn_rstd[:, ds(b, 1)], ALU.add, ALU.mult).then_inc(xn_ready.s, 1)
                        for j, buf in ((1, Kp), (2, Vp)):
                            dve.wait_ge(qkv_done.s, qkv_done.at(it * 3 + j + 1))
                            nc.vector.tensor_scalar(rows(buf)[:, ds(i * 8 + PAD, 8), PAD:PAD + HW],
                                                    ps[:, j, 0:CH].rearrange("p (r w) -> p r w", w=HW),
                                                    bqkv[:, j:j + 1], None, ALU.add).then_inc(kv_out.s, 1)
                    with dve.Fori(0, NPAIR) as i:
                        dve.wait_ge(v_turned.s, b * NPAIR + i + 1)
                        nc.vector.tensor_copy(V[:, ds(i, 1), :].rearrange("p a c -> p (a c)"), ps[0:PAIR, 3, 0:C]).then_inc(v_out.s, 1)
                    with dve.Fori(0, TPB) as r:
                        it = b * TPB + r
                        n0 = it * NH0
                        dve.wait_ge(q_out.s, q_out.at((b + 1) * CPB))
                        dve.wait_ge(s_done.s, s_done.at(n0))
                        nc.vector.tensor_tensor(qh[:], Q[:, ds(r * TILE, TILE)].unsqueeze(1).to_broadcast([C, NH0, TILE]),
                                                head_scale[:].unsqueeze(2).to_broadcast([C, NH0, TILE]),
                                                ALU.mult).then_inc(qh_ready.s, 1)
                        for h in range(NH0):
                            s, n = h % 2, n0 + h
                            dve.wait_ge(s_done.s, s_done.at(n + 1))
                            dve.wait_ge(p_ready.s, p_ready.at(n - 1))
                            nc.vector.memset(junk[:], 0.0)
                            nc.vector.tensor_tensor_reduce(out=scored[:, s, :], in0=ps[0:TILE, s, 0:WIN], in1=bias[:, h, :],
                                                           scale=1.0, scalar=-3.0e38, op0=ALU.add, op1=ALU.max,
                                                           accum_out=rmax[:, h:h + 1]).then_inc(s_read.s, 1)
                            dve.wait_ge(s_read.s, s_read.at(n + 1))
                            nc.vector.tensor_scalar(nmax[:, h:h + 1], rmax[:, h:h + 1], -1.0, None, ALU.mult).then_inc(mx_ready.s, 1)
                        dve.wait_ge(p_ready.s, p_ready.at(n0 + NH0))
                        nc.vector.reciprocal(rinv[:], rsum[:]).then_inc(own.s, 1)
                        dve.wait_ge(own.s, it + 2)
                        dve.wait_ge(pv_done.s, pv_done.at(n0 + NH0))
                        nc.vector.tensor_tensor(o[:].rearrange("p (h d) -> p h d", h=NH0),
                                                ps[0:TILE, 4, 0:C].rearrange("p (h d) -> p h d", h=NH0),
                                                rinv[:].unsqueeze(2).to_broadcast([TILE, NH0, HD0]), ALU.mult).then_inc(o_ready.s, 1)
                        dve.wait_ge(proj_done.s, it + 1)
                        xs = X[:, ds(b * L + r * TILE, TILE)]
                        nc.vector.scalar_tensor_tensor(xs, ps[:, 6, 0:TILE], bproj[:, 0:1], xs, ALU.add, ALU.add)

            @block.scalar
            def _(act):
                for q in (p_ready, pt_ready, q_out):
                    act.sem_inc(q.s, q.credit)
                act.wait_ge(w_in.s, 16 * len(loads))

                def turned_out(n, s):
                    act.wait_ge(p_turned.s, p_turned.at(n + 1))
                    act.wait_ge(pv_done.s, pv_done.at(n - 1))
                    nc.scalar.activation(PT[:, s, :], ps[0:PAIR, 2 + s, 0:NWIN * TILE], ACT.Copy).then_inc(pt_ready.s, 1)

                with act.Fori(0, B) as b:
                    with act.Fori(0, CPB) as i:
                        act.wait_ge(qkv_done.s, qkv_done.at((b * CPB + i) * 3 + 1))
                        nc.scalar.activation(Q[:, ds(i * CH, CH)], ps[:, 0, 0:CH], ACT.Identity, bias=bqkv[:, 0:1]).then_inc(q_out.s, 1)
                    act.wait_ge(kv_out.s, (b + 1) * (2 * CPB))
                    with act.Fori(0, NPAIR) as i:
                        act.wait_ge(v_out.s, v_out.at(b * NPAIR + i))
                        nc.scalar.activation(vst[:], Vp[:, ds(i * PAIR, PAIR)], ACT.Copy).then_inc(v_staged.s, 1)
                    with act.Fori(0, TPB) as r:
                        it = b * TPB + r
                        for h in range(NH0):
                            s, n = h % 2, it * NH0 + h
                            act.wait_ge(mx_ready.s, n + 1)
                            act.wait_ge(p_turned.s, p_turned.at(n - 1))
                            nc.scalar.activation(P[:, s, :], scored[:, s, :], ACT.Exp, bias=nmax[:, h:h + 1],
                                                 accum_out=rsum[:, h:h + 1]).then_inc(p_ready.s, 1)
                            if h > 0:
                                turned_out(n - 1, 1 - s)
                        turned_out(it * NH0 + NH0 - 1, 1)
                        act.wait_ge(o_turned.s, it + 1)
                        nc.scalar.activation(oT[:], ps[:, 5, 0:TILE], ACT.Copy).then_inc(ot_ready.s, 1)

            @block.tensor
            def _(pe):
                for q in (qkv_done, s_done, p_turned, pv_done):
                    pe.sem_inc(q.s, q.credit)
                pe.wait_ge(w_in.s, 16 * len(loads))

                def scores(it, r, h):
                    n = it * NH0 + h
                    pe.wait_ge(s_read.s, s_read.at(n - 1))
                    nc.tensor.matmul(ps[0:TILE, h % 2, 0:WIN], qh[:, h, :], Kp[:, ds(r * PAIR, WIN)],
                                     start=True, stop=True).then_inc(s_done.s, 1)

                def turn(it, h):
                    s, n = h % 2, it * NH0 + h
                    pe.wait_ge(p_ready.s, p_ready.at(n + 1))
                    pe.wait_ge(pt_ready.s, pt_ready.at(n - 1))
                    for j in range(NWIN):
                        ins = nc.tensor.transpose(ps[0:PAIR, 2 + s, j * TILE:(j + 1) * TILE],
                                                  P[:, s, j * PAIR:(j + 1) * PAIR], k.ident[0:TILE, 0:TILE])
                    ins.then_inc(p_turned.s, 1)

                def weigh(it, r, h):
                    s, n = h % 2, it * NH0 + h
                    pe.wait_ge(pt_ready.s, pt_ready.at(n + 1))
                    for j in range(NWIN):
                        ins = nc.tensor.matmul(ps[0:TILE, 4, h * HD0:(h + 1) * HD0], PT[:, s, j * TILE:(j + 1) * TILE],
                                               V[:, ds(r + j, 1), h * HD0:(h + 1) * HD0].rearrange("p a c -> p (a c)"),
                                               start=(j == 0), stop=(j == NWIN - 1))
                    ins.then_inc(pv_done.s, 1)

                with pe.Fori(0, B) as b:
                    with pe.Fori(0, CPB) as i:
                        it = b * CPB + i
                        pe.wait_ge(xn_ready.s, it + 1)
                        pe.wait_ge(q_out.s, q_out.at(it))
                        for j in range(3):
                            nc.tensor.matmul(ps[:, j, 0:CH], wqkv[:, j * C:(j + 1) * C], xn[:],
                                             start=True, stop=True).then_inc(qkv_done.s, 1)
                    with pe.Fori(0, NPAIR) as i:
                        pe.wait_ge(v_staged.s, b * NPAIR + i + 1)
                        nc.tensor.transpose(ps[0:PAIR, 3, 0:C], vst[:], k.ident[:]).then_inc(v_turned.s, 1)
                    with pe.Fori(0, TPB) as r:
                        it = b * TPB + r
                        pe.wait_ge(v_out.s, v_out.at((b + 1) * NPAIR))
                        pe.wait_ge(qh_ready.s, it + 1)
                        scores(it, r, 0)
                        scores(it, r, 1)
                        turn(it, 0)
                        for h in range(2, NH0):
                            scores(it, r, h)
                            weigh(it, r, h - 2)
                            turn(it, h - 1)
                        weigh(it, r, NH0 - 2)
                        turn(it, NH0 - 1)
                        weigh(it, r, NH0 - 1)
                        pe.wait_ge(o_ready.s, it + 1)
                        nc.tensor.transpose(ps[:, 5, 0:TILE], o[:], k.ident[0:TILE, 0:TILE]).then_inc(o_turned.s, 1)
                        pe.wait_ge(ot_ready.s, it + 1)
                        nc.tensor.matmul(ps[:, 6, 0:TILE], wproj[:], oT[:], start=True, stop=True).then_inc(proj_done.s, 1)


def layer_norm(k, tag, eps_value):
    nc, X, N, ps = k.nc, k.X, k.normed(), k.ps
    with ExitStack() as ctx:
        sb = lambda n, s, dt=F32: k.sb(f"{tag}_{n}", s, dt, ctx)
        sem = lambda n, credit=0: k.sem(f"{tag}_{n}", credit)
        xc, sq, std = sb("xc", [C, 2, CH]), sb("sq", [C, 2, CH]), sb("std", [C, 2, CH])
        eps = sb("eps", [C, 1])
        two = lambda n, credit=0: [sem(f"{n}{i}", credit) for i in range(2)]
        eps_set, mean_done, centred, squared, var_done, std_ready, inverted, done = (
            sem("eps_set"), two("mean_done"), two("centred", 1), two("squared", 1), two("var_done", 1),
            two("std_ready", 1), two("inverted", 1), two("done", 1))
        with nc.Block() as block:
            @block.tensor
            def _(pe):
                for s in range(2):
                    pe.sem_inc(var_done[s].s, 1)
                with pe.Fori(0, NCH // 2) as i:
                    for s in range(2):
                        pe.wait_ge(centred[s].s, centred[s].at(i))
                        nc.tensor.matmul(ps[:, s, 0:CH], k.mean_mat[:], X[:, ds(i * (2 * CH) + s * CH, CH)],
                                         start=True, stop=True).then_inc(mean_done[s].s, 1)
                    for s in range(2):
                        pe.wait_ge(squared[s].s, squared[s].at(i + 1))
                        pe.wait_ge(std_ready[s].s, std_ready[s].at(i))
                        nc.tensor.matmul(ps[:, 2 + s, 0:CH], k.mean_mat[:], sq[:, s, :],
                                         start=True, stop=True).then_inc(var_done[s].s, 1)

            @block.scalar
            def _(act):
                for s in range(2):
                    act.sem_inc(squared[s].s, 1)
                    act.sem_inc(std_ready[s].s, 1)
                act.wait_ge(eps_set.s, 1)
                with act.Fori(0, NCH // 2) as i:
                    for s in range(2):
                        act.wait_ge(centred[s].s, centred[s].at(i + 1))
                        act.wait_ge(var_done[s].s, var_done[s].at(i))
                        nc.scalar.activation(sq[:, s, :], xc[:, s, :], ACT.Square).then_inc(squared[s].s, 1)
                    for s in range(2):
                        act.wait_ge(var_done[s].s, var_done[s].at(i + 1))
                        act.wait_ge(inverted[s].s, inverted[s].at(i))
                        nc.scalar.activation(std[:, s, :], ps[:, 2 + s, 0:CH], ACT.Sqrt, bias=eps[:]).then_inc(std_ready[s].s, 1)

            @block.vector
            def _(dve):
                nc.vector.memset(eps[:], eps_value).then_inc(eps_set.s, 1)
                for s in range(2):
                    dve.sem_inc(centred[s].s, 1)
                    dve.sem_inc(inverted[s].s, 1)
                    dve.sem_inc(done[s].s, 1)
                with dve.Fori(0, NCH // 2) as i:
                    for s in range(2):
                        dve.wait_ge(mean_done[s].s, i + 1)
                        dve.wait_ge(done[s].s, done[s].at(i))
                        nc.vector.tensor_tensor(xc[:, s, :], X[:, ds(i * (2 * CH) + s * CH, CH)], ps[:, s, 0:CH],
                                                ALU.subtract).then_inc(centred[s].s, 1)
                    for s in range(2):
                        dve.wait_ge(std_ready[s].s, std_ready[s].at(i + 1))
                        dve.wait_ge(done[s].s, done[s].at(i))
                        nc.vector.reciprocal(std[:, s, :], std[:, s, :]).then_inc(inverted[s].s, 1)
                        dve.wait_ge(inverted[s].s, inverted[s].at(i + 1))
                        nc.vector.tensor_tensor(N[:, ds(i * (2 * CH) + s * CH, CH)], xc[:, s, :], std[:, s, :],
                                                ALU.mult).then_inc(done[s].s, 1)


def attention(k, tag, heads, wqkv_name, wproj_name):
    nc, X, N, ps = k.nc, k.X, k.normed(), k.ps
    H, hd = heads, C // heads
    HP = max(1, H // 2)
    with ExitStack() as ctx:
        sb = lambda n, s, dt=F32: k.sb(f"{tag}_{n}", s, dt, ctx)
        sem = lambda n, credit=0: k.sem(f"{tag}_{n}", credit)
        wqkv = sb("wqkv", [C, 3 * C])
        wproj = sb("wproj", [C, C]) if wproj_name else None
        head_scale, masks = sb("head_scale", [C, H]), sb("masks", [TILE, TPC, CH])
        Q, K, V = sb("Q", [C, L]), sb("K", [C, L]), sb("V", [TILE, TPB, C])
        ncs = sb("ncs", [C, CH])
        qh, row = sb("qh", [C, 2, TILE]), sb("row", [TILE, 2, L])
        PT = sb("PT", [TILE, 2, CH])
        rmax, nmax, rsum, rinv = (sb(n, [TILE, 2]) for n in ("rmax", "nmax", "rsum", "rinv"))
        o, oT = sb("o", [TILE, 2, C]), sb("oT", [C, TILE])
        w_in, own, n_copied, qkv_done, q_out, kv_out = (
            sem("w_in"), sem("own"), sem("n_copied"), sem("qkv_done", 1), sem("q_out", 1), sem("kv_out", 1))
        qh_ready, s_done, s_read, row_max, neg_max = sem("qh_ready"), sem("s_done"), sem("s_read", 2), sem("row_max"), sem("neg_max")
        p_ready, pt_ready, pv_blk = sem("p_ready"), sem("pt_ready", 2), sem("pv_blk", 2)
        inverted, o_ready, o_turned, ot_ready, proj_done, x_done = (
            sem("inverted"), sem("o_ready"), sem("o_turned"), sem("ot_ready"), sem("proj_done"), sem("x_done", 2))
        blk_turned = sem("blk_turned")
        loads = [(wqkv[:], wqkv_name), (head_scale[:], f"head_scale_{tag}"), (masks[:], "causal_masks")]
        if wproj_name:
            loads.append((wproj[:], wproj_name))

        def steps(eng, b, body):
            for I in range(TPB // TPC):
                nb = b * (TPB * H) + I * TPC * H
                gb = b * (TPC * H * sum(range(1, TPB // TPC + 1))) + TPC * H * (I * (I + 1) // 2)
                if H == 1:
                    with eng.Fori(0, TPC // 2) as jp:
                        body(I, [(jp * 2 + s, None, s, nb + jp * 2 + s, gb + (jp * 2 + s) * (I + 1)) for s in range(2)], None)
                else:
                    with eng.Fori(0, TPC) as j:
                        with eng.Fori(0, HP) as hp:
                            body(I, [(j, hp * 2 + s, s, nb + j * H + hp * 2 + s, gb + (j * H + hp * 2 + s) * (I + 1))
                                     for s in range(2)], None)
                        body(I, [], (j, b * TPB + I * TPC + j))

        with nc.Block() as block:
            @block.sync
            def _(sp):
                for dst, name in loads:
                    sp.dma_start(dst, k.dram[name]).then_inc(w_in.s, 16)

            @block.vector
            def _(dve):
                for q in (s_read, kv_out, x_done):
                    dve.sem_inc(q.s, q.credit)
                dve.wait_ge(w_in.s, 16 * len(loads))
                with dve.Fori(0, B) as b:
                    with dve.Fori(0, CPB) as i:
                        it = b * CPB + i
                        dve.wait_ge(qkv_done.s, qkv_done.at(it * 3))
                        nc.vector.tensor_copy(ncs[:], N[:, ds(b * L + i * CH, CH)]).then_inc(n_copied.s, 1)
                        dve.wait_ge(qkv_done.s, qkv_done.at(it * 3 + 2))
                        nc.vector.tensor_copy(K[:, ds(i * CH, CH)], ps[:, 1, 0:CH]).then_inc(kv_out.s, 1)
                        dve.wait_ge(qkv_done.s, qkv_done.at(it * 3 + 3))
                        nc.vector.tensor_copy(V[:, ds(i * TPC, TPC), :], ps[0:TILE, 2, :].rearrange("p (t c) -> p t c", c=C)).then_inc(kv_out.s, 1)

                    def body(I, items, tile):
                        for j, h, s, n, g in items:
                            dve.wait_ge(q_out.s, q_out.at((b + 1) * CPB))
                            nc.vector.tensor_scalar(qh[:, s, :], Q[:, ds((j + I * TPC) * TILE, TILE)],
                                                    head_scale[:, 0:1] if h is None else head_scale[:, ds(h, 1)],
                                                    None, ALU.mult).then_inc(qh_ready.s, 1)
                            for c in range(I + 1):
                                dve.wait_ge(s_done.s, g + c + 1)
                                dst, src = row[:, s, c * CH:(c + 1) * CH], ps[0:TILE, 2 * s + c % 2, 0:CH]
                                if c < I:
                                    nc.vector.tensor_copy(dst, src).then_inc(s_read.s, 1)
                                else:
                                    nc.vector.tensor_tensor(dst, src, masks[:, ds(j, 1), :].rearrange("p a k -> p (a k)"),
                                                            ALU.add).then_inc(s_read.s, 1)
                            dve.wait_ge(s_read.s, s_read.at(g + I + 1))
                            nc.vector.tensor_reduce(rmax[:, s:s + 1], row[:, s, 0:(I + 1) * CH], AX.X, ALU.max).then_inc(row_max.s, 1)
                            dve.wait_ge(row_max.s, n + 1)
                            nc.vector.tensor_scalar(nmax[:, s:s + 1], rmax[:, s:s + 1], -1.0, None, ALU.mult).then_inc(neg_max.s, 1)
                        for j, h, s, n, g in items:
                            dve.wait_ge(p_ready.s, n + 1)
                            nc.vector.reciprocal(rinv[:, s:s + 1], rsum[:, s:s + 1]).then_inc(inverted.s, 1)
                            dve.wait_ge(inverted.s, n + 1)
                            dve.wait_ge(pv_blk.s, pv_blk.at(g + I + 1))
                            dst = o[:, s, :] if h is None else o[:, 0, ds(h * hd, hd)]
                            nc.vector.tensor_scalar(dst, ps[0:TILE, 6 + s, 0:hd], rinv[:, s:s + 1], None, ALU.mult).then_inc(o_ready.s, 1)
                        if H == 1:
                            for j, h, s, n, g in items:
                                dve.wait_ge(o_turned.s, n + 1)
                                xs = X[:, ds(b * L + (j + I * TPC) * TILE, TILE)]
                                nc.vector.tensor_tensor(xs, xs, ps[:, 6 + s, C:C + TILE], ALU.add).then_inc(x_done.s, 1)
                        elif tile:
                            j, t = tile
                            dve.wait_ge(proj_done.s, t + 1)
                            xs = X[:, ds(b * L + (j + I * TPC) * TILE, TILE)]
                            nc.vector.tensor_tensor(xs, xs, ps[:, 7, C:C + TILE], ALU.add).then_inc(x_done.s, 1)

                    steps(dve, b, body)

            @block.scalar
            def _(act):
                for q in (pt_ready, q_out):
                    act.sem_inc(q.s, q.credit)
                with act.Fori(0, B) as b:
                    with act.Fori(0, CPB) as i:
                        act.wait_ge(qkv_done.s, qkv_done.at((b * CPB + i) * 3 + 1))
                        nc.scalar.activation(Q[:, ds(i * CH, CH)], ps[:, 0, 0:CH], ACT.Copy).then_inc(q_out.s, 1)

                    def body(I, items, tile):
                        for j, h, s, n, g in items:
                            act.wait_ge(neg_max.s, n + 1)
                            p = row[:, s, 0:(I + 1) * CH]
                            nc.scalar.activation(p, p, ACT.Exp, bias=nmax[:, s:s + 1], accum_out=rsum[:, s:s + 1]).then_inc(p_ready.s, 1)
                            for c in range(I + 1):
                                act.wait_ge(blk_turned.s, g + c + 1)
                                act.wait_ge(pv_blk.s, pv_blk.at(g + c - (1 if c else 0)))
                                nc.scalar.activation(PT[:, c % 2, :], ps[0:TILE, 4 + c % 2, 0:CH], ACT.Copy).then_inc(pt_ready.s, 1)
                        if tile:
                            act.wait_ge(o_turned.s, tile[1] + 1)
                            nc.scalar.activation(oT[:], ps[:, 6, C:C + TILE], ACT.Copy).then_inc(ot_ready.s, 1)

                    steps(act, b, body)

            @block.tensor
            def _(pe):
                for q in (qkv_done, pv_blk):
                    pe.sem_inc(q.s, q.credit)
                pe.wait_ge(w_in.s, 16 * len(loads))
                with pe.Fori(0, B) as b:
                    with pe.Fori(0, CPB) as i:
                        it = b * CPB + i
                        pe.wait_ge(n_copied.s, it + 1)
                        pe.wait_ge(q_out.s, q_out.at(it))
                        for j in range(2):
                            nc.tensor.matmul(ps[:, j, 0:CH], wqkv[:, j * C:(j + 1) * C], ncs[:],
                                             start=True, stop=True).then_inc(qkv_done.s, 1)
                        for t in range(TPC):
                            ins = nc.tensor.matmul(ps[0:TILE, 2, t * C:(t + 1) * C], ncs[:, t * TILE:(t + 1) * TILE],
                                                   wqkv[:, 2 * C:3 * C], start=True, stop=True)
                        ins.then_inc(qkv_done.s, 1)

                    def body(I, items, tile):
                        for j, h, s, n, g in items:
                            pe.wait_ge(kv_out.s, kv_out.at((b + 1) * (2 * CPB)))
                            pe.wait_ge(qh_ready.s, n + 1)
                            for c in range(I + 1):
                                pe.wait_ge(s_read.s, s_read.at(g + c - 1))
                                nc.tensor.matmul(ps[0:TILE, 2 * s + c % 2, 0:CH], qh[:, s, :], K[:, c * CH:(c + 1) * CH],
                                                 start=True, stop=True).then_inc(s_done.s, 1)
                        for j, h, s, n, g in items:
                            pe.wait_ge(p_ready.s, n + 1)
                            if H == 1:
                                pe.wait_ge(x_done.s, x_done.at(n - 1))
                            for c in range(I + 1):
                                pe.wait_ge(pt_ready.s, pt_ready.at(g + c - (1 if c else 0)))
                                for t in range(TPC):
                                    ins = nc.tensor.transpose(ps[0:TILE, 4 + c % 2, t * TILE:(t + 1) * TILE],
                                                              row[:, s, c * CH + t * TILE:c * CH + (t + 1) * TILE],
                                                              k.ident[0:TILE, 0:TILE])
                                ins.then_inc(blk_turned.s, 1)
                                if c > 0:
                                    weigh(I, c - 1, h, s, n, g)
                            weigh(I, I, h, s, n, g)
                        if H == 1:
                            for j, h, s, n, g in items:
                                pe.wait_ge(o_ready.s, n + 1)
                                nc.tensor.transpose(ps[:, 6 + s, C:C + TILE], o[:, s, :], k.ident[0:TILE, 0:TILE]).then_inc(o_turned.s, 1)
                        elif tile:
                            t = tile[1]
                            pe.wait_ge(o_ready.s, (t + 1) * H)
                            nc.tensor.transpose(ps[:, 6, C:C + TILE], o[:, 0, :], k.ident[0:TILE, 0:TILE]).then_inc(o_turned.s, 1)
                            pe.wait_ge(ot_ready.s, t + 1)
                            nc.tensor.matmul(ps[:, 7, C:C + TILE], wproj[:], oT[:], start=True, stop=True).then_inc(proj_done.s, 1)
                            pe.wait_ge(x_done.s, x_done.at(t + 1))

                    def weigh(I, c, h, s, n, g):
                        pe.wait_ge(pt_ready.s, pt_ready.at(g + c + 1))
                        for t in range(TPC):
                            v = V[:, c * TPC + t, :] if h is None else V[:, c * TPC + t, ds(h * hd, hd)]
                            first, last = c == 0 and t == 0, c == I and t == TPC - 1
                            ins = nc.tensor.matmul(ps[0:TILE, 6 + s, 0:hd], PT[:, c % 2, t * TILE:(t + 1) * TILE], v,
                                                   start=first, stop=last)
                        ins.then_inc(pv_blk.s, 1)

                    steps(pe, b, body)


def attention_heads(k, tag):
    nc, X, N, ps = k.nc, k.X, k.normed(), k.ps
    v, g = nc.vector, nc.gpsimd
    H, D = NH3, HD3
    NI = TPB // TPC
    ROWS = 6 * D
    KR = ROWS + 3
    VC = 32
    Q_PARTS, K_PARTS = (0, 0, 1, 1, 0, 2), (0, 1, 0, 1, 2, 0)
    with ExitStack() as ctx:
        sb = lambda n, s, dt=F32: k.sb(f"{tag}_{n}", s, dt, ctx)
        sem = lambda n, credit=0: k.sem(f"{tag}_{n}", credit)
        wqkv, wproj = sb("wqkv", [C, 3 * C]), sb("wproj", [C, C])
        identb = sb("identb", [TILE, TILE], BF16)
        tri, triT, full = (sb(n, [TILE, TILE], BF16) for n in ("tri", "triT", "full"))
        part = [sb(f"part{i}", [TILE, TPC, 2, C], BF16) for i in range(3)]
        stack = [sb(n, [TILE, TPC, H, ROWS], BF16) for n in ("q_stack", "k_stack")]
        KT, QT = sb("KT", [KR, H, L], BF16), sb("QT", [KR, H, CH], BF16)
        V, Vh = sb("V", [TILE, TPB, H, D]), sb("Vh", [TILE, 2, TPB, VC])
        fold = sb("fold", [C, D + 1])
        PT = sb("PT", [TILE, 2, 2, CH])
        rest = PT[:].rearrange("p a b c -> p (a b c)")[:, 0:TPC * 2 * C].rearrange("p (t a c) -> p t a c", t=TPC, a=2)
        maxes, nmax, nrest = sb("maxes", [TILE, TPC, NI]), sb("nmax", [TILE, TPC]), sb("nrest", [TILE, TPC])
        mrow = sb("mrow", [TILE, TPC, KR], BF16)
        rinv, oT = sb("rinv", [TILE, TPC]), sb("oT", [C, CH])
        o = part[0][:].rearrange("p t a c -> p t (a c)").bitcast(F32)
        zero, junk, zero_set = sb("zero", [TILE, 1]), sb("junk", [TILE, 3]), sem("zero_set")
        ncs = oh = oT
        w_in, own, const_ready = sem("w_in"), sem("own"), sem("const_ready")
        ncs_ready, tok_done, split_done, v_copied = sem("ncs_ready"), sem("tok_done"), sem("split_done"), sem("v_copied")
        hi_done, mid_done, lo_done = sem("hi_done"), sem("mid_done"), sem("lo_done")
        qk_read, q_stacked, inverted = sem("qk_read"), sem("q_stacked"), sem("inverted")
        vh_ready, oh_ready, folded = sem("vh_ready"), sem("oh_ready", 2), sem("folded")
        turned, q_out, k_out = sem("turned"), sem("q_out", 2), sem("k_out", 2)
        sm_done, sm_read, mrow_ready, mrow_turned, qm_ready = (
            sem("sm_done"), sem("sm_read", 2), sem("mrow_ready"), sem("mrow_turned"), sem("qm_ready"))
        st_done, p_ready, pv_done, o_read = sem("st_done"), sem("p_ready", 2), sem("pv_done", 2), sem("o_read", 2)
        o_turned, ot_ready, proj_done, x_done = sem("o_turned"), sem("ot_ready"), sem("proj_done"), sem("x_done", 1)
        u16 = mybir.dt.uint16
        loads = [(wqkv[:], "w3_qkv"), (wproj[:], "w3_proj"), (identb[:].bitcast(u16), "identb"),
                 (tri[:].bitcast(u16), "tri"), (triT[:].bitcast(u16), "triT"),
                 (full[:].bitcast(u16), "full"), (fold[:], "fold")]
        bank16 = lambda i: ps[:, i, :].bitcast(BF16)

        unit0 = lambda b, I, h: b * (H * 2 * NI * (NI + 1)) + H * 2 * I * (I + 1) + h * (4 * (I + 1))
        pair0 = lambda b, I, h: b * (H * NI * (NI + 1)) + H * I * (I + 1) + h * (2 * (I + 1))

        def heads(eng, first, step, last):
            first()
            with eng.Fori(0, (H - 2) // 2) as i:
                step(i * 2, i * 2 + 2, i * 2 + 1, 0)
                step(i * 2 + 1, i * 2 + 3, i * 2 + 2, 1)
            step(H - 2, None, H - 1, 0)
            step(H - 1, None, None, 1)
            last()

        with nc.Block() as block:
            @block.sync
            def _(sp):
                for dst, name in loads:
                    sp.dma_start(dst, k.dram[name]).then_inc(w_in.s, 16)

            @block.gpsimd
            def _(pool):
                g.memset(zero[:], 0.0).then_inc(zero_set.s, 1)
                pool.wait_ge(zero_set.s, 1)
                with pool.Fori(0, B) as b:
                    with pool.Fori(0, NI) as i:
                        it = b * NI + i
                        pool.wait_ge(lo_done.s, it + 1)
                        g.tensor_tensor(junk[:, 2:3], zero[:], zero[:], ALU.mult)
                        for r in range(6):
                            for t in range(TPC):
                                ins = g.tensor_copy(stack[1][:, t, :, r * D:(r + 1) * D],
                                                    part[K_PARTS[r]][:, t, 1, :].rearrange("p (h d) -> p h d", d=D))
                        ins.then_inc(split_done.s, 1)

                        def stage_values(h, s):
                            pool.wait_ge(v_copied.s, it + 1)
                            pool.wait_ge(oh_ready.s, oh_ready.at(it * H + h - 1))
                            g.tensor_tensor(junk[:, s:s + 1], zero[:], zero[:], ALU.mult)
                            g.tensor_copy(Vh[:, s, :, 0:D], V[:, :, ds(h, 1), :].rearrange("p t a d -> p (t a) d")).then_inc(vh_ready.s, 1)

                        with pool.Fori(0, H // 2) as hh:
                            for s in range(2):
                                stage_values(hh * 2 + s, s)

            @block.vector
            def _(dve):
                for q in (q_out, sm_read, o_read, x_done):
                    dve.sem_inc(q.s, q.credit)
                v.memset(KT[ROWS:KR], 1.0)
                v.memset(V[:], 0.0)
                v.memset(Vh[:, :, :, D + 1:VC], 0.0)
                v.memset(Vh[:, :, :, D:D + 1], 1.0)
                v.memset(mrow[:], 0.0).then_inc(const_ready.s, 1)
                dve.wait_ge(w_in.s, 16 * len(loads))
                with dve.Fori(0, B) as b:
                    for I in range(NI):
                        it = b * NI + I
                        v.tensor_copy(ncs[:], N[:, ds(b * L + I * CH, CH)]).then_inc(ncs_ready.s, 1)
                        dve.wait_ge(tok_done.s, it + 1)
                        flat = lambda t: t[:].rearrange("p t a c -> p t (a c)")
                        v.tensor_copy(flat(part[0]), ps[0:TILE, 0:TPC, 0:2 * C]).then_inc(hi_done.s, 1)
                        dve.wait_ge(hi_done.s, it + 1)
                        restf = rest.rearrange("p t a c -> p t (a c)")
                        v.tensor_tensor(restf, ps[0:TILE, 0:TPC, 0:2 * C], flat(part[0]), ALU.subtract).then_inc(qk_read.s, 1)
                        dve.wait_ge(qk_read.s, it + 1)
                        v.tensor_copy(flat(part[1]), restf).then_inc(mid_done.s, 1)
                        dve.wait_ge(mid_done.s, it + 1)
                        v.tensor_tensor(flat(part[2]), restf, flat(part[1]), ALU.subtract).then_inc(lo_done.s, 1)
                        dve.wait_ge(lo_done.s, it + 1)
                        for r in range(6):
                            for t in range(TPC):
                                ins = v.tensor_copy(stack[0][:, t, :, r * D:(r + 1) * D],
                                                    part[Q_PARTS[r]][:, t, 0, :].rearrange("p (h d) -> p h d", d=D))
                        ins.then_inc(q_stacked.s, 1)
                        for h in range(H):
                            dve.wait_ge(turned.s, it * H + h + 1)
                            v.tensor_copy(QT[0:ROWS, h, :], bank16(4 + h % 2)[0:ROWS, 0:CH]).then_inc(q_out.s, 1)

                        def reduces(h):
                            for u in range(4 * (I + 1)):
                                j, c = u // (I + 1), u % (I + 1)
                                n = unit0(b, I, h) + u
                                dve.wait_ge(sm_done.s, n + 1)
                                w = CH if c < I else (j + 1) * TILE
                                v.tensor_reduce(maxes[:, j, c:c + 1], ps[0:TILE, u % 2, 0:w], AX.X, ALU.max).then_inc(sm_read.s, 1)

                        def max_parts(h):
                            hn = it * H + h
                            dve.wait_ge(sm_read.s, sm_read.at(unit0(b, I, h) + 4 * (I + 1)))
                            chain = Chain(dve, own.s, hn * 6)
                            link = chain.link
                            link(v.tensor_reduce(nmax[:], maxes[:, :, 0:I + 1], AX.X, ALU.max))
                            link(v.tensor_scalar(nmax[:], nmax[:], -1.0, None, ALU.mult))
                            link(v.tensor_copy(mrow[:, :, ROWS], nmax[:]))
                            link(v.tensor_tensor(nrest[:], nmax[:], mrow[:, :, ROWS], ALU.subtract))
                            link(v.tensor_copy(mrow[:, :, ROWS + 1], nrest[:]))
                            link(v.tensor_tensor(mrow[:, :, ROWS + 2], nrest[:], mrow[:, :, ROWS + 1], ALU.subtract))
                            dve.sem_inc(mrow_ready.s, 1)

                        def first():
                            reduces(0)
                            max_parts(0)
                            reduces(1)

                        def step(h, hm, ht, s):
                            hn = it * H + h
                            if ht is not None:
                                dve.wait_ge(mrow_turned.s, hn + 1)
                                max_parts(ht)
                            if hm is not None:
                                reduces(hm)
                            dve.wait_ge(folded.s, hn + 1)
                            O = ps[0:TILE, 2, 256:256 + TPC * (D + 1)].rearrange("p (t d) -> p t d", d=D + 1)
                            v.reciprocal(rinv[:], O[:, :, D]).then_inc(inverted.s, 1)
                            dve.wait_ge(inverted.s, hn + 1)
                            v.tensor_tensor(o[:, :, ds(h * D, D)], O[:, :, 0:D],
                                            rinv[:].unsqueeze(2).to_broadcast([TILE, TPC, D]), ALU.mult).then_inc(o_read.s, 1)

                        def last():
                            dve.wait_ge(proj_done.s, it + 1)
                            xs = X[:, ds(b * L + I * CH, CH)]
                            v.tensor_tensor(xs, xs, ps[:, 0, 0:CH], ALU.add).then_inc(x_done.s, 1)

                        heads(dve, first, step, last)

            @block.scalar
            def _(act):
                for q in (k_out, p_ready, oh_ready):
                    act.sem_inc(q.s, q.credit)
                with act.Fori(0, B) as b:
                    for I in range(NI):
                        it = b * NI + I
                        for t in range(TPC):
                            act.wait_ge(const_ready.s, 1)
                            act.wait_ge(qk_read.s, it + 1)
                            ins = nc.scalar.activation(V[:, I * TPC + t, :, 0:D],
                                                       ps[0:TILE, t, 2 * C:3 * C].rearrange("p (h d) -> p h d", d=D), ACT.Copy)
                        ins.then_inc(v_copied.s, 1)
                        for h in range(H):
                            act.wait_ge(q_out.s, q_out.at(it * H + h + 1))
                            nc.scalar.activation(KT[0:ROWS, h, I * CH:(I + 1) * CH], bank16(4 + h % 2)[0:ROWS, CH:2 * CH],
                                                 ACT.Copy).then_inc(k_out.s, 1)

                        def max_out(h):
                            act.wait_ge(mrow_turned.s, it * H + h + 1)
                            nc.scalar.activation(QT[ROWS:KR, ds(h, 1), :].rearrange("p a c -> p (a c)"),
                                                 bank16(2)[ROWS:KR, 0:CH], ACT.Copy).then_inc(qm_ready.s, 1)

                        def step(h, hm, ht, s):
                            for e in range(2 * (I + 1)):
                                n = pair0(b, I, h) + e
                                w = CH if e < 2 * I + 1 or I == 0 else CH // 2
                                act.wait_ge(st_done.s, n + 1)
                                act.wait_ge(pv_done.s, pv_done.at(n - 1))
                                bank = 3 + 2 * (e % 2)
                                nc.scalar.activation(PT[:, e % 2, :, 0:w], ps[0:TILE, bank:bank + 2, 0:w], ACT.Exp,
                                                     scale=D ** -0.5).then_inc(p_ready.s, 1)
                                if e == 1 and ht is not None:
                                    max_out(ht)
                            act.wait_ge(pv_done.s, pv_done.at(pair0(b, I, h) + 2 * (I + 1)))
                            nc.scalar.activation(oh[:], ps[:, 7, 0:CH], ACT.Copy).then_inc(oh_ready.s, 1)

                        def last():
                            act.wait_ge(o_turned.s, it + 1)
                            nc.scalar.activation(oT[:], ps[:, 2, 0:CH], ACT.Copy).then_inc(ot_ready.s, 1)

                        heads(act, lambda: max_out(0), step, last)

            @block.tensor
            def _(pe):
                pe.sem_inc(pv_done.s, pv_done.credit)
                pe.wait_ge(w_in.s, 16 * len(loads))
                with pe.Fori(0, B) as b:
                    for I in range(NI):
                        it = b * NI + I
                        pe.wait_ge(ncs_ready.s, it + 1)
                        pe.wait_ge(x_done.s, x_done.at(it))
                        for t in range(TPC):
                            ins = nc.tensor.matmul(ps[0:TILE, t, 0:3 * C], ncs[:, t * TILE:(t + 1) * TILE], wqkv[:],
                                                   start=True, stop=True)
                        ins.then_inc(tok_done.s, 1)
                        for h in range(H):
                            pe.wait_ge(q_stacked.s, it + 1)
                            pe.wait_ge(split_done.s, it + 1)
                            pe.wait_ge(k_out.s, k_out.at(it * H + h - 1))
                            for a in range(2):
                                for t in range(TPC):
                                    ins = nc.tensor.transpose(bank16(4 + h % 2)[0:ROWS, a * CH + t * TILE:a * CH + (t + 1) * TILE],
                                                              stack[a][:, t, h, :], identb[:])
                            ins.then_inc(turned.s, 1)

                        def m_unit(h, u):
                            j, c = u // (I + 1), u % (I + 1)
                            pe.wait_ge(sm_read.s, sm_read.at(unit0(b, I, h) + u - 1))
                            w = CH if c < I else (j + 1) * TILE
                            q = QT[0:ROWS, ds(h, 1), j * TILE:(j + 1) * TILE].rearrange("p a c -> p (a c)")
                            keys = KT[0:ROWS, ds(h, 1), c * CH:c * CH + w].rearrange("p a c -> p (a c)")
                            ins = nc.tensor.matmul(ps[0:TILE, u % 2, 0:w], q, keys, start=True, stop=(c < I))
                            if c == I:
                                ins = nc.tensor.matmul(ps[0:TILE, u % 2, j * TILE:w], identb[:], tri[:], start=False, stop=True)
                            ins.then_inc(sm_done.s, 1)

                        def turn_max(h):
                            hn = it * H + h
                            pe.wait_ge(mrow_ready.s, hn + 1)
                            pe.wait_ge(o_read.s, o_read.at(hn - 1))
                            for t in range(TPC):
                                ins = nc.tensor.transpose(bank16(2)[0:KR, t * TILE:(t + 1) * TILE], mrow[:, t, :], identb[:])
                            ins.then_inc(mrow_turned.s, 1)

                        def e_scores(h, e):
                            pe.wait_ge(p_ready.s, p_ready.at(pair0(b, I, h) + e - 1))
                            diagonal = e - 2 * I
                            q0 = CH // 2 if diagonal == 1 and I > 0 else 0
                            for t in range(2):
                                kt = 2 * e + t
                                bank = 3 + 2 * (e % 2) + t
                                keys = KT[:, ds(h, 1), kt * TILE:(kt + 1) * TILE].rearrange("p a c -> p (a c)")
                                q = QT[:, ds(h, 1), q0:CH].rearrange("p a c -> p (a c)")
                                ins = nc.tensor.matmul(ps[0:TILE, bank, 0:CH - q0], keys, q, start=True, stop=(diagonal < 0))
                                if diagonal >= 0:
                                    own_tile = kt - 4 * I - q0 // TILE
                                    for j in range(own_tile if I == 0 else 0):
                                        nc.tensor.matmul(ps[0:TILE, bank, j * TILE:(j + 1) * TILE], identb[:], full[:],
                                                         start=False, stop=False)
                                    ins = nc.tensor.matmul(ps[0:TILE, bank, own_tile * TILE:(own_tile + 1) * TILE], identb[:], triT[:],
                                                           start=False, stop=True)
                            ins.then_inc(st_done.s, 1)

                        def e_values(h, e, s):
                            pe.wait_ge(p_ready.s, p_ready.at(pair0(b, I, h) + e + 1))
                            if e == 0:
                                pe.wait_ge(vh_ready.s, it * H + h + 1)
                                pe.wait_ge(oh_ready.s, oh_ready.at(it * H + h))
                            q0 = CH // 2 if e == 2 * I + 1 and I > 0 else 0
                            for t in range(2):
                                kt = 2 * e + t
                                c0 = TILE * max(kt - 4 * I, 0) if I > 0 else 0
                                col = VC * (kt % 4)
                                ins = nc.tensor.matmul(ps[col:col + VC, 7, c0:CH], Vh[:, s, kt, :], PT[:, e % 2, t, c0 - q0:CH - q0],
                                                       start=(kt < 4), stop=(kt >= 4 * I), skip_group_check=True)
                            ins.then_inc(pv_done.s, 1)

                        def fold_head(h):
                            pe.wait_ge(oh_ready.s, oh_ready.at(it * H + h + 1))
                            pe.wait_ge(o_read.s, o_read.at(it * H + h))
                            for t in range(TPC):
                                ins = nc.tensor.matmul(ps[0:TILE, 2, 256 + t * (D + 1):256 + (t + 1) * (D + 1)],
                                                       oh[:, t * TILE:(t + 1) * TILE], fold[:], start=True, stop=True)
                            ins.then_inc(folded.s, 1)

                        def first():
                            pe.wait_ge(k_out.s, k_out.at(it * H + H))
                            pe.wait_ge(v_copied.s, it + 1)
                            for u in range(4 * (I + 1)):
                                m_unit(0, u)
                            for u in range(4 * (I + 1)):
                                m_unit(1, u)
                                if u == 1:
                                    turn_max(0)

                        def step(h, hm, ht, s):
                            pe.wait_ge(qm_ready.s, it * H + h + 1)
                            pairs = 2 * (I + 1)
                            for e in range(pairs + 1):
                                if e < pairs:
                                    e_scores(h, e)
                                if hm is not None and 0 < e:
                                    m_unit(hm, 2 * e - 2)
                                    m_unit(hm, 2 * e - 1)
                                if e == 1 and ht is not None:
                                    turn_max(ht)
                                if e > 0:
                                    e_values(h, e - 1, s)
                            fold_head(h)

                        def last():
                            pe.wait_ge(o_read.s, o_read.at(it * H + H))
                            for t in range(TPC):
                                ins = nc.tensor.transpose(ps[:, 2, t * TILE:(t + 1) * TILE], o[:, t, :], k.ident[0:TILE, 0:TILE])
                            ins.then_inc(o_turned.s, 1)
                            pe.wait_ge(ot_ready.s, it + 1)
                            nc.tensor.matmul(ps[:, 0, 0:CH], wproj[:], oT[:], start=True, stop=True).then_inc(proj_done.s, 1)

                        heads(pe, first, step, last)


def experts(k):
    nc, X, N, ps = k.nc, k.X, k.normed(), k.ps
    NT = T // TILE
    with ExitStack() as ctx:
        sb = lambda n, s, dt=F32: k.sb(f"moe_{n}", s, dt, ctx)
        sem = lambda n, credit=0: k.sem(f"moe_{n}", credit)
        wr, br = sb("wr", [C, NE]), sb("br", [NE, 1])
        we, be, spread = sb("we", [C, NE, C]), sb("be", [NE, C]), sb("spread", [NE, NE, C])
        rank = sb("rank", [TILE, NE])
        lt = sb("lt", [NE, CH])
        logit, prob, left, pick = (sb(n, [TILE, NT, NE]) for n in ("logit", "prob", "left", "pick"))
        best, top1, top2 = (sb(n, [TILE, NT]) for n in ("best", "top1", "top2"))
        gst, gT = sb("gst", [TILE, TPC * NE]), sb("gT", [NE, CH])
        xg = sb("xg", [C, 2, CH])
        w_in, own = sem("w_in"), sem("own")
        logit_done, lt_ready, lt_turned, l_out = sem("logit_done"), sem("lt_ready"), sem("lt_turned"), sem("l_out")
        shifted, exped = sem("shifted"), sem("exped")
        g_staged, g_turned, gt_ready, spread_done, xg_ready, xg_used, y_done, x_done = (
            sem("g_staged"), sem("g_turned"), sem("gt_ready"), sem("spread_done"), sem("xg_ready", 2), sem("xg_used", 2),
            sem("y_done"), sem("x_done", 1))
        loads = [(wr[:], "w2_router"), (br[:], "b2_router"), (we[:], "w2_expert"), (be[:], "b2_expert"),
                 (spread[:], "spread8"), (rank[:], "rank8")]
        over = lambda t: t[:].unsqueeze(2).to_broadcast([TILE, NT, NE])
        with nc.Block() as block:
            @block.sync
            def _(sp):
                for dst, name in loads:
                    sp.dma_start(dst, k.dram[name]).then_inc(w_in.s, 16)

            @block.tensor
            def _(pe):
                pe.sem_inc(xg_used.s, xg_used.credit)
                pe.wait_ge(w_in.s, 16 * len(loads))
                with pe.Fori(0, NCH) as i:
                    nc.tensor.matmul(ps[0:NE, 0, 0:CH], wr[:], N[:, ds(i * CH, CH)], start=True, stop=True).then_inc(logit_done.s, 1)
                    pe.wait_ge(lt_ready.s, i + 1)
                    for t in range(TPC):
                        ins = nc.tensor.matmul(ps[0:TILE, 1, t * NE:(t + 1) * NE], lt[:, t * TILE:(t + 1) * TILE],
                                               k.ident[0:NE, 0:NE], start=True, stop=True)
                    ins.then_inc(lt_turned.s, 1)
                    pe.wait_ge(l_out.s, i + 1)
                with pe.Fori(0, NCH) as i:
                    pe.wait_ge(g_staged.s, i + 1)
                    for t in range(TPC):
                        ins = nc.tensor.transpose(ps[0:NE, 2, t * TILE:(t + 1) * TILE], gst[:, t * NE:(t + 1) * NE],
                                                  k.ident[0:TILE, 0:TILE])
                    ins.then_inc(g_turned.s, 1)
                    pe.wait_ge(gt_ready.s, i + 1)
                    pe.wait_ge(x_done.s, x_done.at(i))
                    nc.tensor.matmul(ps[:, 3, 0:CH], be[:], gT[:], start=True, stop=False)

                    def spread_gate(e):
                        pe.wait_ge(xg_ready.s, xg_ready.at(i * NE + e - 1))
                        nc.tensor.matmul(ps[:, 4 + e % 2, 0:CH], spread[:, e, :], gT[:], start=True, stop=True).then_inc(spread_done.s, 1)

                    spread_gate(0)
                    for e in range(NE):
                        if e + 1 < NE:
                            spread_gate(e + 1)
                        pe.wait_ge(xg_ready.s, xg_ready.at(i * NE + e + 1))
                        ins = nc.tensor.matmul(ps[:, 3, 0:CH], we[:, e, :], xg[:, e % 2, :], start=False, stop=(e == NE - 1))
                        ins.then_inc(xg_used.s, 1)

            @block.scalar
            def _(act):
                act.wait_ge(w_in.s, 16 * len(loads))
                with act.Fori(0, NCH) as i:
                    act.wait_ge(logit_done.s, i + 1)
                    nc.scalar.activation(lt[:], ps[0:NE, 0, 0:CH], ACT.Identity, bias=br[:]).then_inc(lt_ready.s, 1)
                act.wait_ge(shifted.s, 1)
                nc.scalar.activation(prob[:], prob[:], ACT.Exp).then_inc(exped.s, 1)
                with act.Fori(0, NCH) as i:
                    act.wait_ge(g_turned.s, i + 1)
                    nc.scalar.activation(gT[:], ps[0:NE, 2, 0:CH], ACT.Copy).then_inc(gt_ready.s, 1)

            @block.vector
            def _(dve):
                dve.sem_inc(xg_ready.s, xg_ready.credit)
                dve.sem_inc(x_done.s, x_done.credit)
                dve.wait_ge(w_in.s, 16 * len(loads))
                with dve.Fori(0, NCH) as i:
                    dve.wait_ge(lt_turned.s, i + 1)
                    nc.vector.tensor_copy(logit[:, ds(i * TPC, TPC), :], ps[0:TILE, 1, 0:TPC * NE].rearrange("p (t e) -> p t e", e=NE)).then_inc(l_out.s, 1)
                dve.wait_ge(l_out.s, NCH)
                link = Chain(dve, own.s).link
                v = nc.vector
                link(v.tensor_reduce(best[:], logit[:], AX.X, ALU.max))
                v.tensor_tensor(prob[:], logit[:], over(best), ALU.subtract).then_inc(shifted.s, 1)
                dve.wait_ge(exped.s, 1)
                link(v.tensor_reduce(best[:], prob[:], AX.X, ALU.add))
                link(v.reciprocal(best[:], best[:]))
                link(v.tensor_tensor(prob[:], prob[:], over(best), ALU.mult))
                ranks = rank[:].unsqueeze(1).to_broadcast([TILE, NT, NE])

                def choose(chosen, p, top):
                    link(v.tensor_reduce(top[:], p[:], AX.X, ALU.max))
                    link(v.tensor_tensor(chosen[:], p[:], over(top), ALU.is_equal))
                    link(v.tensor_tensor(chosen[:], chosen[:], ranks, ALU.mult))
                    link(v.tensor_reduce(best[:], chosen[:], AX.X, ALU.max))
                    link(v.tensor_tensor(chosen[:], chosen[:], over(best), ALU.is_equal))

                choose(pick, prob, top1)
                link(v.scalar_tensor_tensor(left[:], pick[:], -2.0, prob[:], ALU.mult, ALU.add))
                choose(logit, left, top2)
                link(v.tensor_tensor(pick[:], pick[:], logit[:], ALU.add))
                link(v.tensor_tensor(top1[:], top1[:], top2[:], ALU.add))
                link(v.reciprocal(top1[:], top1[:]))
                link(v.tensor_tensor(prob[:], prob[:], pick[:], ALU.mult))
                link(v.tensor_tensor(prob[:], prob[:], over(top1), ALU.mult))
                with dve.Fori(0, NCH) as i:
                    nc.vector.tensor_copy(gst[:].rearrange("p (t e) -> p t e", e=NE), prob[:, ds(i * TPC, TPC), :]).then_inc(g_staged.s, 1)
                    for e in range(NE):
                        dve.wait_ge(spread_done.s, i * NE + e + 1)
                        dve.wait_ge(xg_used.s, xg_used.at(i * NE + e - 1))
                        nc.vector.tensor_tensor(xg[:, e % 2, :], N[:, ds(i * CH, CH)], ps[:, 4 + e % 2, 0:CH], ALU.mult).then_inc(xg_ready.s, 1)
                    dve.wait_ge(xg_used.s, xg_used.at(i * NE + NE))
                    xs = X[:, ds(i * CH, CH)]
                    nc.vector.tensor_tensor(xs, xs, ps[:, 3, 0:CH], ALU.add).then_inc(x_done.s, 1)


def recurrence(k):
    nc, X, N, ps = k.nc, k.X, k.normed(), k.ps
    G = CH // B
    NG = L // G
    with ExitStack() as ctx:
        sb = lambda n, s, dt=F32: k.sb(f"rnn_{n}", s, dt, ctx)
        sem = lambda n, credit=0: k.sem(f"rnn_{n}", credit)
        wx, w, v = sb("wx", [C, T]), sb("w", [C, C]), sb("v", [C, C])
        gamma, beta = sb("gamma", [C, 1]), sb("beta", [C, 1])
        stats, mv, std, a, c = sb("stats", [C, NCH * 6]), sb("mv", [C, 2]), sb("std", [C, 1]), sb("a", [C, 1]), sb("c", [C, 1])
        y = sb("y", [C, 2, CH])
        w_in, own, zeroed = sem("w_in"), sem("own"), sem("zeroed")
        wx_done, wx_out, stat_done, var_ready, std_ready, wn_ready, added, stepped, y_ready, banks = (
            sem(n, cr) for n, cr in (("wx_done", 0), ("wx_out", 2), ("stat_done", 0), ("var_ready", 0), ("std_ready", 0),
                                     ("wn_ready", 0), ("added", 2), ("stepped", 0), ("y_ready", 1), ("banks", 0)))
        loads = [(w[:], "w3_in"), (v[:], "w3_v"), (gamma[:], "gamma3"), (beta[:], "beta3")]
        steps_major = N[:].rearrange("p (t b) -> p t b", b=B)
        with nc.Block() as block:
            @block.sync
            def _(sp):
                for dst, name in loads:
                    sp.dma_start(dst, k.dram[name]).then_inc(w_in.s, 16)

            @block.vector
            def _(dve):
                nc.vector.memset(y[:], 0.0).then_inc(zeroed.s, 1)
                dve.wait_ge(w_in.s, 16 * len(loads))
                with dve.Fori(0, NCH) as i:
                    dve.wait_ge(wx_out.s, wx_out.at(i + 1))
                    nc.vector.bn_stats(stats[:, ds(i * 6, 6)], wx[:, ds(i * CH, CH)]).then_inc(stat_done.s, 1)
                dve.wait_ge(stat_done.s, NCH)
                chain = Chain(dve, own.s)
                link = chain.link
                link(nc.vector.bn_aggr(mv[:], stats[:]))
                nc.vector.tensor_scalar(std[:], mv[:, 1:2], 1e-5, None, ALU.add).then_inc(var_ready.s, 1)
                dve.wait_ge(std_ready.s, 1)
                link(nc.vector.reciprocal(a[:], std[:]))
                link(nc.vector.tensor_tensor(a[:], a[:], gamma[:], ALU.mult))
                link(nc.vector.tensor_tensor(c[:], mv[:, 0:1], a[:], ALU.mult))
                link(nc.vector.tensor_tensor(c[:], beta[:], c[:], ALU.subtract))
                for b in range(B):
                    nc.vector.tensor_scalar(steps_major[:, :, b], wx[:, b * L:(b + 1) * L], a[:, 0:1], c[:, 0:1],
                                            ALU.mult, ALU.add).then_inc(wn_ready.s, 1)

            @block.gpsimd
            def _(pool):
                pool.sem_inc(added.s, added.credit)
                with pool.Fori(0, NG // 2) as i:
                    for s in range(2):
                        pool.wait_ge(y_ready.s, y_ready.at((i * 2 + s + 1) * G))
                        xs = X[:].rearrange("p (b t) -> p b t", b=B)[:, :, ds((i * 2 + s) * G, G)]
                        nc.gpsimd.tensor_tensor(xs, xs, y[:, s, :].rearrange("p (t b) -> p b t", b=B), ALU.add).then_inc(added.s, 1)

            @block.scalar
            def _(act):
                act.sem_inc(wx_out.s, wx_out.credit)
                act.sem_inc(y_ready.s, y_ready.credit)
                with act.Fori(0, NCH // 2) as i:
                    for s in range(2):
                        act.wait_ge(wx_done.s, i * 2 + s + 1)
                        nc.scalar.activation(wx[:, ds(i * (2 * CH) + s * CH, CH)], ps[:, s, 0:CH], ACT.Copy).then_inc(wx_out.s, 1)
                act.wait_ge(var_ready.s, 1)
                nc.scalar.activation(std[:], std[:], ACT.Sqrt).then_inc(std_ready.s, 1)
                with act.Fori(0, NG // 2) as i:
                    for s in range(2):
                        act.wait_ge(added.s, added.at(i * 2 + s - 1))
                        for t in range(G):
                            act.wait_ge(stepped.s, (i * 2 + s) * G + t + 1)
                            nc.scalar.activation(y[:, s, t * B:(t + 1) * B], ps[:, 2 + s, t * B:(t + 1) * B],
                                                 ACT.Sigmoid).then_inc(y_ready.s, 1)

            @block.tensor
            def _(pe):
                pe.wait_ge(w_in.s, 16 * len(loads))
                with pe.Fori(0, NCH // 2) as i:
                    for s in range(2):
                        pe.wait_ge(wx_out.s, wx_out.at(i * 2 + s - 1))
                        nc.tensor.matmul(ps[:, s, 0:CH], w[:], N[:, ds(i * (2 * CH) + s * CH, CH)], start=True, stop=True).then_inc(wx_done.s, 1)
                pe.wait_ge(wn_ready.s, B)
                nc.tensor.matmul(ps[:, 2, 0:CH], k.ident[:], N[:, 0:CH], start=True, stop=True)
                pe.wait_ge(zeroed.s, 1)

                def group(i, s, fill):
                    for t in range(G):
                        pe.wait_ge(y_ready.s, y_ready.at((i * 2 + s) * G + t))
                        prev = y[:, s, (t - 1) * B:t * B] if t else y[:, 1 - s, CH - B:CH]
                        nc.tensor.matmul(ps[:, 2 + s, t * B:(t + 1) * B], v[:], prev, start=False, stop=True,
                                         skip_group_check=True).then_inc(stepped.s, 1)
                        if t == G // 2 and fill:
                            nc.tensor.matmul(ps[:, 3 - s, 0:CH], k.ident[:], N[:, ds((i * 2 + s + 1) * CH, CH)], start=True, stop=True)

                with pe.Fori(0, NG // 2 - 1) as i:
                    group(i, 0, True)
                    group(i, 1, True)
                group(NG // 2 - 1, 0, True)
                group(NG // 2 - 1, 1, False)


def layer1(k):
    nc, X, ps = k.nc, k.X, k.ps
    WPD = HW + 2
    v = nc.vector
    with ExitStack() as ctx:
        sb = lambda n, s, dt=F32: k.sb(f"l1_{n}", s, dt, ctx)
        sem = lambda n, credit=0: k.sem(f"l1_{n}", credit)
        w_in_proj = sb("w_in_proj", [C, 2 * DI])
        w_taps, b_conv = sb("w_taps", [C, CT, 9]), sb("b_conv", [C, CT])
        w_bc, w_dt_in, w_dt = sb("w_bc", [C, ND, CT, 96]), sb("w_dt_in", [C, ND, CT, DTR]), sb("w_dt", [DTR + 1, ND, DI])
        A, D = sb("A", [C, ND, CT, NS]), sb("D", [C, ND, CT])
        ln_w, ln_b, w_out = sb("ln_w", [C, CT]), sb("ln_b", [C, CT]), sb("w_out", [C, CT, C])
        mean256, eps = sb("mean256", [C, C]), sb("eps", [C, 1])
        spread = sb("spread", [96, 2 * NS, C], BF16)
        d_mat = sb("d_mat", [C, ND, CT, C])
        xn, u, Y = sb("xn", [C, L]), sb("u", [C, CT, L]), sb("Y", [C, CT, L])
        xpad = sb("xpad", [C, WPD, WPD])
        bc, rest = sb("bc", [96, 2, CS], BF16), sb("rest", [96, CS])
        dtr, relu, e, w = sb("dtr", [DTR + 1, CS]), sb("relu", [C, CT, CS]), sb("e", [C, CT, CS]), sb("w", [C, CT, CS])
        dt, dtu = sb("dt", [C, 2, CT, CS]), sb("dtu", [C, 2, CT, CS])
        dA, dBu, h, hC = (sb(n, [C, 2, CT, CS]) for n in ("dA", "dBu", "h", "hC"))
        Cs, mid, state = sb("Cs", [C, 2, CS]), sb("mid", [96, CS], BF16), sb("state", [C, 2, CT, NS])
        one, minus_one = sb("one", [C, 1]), sb("minus_one", [C, 1])
        flat = lambda t, n, w: t[:].rearrange("p a b c -> p (a b c)")[:, 0:n * w].rearrange("p (a c) -> p a c", a=n)
        yc, sq, std, sz = flat(dA, CT, CH), flat(dBu, CT, CH), flat(h, 1, CH), flat(hC, CT, CH)

        const_ready = sem("const_ready")
        w_loaded, conv_own, end_own, a_negated, d_ready = (
            sem(n) for n in ("w_loaded", "conv_own", "end_own", "a_negated", "d_ready"))
        xn_ready, xc_done, xc_out, conv_done, sg_ready, u_ready = (
            sem("xn_ready"), sem("xc_done"), sem("xc_out", 1), sem("conv_done", 1), sem("sg_ready"), sem("u_ready"))
        proj_done, dtr_ready, abs_ready, less_one, hi_ready, rest_ready, mid_ready, split_done, delta_done = (
            sem(n) for n in ("proj_done", "dtr_ready", "abs_ready", "less_one", "hi_ready", "rest_ready", "mid_ready", "split_done", "delta_done"))
        delta_out, e_ready, w_ready, ln_ready, pool_own, dt_ready, dtu_ready = (
            sem(n, int(n == "delta_out")) for n in ("delta_out", "e_ready", "w_ready", "ln_ready", "pool_own", "dt_ready", "dtu_ready"))
        bc_done, dbu_ready, a_ready, c_copied, scan_done, hc_ready, y_done, y_out, state_zeroed = (
            sem("bc_done"), sem("dbu_ready", 2 * CT), sem("a_ready"), sem("c_copied", 2), sem("scan_done", 2 * CT),
            sem("hc_ready", 2), sem("y_done", 2), sem("y_out", 1), sem("state_zeroed"))
        m_done, yc_ready, sq_ready, var_done, std_ready, z_done, sz_ready, g_ready, out_done, x_done = (
            sem("m_done"), sem("yc_ready"), sem("sq_ready"), sem("var_done"), sem("std_ready"), sem("z_done"),
            sem("sz_ready"), sem("g_ready"), sem("out_done"), sem("x_done", 1))
        loads = [(w_in_proj[:], "w1_in"), (w_taps[:], "w1_taps"), (b_conv[:], "b1_conv"), (w_bc[:], "w1_bc"),
                 (w_dt_in[:], "w1_dt_in"), (w_dt[:], "w1_dt"), (A[:], "A_logs"), (D[:], "D1"),
                 (ln_w[:], "ln1_w"), (ln_b[:], "ln1_b"), (w_out[:], "w1_out"), (mean256[:], "mean256"),
                 (spread[:].bitcast(mybir.dt.uint16), "spread_bc")]

        def forward(kk, o, more=0):
            return o + more if kk < 2 else o * -1 + (NCS // 2 - 1 - more)

        def chunks(eng, b, body):
            for kk in range(ND):
                place = lambda o: forward(kk, o)
                start = (b * ND + kk) * NCS
                first = (kk, place(0), start, 0)
                last = (kk, place(NCS // 2 - 1), start + (NCS - 1), 1)
                before = (kk - 1, forward(kk - 1, NCS // 2 - 1), start - 1, 1) if kk > 0 else None
                after = (kk + 1, forward(kk + 1, 0), start + NCS, 0) if kk + 1 < ND else None
                body(first, before, (kk, place(0), start + 1, 1))
                with eng.Fori(0, NCS // 2 - 1) as o:
                    here, there, q = place(o), forward(kk, o, 1), start + o * 2
                    body((kk, here, q + 1, 1), (kk, here, q, 0), (kk, there, q + 2, 0))
                    body((kk, there, q + 2, 0), (kk, here, q + 1, 1), (kk, there, q + 3, 1))
                body(last, (kk, place(NCS // 2 - 1), start + (NCS - 2), 0), after)

        def u_view(ct, kk, o, p):
            p = p if kk < 2 else 1 - p
            win = u[:, ct, :].rearrange("p (hg wh wg ww) -> p hg wh wg ww", hg=4, wh=WS, wg=4)
            if kk % 2 == 0:
                return win[:, ds(o, 1), :, 2 * p:2 * p + 2, :].rearrange("p a wh wg ww -> p (a wg) wh ww")
            return win[:, 2 * p:2 * p + 2, :, ds(o, 1), :].rearrange("p hg wh a ww -> p (a hg) ww wh")

        def y_view(ct, kk, o, p):
            p = p if kk < 2 else 1 - p
            pos = "p (i j) -> p i j" if kk % 2 == 0 else "p (i j) -> p j i"
            return Y[:, ct, :].rearrange(pos, i=HW)[:, ds((o * 2 + p) * RC, RC), :]

        windows = lambda t: t.rearrange("p (g a b) -> p g a b", g=2, a=WS)
        lines = lambda t: t.rearrange("p (r c) -> p r c", c=HW)
        order = lambda t, kk: t if kk < 2 else t[:, ::-1]

        with nc.Block() as block:
            @block.sync
            def _(sp):
                for dst, name in loads:
                    sp.dma_start(dst, k.dram[name]).then_inc(w_loaded.s, 16)

            @block.tensor
            def _(pe):
                for q in (y_done,):
                    pe.sem_inc(q.s, q.credit)
                pe.wait_ge(w_loaded.s, 16 * len(loads))
                with pe.Fori(0, B) as b:
                    for ct in range(CT):
                        with pe.Fori(0, CPB) as i:
                            pe.wait_ge(xn_ready.s, b + 1)
                            pe.wait_ge(xc_out.s, xc_out.at((b * CT + ct) * CPB + i))
                            nc.tensor.matmul(ps[:, 0, 0:CH], w_in_proj[:, ct * C:(ct + 1) * C], xn[:, ds(i * CH, CH)],
                                             start=True, stop=True).then_inc(xc_done.s, 1)

                    def project(chunk, n):
                        kk, f, q, p = chunk
                        if n == 0:
                            pe.wait_ge(u_ready.s, (b + 1) * CT)
                            pe.wait_ge(delta_out.s, delta_out.at(q))
                            for ct in range(CT):
                                nc.tensor.matmul(ps[0:96, 6, 0:CS], w_bc[:, kk, ct, :], u_view(ct, kk, f, p),
                                                 start=(ct == 0), stop=(ct == CT - 1))
                        if n == 1:
                            for ct in range(CT):
                                ins = nc.tensor.matmul(ps[0:DTR, 7, 0:CS], w_dt_in[:, kk, ct, :], u_view(ct, kk, f, p),
                                                       start=(ct == 0), stop=(ct == CT - 1))
                            ins.then_inc(proj_done.s, 1)
                        if n == 4:
                            pe.wait_ge(rest_ready.s, q + 1)
                            pe.wait_ge(dtr_ready.s, q + 1)
                            for ct in range(CT):
                                ins = nc.tensor.matmul(ps[:, 6 + ct, 0:CS], w_dt[:, kk, ct * C:(ct + 1) * C], dtr[:],
                                                       start=True, stop=True)
                            ins.then_inc(delta_done.s, 1)

                    AHEAD = 3

                    def spread_bc(chunk, n):
                        kk, f, q, p = chunk
                        m = q * NS + n
                        pe.wait_ge(split_done.s, q + 1)
                        pe.wait_ge(dbu_ready.s, dbu_ready.at((m - 1) * CT))
                        pe.wait_ge(c_copied.s, c_copied.at(m - 1))
                        nc.tensor.matmul(ps[:, n % 2, 0:CS], spread[:, n, :], bc[:, p, :], start=True, stop=True)
                        nc.tensor.matmul(ps[:, 2 + n % 2, 0:CS], spread[:, NS + n, :], bc[:, p, :],
                                         start=True, stop=True).then_inc(bc_done.s, 1)

                    def scan_chunk(chunk, before, after):
                        kk, f, q, p = chunk
                        if kk == 0 and before is None:
                            for n in range(NS):
                                project(chunk, n)
                            for n in range(AHEAD):
                                spread_bc(chunk, n)
                        for n in range(NS):
                            if n + AHEAD < NS:
                                spread_bc(chunk, n + AHEAD)
                            elif after is not None:
                                spread_bc(after, n + AHEAD - NS)
                            if after is not None:
                                project(after, n)
                            if n == 0:
                                pe.wait_ge(y_out.s, y_out.at(q))
                            if n >= NS - CT - 2 and n < NS - 2:
                                ct = n - (NS - CT - 2)
                                pe.wait_ge(d_ready.s, 1)
                                nc.tensor.matmul(ps[:, 4 + ct, 0:CS], d_mat[:, kk, ct, :], u_view(ct, kk, f, p),
                                                 start=False, stop=False)
                            pe.wait_ge(hc_ready.s, hc_ready.at(q * NS + n + 1))
                            for ct in range(CT):
                                ins = nc.tensor.matmul(ps[:, 4 + ct, 0:CS], k.ident[:], hC[:, n % 2, ct, :],
                                                       start=(n == 0), stop=(n == NS - 1))
                            ins.then_inc(y_done.s, 1)

                    chunks(pe, b, scan_chunk)
                    with pe.Fori(0, CPB) as i:
                        it = b * CPB + i
                        pe.wait_ge(y_out.s, y_out.at((b + 1) * (ND * NCS)))
                        pe.wait_ge(x_done.s, x_done.at(it))
                        for ct in range(CT):
                            ins = nc.tensor.matmul(ps[:, 0, 0:CH], mean256[:], Y[:, ct, ds(i * CH, CH)],
                                                   start=(ct == 0), stop=(ct == CT - 1))
                        ins.then_inc(m_done.s, 1)
                        for ct in range(CT):
                            ins = nc.tensor.matmul(ps[:, 2 + ct, 0:CH], w_in_proj[:, DI + ct * C:DI + (ct + 1) * C],
                                                   xn[:, ds(i * CH, CH)], start=True, stop=True)
                        ins.then_inc(z_done.s, 1)
                        pe.wait_ge(sq_ready.s, it + 1)
                        for ct in range(CT):
                            ins = nc.tensor.matmul(ps[:, 1, 0:CH], mean256[:], sq[:, ct, :], start=(ct == 0), stop=(ct == CT - 1))
                        ins.then_inc(var_done.s, 1)
                        pe.wait_ge(g_ready.s, it + 1)
                        for ct in range(CT):
                            ins = nc.tensor.matmul(ps[:, 4, 0:CH], w_out[:, ct, :], sz[:, ct, :], start=(ct == 0), stop=(ct == CT - 1))
                        ins.then_inc(out_done.s, 1)

            @block.scalar
            def _(act):
                for q in (xc_out, c_copied, delta_out):
                    act.sem_inc(q.s, q.credit)
                act.wait_ge(w_loaded.s, 16 * len(loads))
                nc.scalar.activation(A[:], A[:], ACT.Exp).then_inc(a_negated.s, 1)
                with act.Fori(0, B) as b:
                    for ct in range(CT):
                        with act.Fori(0, CPB) as i:
                            act.wait_ge(xc_done.s, (b * CT + ct) * CPB + i + 1)
                            act.wait_ge(conv_done.s, conv_done.at(b * CT + ct))
                            nc.scalar.activation(xpad[:, ds(i * 8 + 1, 8), 1:1 + HW], ps[:, 0, 0:CH].rearrange("p (r w) -> p r w", w=HW),
                                                 ACT.Copy).then_inc(xc_out.s, 1)
                        act.wait_ge(conv_done.s, conv_done.at(b * CT + ct + 1))
                        nc.scalar.activation(Y[:, ct, :], u[:, ct, :], ACT.Sigmoid, bias=b_conv[:, ct:ct + 1]).then_inc(sg_ready.s, 1)

                    def set_up(chunk, n):
                        kk, f, q, p = chunk
                        if n == 2:
                            act.wait_ge(proj_done.s, q + 1)
                            nc.scalar.activation(bc[:, p, :], ps[0:96, 6, 0:CS], ACT.Copy).then_inc(hi_ready.s, 1)
                        if n == 3:
                            nc.scalar.activation(dtr[0:DTR, :], ps[0:DTR, 7, 0:CS], ACT.Copy).then_inc(dtr_ready.s, 1)
                        if n == 4:
                            act.wait_ge(rest_ready.s, q + 1)
                            nc.scalar.activation(mid[:], rest[:], ACT.Copy)
                            nc.scalar.activation(bc[32:64, p, :], rest[32:64, :], ACT.Copy).then_inc(mid_ready.s, 1)
                        if n == 6:
                            act.wait_ge(delta_done.s, q + 1)
                            nc.scalar.activation(e[:], ps[:, 6:6 + CT, 0:CS], ACT.Abs).then_inc(abs_ready.s, 1)
                        if n == 7:
                            act.wait_ge(abs_ready.s, q + 1)
                            nc.scalar.activation(e[:], e[:], ACT.Exp, scale=-1.0).then_inc(e_ready.s, 1)
                        if n == 8:
                            act.wait_ge(e_ready.s, q + 1)
                            nc.scalar.activation(w[:], e[:], ACT.Identity, bias=one[:]).then_inc(w_ready.s, 1)
                        if n == 9:
                            act.wait_ge(w_ready.s, q + 1)
                            nc.scalar.activation(dtu[:, p], w[:], ACT.Identity, bias=minus_one[:]).then_inc(less_one.s, 1)
                        if n == 10:
                            nc.scalar.activation(relu[:], ps[:, 6:6 + CT, 0:CS], ACT.Relu).then_inc(delta_out.s, 1)
                        if n == 11:
                            nc.scalar.activation(dt[:, p], w[:], ACT.Ln).then_inc(ln_ready.s, 1)

                    def scan_chunk(chunk, before, after):
                        kk, f, q, p = chunk
                        if kk == 0 and before is None:
                            act.wait_ge(const_ready.s, 1)
                            for n in range(NS):
                                set_up(chunk, n)
                        for n in range(NS):
                            m = q * NS + n
                            act.wait_ge(a_negated.s, 2)
                            act.wait_ge(dt_ready.s, q + 1)
                            act.wait_ge(scan_done.s, scan_done.at((m - 1) * CT))
                            for ct in range(CT):
                                ins = nc.scalar.activation(dA[:, n % 2, ct, :], dt[:, p, ct, :], ACT.Exp,
                                                           scale=A[:, kk, ct, n:n + 1])
                            ins.then_inc(a_ready.s, 1)
                            act.wait_ge(bc_done.s, m + 1)
                            act.wait_ge(hc_ready.s, hc_ready.at(m - 1))
                            nc.scalar.activation(Cs[:, n % 2, :], ps[:, 2 + n % 2, 0:CS], ACT.Copy).then_inc(c_copied.s, 1)
                            if after is not None:
                                set_up(after, n)

                    chunks(act, b, scan_chunk)
                    with act.Fori(0, CPB) as i:
                        it = b * CPB + i
                        act.wait_ge(z_done.s, it + 1)
                        act.wait_ge(x_done.s, x_done.at(it))
                        nc.scalar.activation(sz, ps[:, 2:4, 0:CH], ACT.Sigmoid).then_inc(sz_ready.s, 1)
                        act.wait_ge(yc_ready.s, it + 1)
                        nc.scalar.activation(sq, yc, ACT.Square).then_inc(sq_ready.s, 1)
                        act.wait_ge(var_done.s, it + 1)
                        nc.scalar.activation(std[:, 0, :], ps[:, 1, 0:CH], ACT.Sqrt, bias=eps[:]).then_inc(std_ready.s, 1)

            @block.gpsimd
            def _(pool):
                pool.sem_inc(hc_ready.s, hc_ready.credit)
                with pool.Fori(0, B) as b:

                    def set_up(chunk, n):
                        kk, f, q, p = chunk
                        if n == 9:
                            pool.wait_ge(less_one.s, q + 1)
                            nc.gpsimd.tensor_tensor(e[:], dtu[:, p], e[:], ALU.subtract).then_inc(pool_own.s, 1)
                        if n == 10:
                            pool.wait_ge(delta_out.s, delta_out.at(q + 1))
                            pool.wait_ge(pool_own.s, q * 2 + 1)
                            nc.gpsimd.tensor_tensor(e[:], relu[:], e[:], ALU.subtract).then_inc(pool_own.s, 1)
                        if n == 12:
                            pool.wait_ge(ln_ready.s, q + 1)
                            pool.wait_ge(pool_own.s, q * 2 + 2)
                            nc.gpsimd.tensor_tensor(dt[:, p], dt[:, p], e[:], ALU.add).then_inc(dt_ready.s, 1)

                    def scan_chunk(chunk, before, after):
                        kk, f, q, p = chunk
                        if kk == 0 and before is None:
                            for n in range(NS):
                                set_up(chunk, n)
                        last = CS - 1 if kk < 2 else 0
                        for n in range(NS):
                            m = q * NS + n
                            pool.wait_ge(scan_done.s, scan_done.at((m + 1) * CT))
                            pool.wait_ge(c_copied.s, c_copied.at(m + 1))
                            pool.wait_ge(y_done.s, y_done.at(m - 1))
                            nc.gpsimd.tensor_tensor(hC[:, n % 2], h[:, n % 2], Cs[:, n % 2, :].unsqueeze(1).to_broadcast([C, CT, CS]),
                                                    ALU.mult)
                            nc.gpsimd.tensor_copy(state[:, kk % 2, :, n:n + 1], h[:, n % 2, :, last:last + 1]).then_inc(hc_ready.s, 1)
                            if after is not None:
                                set_up(after, n)

                    chunks(pool, b, scan_chunk)

            @block.vector
            def _(dve):
                for q in (conv_done, dbu_ready, scan_done, y_out, x_done):
                    dve.sem_inc(q.s, q.credit)
                v.memset(xpad[:], 0.0)
                v.memset(eps[:], 1e-5)
                v.memset(one[:], 1.0)
                v.memset(dtr[:], 1.0)
                v.memset(minus_one[:], -1.0).then_inc(const_ready.s, 1)
                dve.wait_ge(a_negated.s, 1)
                v.tensor_scalar(A[:], A[:], -1.0, None, ALU.mult).then_inc(a_negated.s, 1)
                for kk in range(ND):
                    for ct in range(CT):
                        ins = v.tensor_scalar(d_mat[:, kk, ct, :], k.ident[:], D[:, kk, ct:ct + 1], None, ALU.mult)
                ins.then_inc(d_ready.s, 1)
                PER_B = 1 + CT * 10
                with dve.Fori(0, B) as b:
                    chain = Chain(dve, conv_own.s, b * PER_B)
                    chain.link(v.tensor_scalar(xn[:], X[:, ds(b * L, L)], k.gn_nmean[:, ds(b, 1)], k.gn_rstd[:, ds(b, 1)],
                                               ALU.add, ALU.mult))
                    dve.sem_inc(xn_ready.s, 1)
                    for ct in range(CT):
                        dve.wait_ge(xc_out.s, xc_out.at((b * CT + ct + 1) * CPB))
                        image = u[:, ct, :].rearrange("p (r c) -> p r c", c=HW)
                        for tap in range(9):
                            src = xpad[:, tap // 3:tap // 3 + HW, tap % 3:tap % 3 + HW]
                            if tap == 0:
                                ins = v.tensor_scalar(image, src, w_taps[:, ct, 0:1], None, ALU.mult)
                            else:
                                ins = v.scalar_tensor_tensor(image, src, w_taps[:, ct, tap:tap + 1], image, ALU.mult, ALU.add)
                            chain.link(ins)
                        dve.sem_inc(conv_done.s, 1)
                        dve.wait_ge(sg_ready.s, b * CT + ct + 1)
                        chain.link(v.scalar_tensor_tensor(u[:, ct, :], u[:, ct, :], b_conv[:, ct:ct + 1], Y[:, ct, :],
                                                          ALU.add, ALU.mult))
                        dve.sem_inc(u_ready.s, 1)
                    assert chain.n == PER_B

                    def zero_states(kk, done):
                        dve.wait_ge(hc_ready.s, hc_ready.at(done))
                        v.memset(state[:, kk % 2], 0.0).then_inc(state_zeroed.s, 1)

                    def set_up(chunk, n):
                        kk, f, q, p = chunk
                        if n == 3:
                            dve.wait_ge(hi_ready.s, q + 1)
                            v.tensor_tensor(rest[:], ps[0:96, 6, 0:CS], bc[:, p, :], ALU.subtract).then_inc(rest_ready.s, 1)
                        if n == 6:
                            dve.wait_ge(mid_ready.s, q + 1)
                            v.tensor_tensor(bc[64:96, p, :], rest[64:96, :], mid[64:96, :], ALU.subtract).then_inc(split_done.s, 1)
                        if n == NS - 2:
                            dve.wait_ge(dt_ready.s, q + 1)
                            for ct in range(CT):
                                ins = v.tensor_tensor(windows(dtu[:, p, ct, :]), windows(dt[:, p, ct, :]), u_view(ct, kk, f, p), ALU.mult)
                            ins.then_inc(dtu_ready.s, 1)

                    def add_output(chunk):
                        kk, f, q, p = chunk
                        dve.wait_ge(y_done.s, y_done.at((q + 1) * NS))
                        dve.wait_ge(y_out.s, y_out.at(q))
                        for ct in range(CT):
                            dst, src = y_view(ct, kk, f, p), lines(ps[:, 4 + ct, 0:CS])
                            if kk == 0:
                                ins = v.tensor_copy(dst, src)
                            else:
                                ins = v.tensor_tensor(dst, dst, src, ALU.add)
                        ins.then_inc(y_out.s, 1)

                    def weigh_b(chunk, n, ct):
                        kk, f, q, p = chunk
                        m = q * NS + n
                        dve.wait_ge(dtu_ready.s, q + 1)
                        dve.wait_ge(bc_done.s, m + 1)
                        dve.wait_ge(scan_done.s, scan_done.at((m - 2) * CT + ct + 1))
                        v.tensor_tensor(dBu[:, n % 2, ct, :], dtu[:, p, ct, :], ps[:, n % 2, 0:CS], ALU.mult).then_inc(dbu_ready.s, 1)

                    def scan_chunk(chunk, before, after):
                        kk, f, q, p = chunk
                        if kk == 0 and before is None:
                            zero_states(0, q * NS)
                            for n in range(NS):
                                set_up(chunk, n)
                            for ct in range(CT):
                                weigh_b(chunk, 0, ct)
                        for n in range(NS):
                            m, s = q * NS + n, n % 2
                            for ct in range(CT):
                                dve.wait_ge(dbu_ready.s, dbu_ready.at(m * CT + ct + 1))
                                dve.wait_ge(a_ready.s, m + 1)
                                dve.wait_ge(hc_ready.s, hc_ready.at(m - 1))
                                dve.wait_ge(state_zeroed.s, b * ND + kk + 1)
                                v.tensor_tensor_scan(order(h[:, s, ct, :], kk), order(dA[:, s, ct, :], kk),
                                                     order(dBu[:, s, ct, :], kk), state[:, kk % 2, ct, n:n + 1],
                                                     ALU.mult, ALU.add).then_inc(scan_done.s, 1)
                                if n + 1 < NS:
                                    weigh_b(chunk, n + 1, ct)
                                elif after is not None:
                                    weigh_b(after, 0, ct)
                            if n == 1 and before is not None:
                                add_output(before)
                            if after is not None:
                                set_up(after, n)
                                if n == 8 and after[0] != kk:
                                    zero_states(kk + 1, q * NS)
                        if after is None:
                            add_output(chunk)

                    chunks(dve, b, scan_chunk)
                    PER_I = 5
                    with dve.Fori(0, CPB) as i:
                        it = b * CPB + i
                        chain = Chain(dve, end_own.s, it * PER_I)
                        over = lambda t: t.unsqueeze(1).to_broadcast([C, CT, CH])
                        dve.wait_ge(m_done.s, it + 1)
                        v.tensor_tensor(yc, Y[:, :, ds(i * CH, CH)], over(ps[:, 0, 0:CH]), ALU.subtract).then_inc(yc_ready.s, 1)
                        dve.wait_ge(std_ready.s, it + 1)
                        chain.link(v.reciprocal(std[:, 0, :], std[:, 0, :]))
                        chain.link(v.tensor_tensor(yc, yc, over(std[:, 0, :]), ALU.mult))
                        for ct in range(CT):
                            chain.link(v.tensor_scalar(yc[:, ct, :], yc[:, ct, :], ln_w[:, ct:ct + 1], ln_b[:, ct:ct + 1], ALU.mult, ALU.add))
                        dve.wait_ge(sz_ready.s, it + 1)
                        chain.link(v.tensor_tensor(sz, sz, ps[:, 2:4, 0:CH], ALU.mult))
                        v.tensor_tensor(sz, sz, yc, ALU.mult).then_inc(g_ready.s, 1)
                        assert chain.n == PER_I
                        dve.wait_ge(out_done.s, it + 1)
                        xs = X[:, ds(b * L + i * CH, CH)]
                        v.tensor_tensor(xs, xs, ps[:, 4, 0:CH], ALU.add).then_inc(x_done.s, 1)


PHASES = {"load": load_x, "store": store_x, "gn0": lambda k: gn_stats(k, "gn0"), "l0": layer0,
          "ln2a": lambda k: layer_norm(k, "ln2a", 1e-5), "a2": lambda k: attention(k, "a2", 1, "w2_qkv", None),
          "gn1": lambda k: gn_stats(k, "gn1"), "l1": layer1,
          "ln2f": lambda k: layer_norm(k, "ln2f", 1e-5), "moe": experts,
          "ln3f": lambda k: layer_norm(k, "ln3f", 1e-5), "rnn": recurrence,
          "ln3a": lambda k: layer_norm(k, "ln3a", 1e-5), "a3": lambda k: attention_heads(k, "a3")}
ORDER = ["load", "gn0", "l0", "gn1", "l1", "ln2a", "a2", "ln2f", "moe", "ln3a", "a3", "ln3f", "rnn", "store"]


def build(nc, dram):
    with ExitStack() as ctx:
        k = Core(nc, ctx, dram)
        for name in ORDER:
            PHASES[name](k)
            k.end_phase()


def arrange(inputs):
    import numpy as np
    f = {n: np.ascontiguousarray(v) for n, v in inputs.items()}
    t = np.ascontiguousarray
    a = {"x": f["x"].reshape(T, C)}
    a["ident"] = np.eye(C, dtype=np.float32)
    a["mean_mat"] = np.full((C, C), 1.0 / C, np.float32)
    a["group_mat"] = np.kron(np.eye(C // 4), np.full((4, 4), 0.25)).astype(np.float32)
    a["w0_qkv"], a["b0_qkv"] = t(f["L0_conv_qkv_w"].T), t(f["L0_conv_qkv_b"].reshape(3, C).T)
    a["w0_proj"], a["b0_proj"] = t(f["L0_conv_proj_w"].T), f["L0_conv_proj_b"].reshape(C, 1)
    a["head_scale0"] = np.kron(np.eye(NH0), np.full((HD0, 1), HD0 ** -0.5)).astype(np.float32)
    ki = np.arange(8)[None, None, :, None] - np.arange(2)[:, None, None, None]
    kj = np.arange(WP)[None, None, None, :] - np.arange(HW)[None, :, None, None]
    ki, kj = (np.broadcast_to(v, (2, HW, 8, WP)).reshape(TILE, WIN) for v in (ki, kj))
    inside = (ki >= 0) & (ki < KS) & (kj >= 0) & (kj < KS)
    a["wmask"] = np.where(inside, 0.0, NEG).astype(np.float32)
    laid = f["L0_conv_rpb"][:, np.clip(ki, 0, KS - 1) + PAD, np.clip(kj, 0, KS - 1) + PAD]
    a["rpb_laid"] = t(laid.transpose(1, 0, 2))
    a["w1_in"] = t(f["L1_conv_W_in"].T)
    a["w1_taps"] = t(f["L1_conv_conv_w"].reshape(CT, C, 9).transpose(1, 0, 2))
    a["b1_conv"] = t(f["L1_conv_conv_b"].reshape(CT, C).T)
    xp = f["L1_conv_x_proj_w"].reshape(ND, DTR + 2 * NS, CT, C).transpose(3, 0, 2, 1)
    a["w1_dt_in"] = t(xp[..., :DTR])
    a["w1_bc"] = t(np.concatenate([xp[..., DTR:]] * 3, axis=-1))
    a["w1_dt"] = t(np.concatenate([f["L1_conv_dt_proj_w"].transpose(2, 0, 1), f["L1_conv_dt_proj_b"].reshape(1, ND, DI)]))
    a["A_logs"] = t(f["L1_conv_A_logs"].reshape(ND, CT, C, NS).transpose(2, 0, 1, 3))
    a["D1"] = t(f["L1_conv_Ds"].reshape(ND, CT, C).transpose(2, 0, 1))
    a["ln1_w"], a["ln1_b"] = t(f["L1_conv_ln_w"].reshape(CT, C).T), t(f["L1_conv_ln_b"].reshape(CT, C).T)
    a["w1_out"] = t(f["L1_conv_W_out"].reshape(C, CT, C).transpose(2, 1, 0))
    a["mean256"] = np.full((C, C), 1.0 / DI, np.float32)
    one = np.tile(np.eye(2 * NS, dtype=np.float32), (3, 1))
    a["spread_bc"] = np.repeat(one[:, :, None], C, axis=2).astype(np.uint16) * np.uint16(0x3F80)
    key = np.arange(CH)[None, None, :]
    query = np.arange(TILE)[:, None, None] + TILE * np.arange(TPC)[None, :, None]
    a["causal_masks"] = np.where(key <= query, 0.0, NEG).astype(np.float32)
    a["w2_qkv"] = np.concatenate([f["L2_attn_Wq"], f["L2_attn_Wk"], f["L2_attn_Wv"]], axis=1)
    a["head_scale_a2"] = np.full((C, 1), L ** -0.5, np.float32)
    a["w3_qkv"], a["w3_proj"] = f["L3_attn_w_attn"], f["L3_attn_w_proj"]
    a["head_scale_a3"] = np.kron(np.eye(NH3), np.full((HD3, 1), HD3 ** -0.5)).astype(np.float32)
    BNEG, ONE = np.uint16(0xF149), np.uint16(0x3F80)
    a["identb"] = np.eye(TILE, dtype=np.uint16) * ONE
    later = np.triu(np.ones((TILE, TILE), np.uint16), 1)
    a["tri"], a["triT"] = later * BNEG, t(later.T * BNEG)
    a["full"] = np.full((TILE, TILE), BNEG, np.uint16)
    a["fold"] = np.tile(np.eye(32, HD3 + 1, dtype=np.float32), (4, 1))
    a["w2_router"], a["b2_router"] = f["L2_ffn_router_w"], f["L2_ffn_router_b"].reshape(NE, 1)
    a["w2_expert"], a["b2_expert"] = t(f["L2_ffn_expert_w"].transpose(1, 0, 2)), f["L2_ffn_expert_b"]
    a["spread8"] = np.repeat(np.eye(NE, dtype=np.float32)[:, :, None], C, axis=2)
    a["rank8"] = np.broadcast_to(np.arange(NE, 0, -1).astype(np.float32), (TILE, NE)).copy()
    a["w3_in"], a["w3_v"] = t(f["L3_ffn_W"].T), t(f["L3_ffn_V"].T)
    a["gamma3"], a["beta3"] = f["L3_ffn_gamma"].reshape(C, 1), f["L3_ffn_beta"].reshape(C, 1)
    return a


def kernel(**inputs):
    import concourse.bacc as _bacc
    from concourse import mybir as _mybir
    from concourse.bass_utils import run_bass_kernel_spmd as _run

    nc = _bacc.Bacc("TRN2", target_bir_lowering=False, num_devices=1)
    arrays, dram = {}, {}
    for name, a in arrange(inputs).items():
        arrays[f"in_{name}_dram"] = a
        dram[name] = nc.dram_tensor(f"in_{name}_dram", a.shape, _mybir.dt.from_np(a.dtype), kind="ExternalInput").ap()
    dram["out"] = nc.dram_tensor("out_0_dram", (T, C), _mybir.dt.float32, kind="ExternalOutput").ap()
    build(nc, dram)
    r = _run(nc, [arrays], core_ids=[0])
    return r.results[0]["out_0_dram"].reshape(B, HW, HW, C)
```

```python
from contextlib import ExitStack

import concourse.bass as bass
from concourse import mybir

ALU = mybir.AluOpType
ACT = mybir.ActivationFunctionType
AX = mybir.AxisListType
F32 = mybir.dt.float32
BF16 = mybir.dt.bfloat16

C = 128
B = 4
HW = 56
L = HW * HW
T = B * L
TILE = 2 * HW
TPC = 4
CH = TPC * TILE
NCH = T // CH
CPB = L // CH
TPB = L // TILE

NH0, HD0, KS = 4, 32, 7
PAD = KS // 2
WP = HW + 2 * PAD
LP = WP * WP
PAIR = 2 * WP
NPAIR = WP // 2
WIN = 8 * WP
NWIN = WIN // PAIR
NEG = -1.0e30

DI, NS, DTR, ND = 256, 16, 8, 4
CT = DI // C
WS = HW // 4
CS = 2 * WS * WS
NCS = L // CS
RC = CS // HW

NE = 8
NH3, HD3 = 8, 16


def ds(start, size):
    return bass.ds(start, size)


class Chain:

    def __init__(self, eng, sem, base=0):
        self.eng, self.sem, self.base, self.n = eng, sem, base, 0

    def link(self, ins):
        self.n += 1
        ins.then_inc(self.sem, 1)
        self.eng.wait_ge(self.sem, self.base + self.n)


class Sem:

    def __init__(self, s, credit):
        self.s, self.credit = s, credit

    def at(self, n):
        return n + self.credit


class Core:

    def __init__(self, nc, ctx, dram):
        self.nc, self.ctx, self.dram = nc, ctx, dram
        self.handles = []
        self.X, self.N = self.sb("X", [C, T]), None
        self.ident = self.sb("ident", [C, C])
        self.mean_mat = self.sb("mean_mat", [C, C])
        self.gn_nmean, self.gn_rstd = self.sb("gn_nmean", [C, B]), self.sb("gn_rstd", [C, B])
        self.ps = ctx.enter_context(nc.psum_tensor("ps", [128, 8, 512], F32))

    def normed(self):
        if self.N is None:
            self.N = self.sb("N", [C, T])
        return self.N

    def sb(self, name, shape, dt=F32, ctx=None):
        return (ctx or self.ctx).enter_context(self.nc.sbuf_tensor(name, shape, dt))

    def sem(self, name, credit=0):
        handle = self.nc.alloc_semaphore(name=name)
        self.handles.append(handle)
        return Sem(handle, credit)

    def end_phase(self):
        self.nc.clear_and_free_semaphores(self.handles)
        self.nc.all_engine_barrier()
        self.handles = []

    def weights(self, block_sync, pairs, sem):
        for dst, src in pairs:
            block_sync.dma_start(dst, src).then_inc(sem, 16)
        return 16 * len(pairs)


def load_x(k):
    nc, X, ps = k.nc, k.X, k.ps
    src = k.dram["x"].rearrange("(t p) c -> p t c", p=TILE)
    with ExitStack() as ctx:
        xin = k.sb("ld_xin", [TILE, 2, TPC, C], ctx=ctx)
        consts_in, landed = k.sem("ld_consts").s, [k.sem("ld_landed0").s, k.sem("ld_landed1").s]
        turned, copied = [k.sem("ld_turned0").s, k.sem("ld_turned1").s], [k.sem("ld_copied0").s, k.sem("ld_copied1").s]
        with nc.Block() as block:
            @block.sync
            def _(sp):
                sp.dma_start(k.ident[:], k.dram["ident"]).then_inc(consts_in, 16)
                sp.dma_start(k.mean_mat[:], k.dram["mean_mat"]).then_inc(consts_in, 16)
                for s in range(2):
                    sp.dma_start(xin[:, s], src[:, s * TPC:(s + 1) * TPC, :]).then_inc(landed[s], 16)
                with sp.Fori(1, NCH // 2) as i:
                    for s in range(2):
                        sp.wait_ge(turned[s], i)
                        sp.dma_start(xin[:, s], src[:, ds(i * (2 * TPC) + s * TPC, TPC), :]).then_inc(landed[s], 16)

            @block.tensor
            def _(pe):
                pe.wait_ge(consts_in, 32)
                with pe.Fori(0, NCH // 2) as i:
                    for s in range(2):
                        pe.wait_ge(landed[s], i * 16 + 16)
                        pe.wait_ge(copied[s], i + 1)
                        for j in range(TPC):
                            last = nc.tensor.transpose(ps[:, s, j * TILE:(j + 1) * TILE], xin[:, s, j, :],
                                                       k.ident[0:TILE, 0:TILE])
                        last.then_inc(turned[s], 1)

            @block.vector
            def _(dve):
                for s in range(2):
                    dve.sem_inc(copied[s], 1)
                with dve.Fori(0, NCH // 2) as i:
                    for s in range(2):
                        dve.wait_ge(turned[s], i + 1)
                        nc.vector.tensor_copy(X[:, ds(i * (2 * CH) + s * CH, CH)], ps[:, s, 0:CH]).then_inc(copied[s], 1)


def store_x(k):
    nc, X, ps = k.nc, k.X, k.ps
    dst = k.dram["out"].rearrange("(t p) c -> p t c", p=TILE)
    with ExitStack() as ctx:
        xst = k.sb("st_in", [C, 2, CH], ctx=ctx)
        xout = k.sb("st_out", [TILE, 2, TPC, C], ctx=ctx)
        staged, turned, copied, stored = ([k.sem(f"st_{n}{s}").s for s in range(2)]
                                          for n in ("staged", "turned", "copied", "stored"))
        with nc.Block() as block:
            @block.scalar
            def _(act):
                for s in range(2):
                    act.sem_inc(turned[s], 1)
                with act.Fori(0, NCH // 2) as i:
                    for s in range(2):
                        act.wait_ge(turned[s], i + 1)
                        nc.scalar.activation(xst[:, s], X[:, ds(i * (2 * CH) + s * CH, CH)], ACT.Copy).then_inc(staged[s], 1)

            @block.tensor
            def _(pe):
                with pe.Fori(0, NCH // 2) as i:
                    for s in range(2):
                        pe.wait_ge(staged[s], i + 1)
                        pe.wait_ge(copied[s], i + 1)
                        for j in range(TPC):
                            last = nc.tensor.transpose(ps[0:TILE, s, j * C:(j + 1) * C], xst[:, s, j * TILE:(j + 1) * TILE],
                                                       k.ident[:])
                        last.then_inc(turned[s], 1)

            @block.vector
            def _(dve):
                for s in range(2):
                    dve.sem_inc(copied[s], 1)
                    dve.sem_inc(stored[s], 16)
                with dve.Fori(0, NCH // 2) as i:
                    for s in range(2):
                        dve.wait_ge(turned[s], i + 2)
                        dve.wait_ge(stored[s], i * 16 + 16)
                        nc.vector.tensor_copy(xout[:, s], ps[0:TILE, s, :]).then_inc(copied[s], 1)

            @block.sync
            def _(sp):
                with sp.Fori(0, NCH // 2) as i:
                    for s in range(2):
                        sp.wait_ge(copied[s], i + 2)
                        sp.dma_start(dst[:, ds(i * (2 * TPC) + s * TPC, TPC), :], xout[:, s]).then_inc(stored[s], 16)
                for s in range(2):
                    sp.wait_ge(stored[s], 16 * (NCH // 2) + 16)


def gn_stats(k, tag):
    nc, X, ps = k.nc, k.X, k.ps
    with ExitStack() as ctx:
        sb = lambda n, s, dt=F32: k.sb(f"{tag}_{n}", s, dt, ctx)
        sem = lambda n: k.sem(f"{tag}_{n}").s
        stats, mv = sb("stats", [C, NCH * 6]), sb("mv", [C, B, 2])
        moments, grp, gsq, gstd = sb("moments", [C, 2, B]), sb("grp", [C, 2, B]), sb("gsq", [C, B]), sb("gstd", [C, B])
        group_mat = sb("group_mat", [C, C])
        eps = sb("eps", [C, 1])
        mat_in, own, moments_ready, grouped, var_ready, std_ready = (
            sem(n) for n in ("mat_in", "own", "moments_ready", "grouped", "var_ready", "std_ready"))
        with nc.Block() as block:
            @block.sync
            def _(sp):
                sp.dma_start(group_mat[:], k.dram["group_mat"]).then_inc(mat_in, 16)

            @block.vector
            def _(dve):
                with dve.Fori(0, NCH) as i:
                    nc.vector.bn_stats(stats[:, ds(i * 6, 6)], X[:, ds(i * CH, CH)]).then_inc(own, 1)
                dve.wait_ge(own, NCH)
                c = Chain(dve, own, NCH)
                for b in range(B):
                    ins = nc.vector.bn_aggr(mv[:, b, :], stats[:, b * CPB * 6:(b + 1) * CPB * 6])
                    if b < B - 1:
                        ins.then_inc(own, 1)
                        c.n += 1
                c.link(ins)
                c.link(nc.vector.tensor_copy(moments[:, 0, :], mv[:, :, 0]))
                c.link(nc.vector.tensor_tensor(moments[:, 1, :], mv[:, :, 0], mv[:, :, 0], ALU.mult))
                nc.vector.tensor_tensor(moments[:, 1, :], moments[:, 1, :], mv[:, :, 1], ALU.add).then_inc(moments_ready, 1)
                dve.wait_ge(grouped, 1)
                c.link(nc.vector.tensor_copy(grp[:], ps[:, 0, 0:2 * B].rearrange("p (a b) -> p a b", a=2)))
                c.link(nc.vector.tensor_tensor(gsq[:], grp[:, 0, :], grp[:, 0, :], ALU.mult))
                c.link(nc.vector.tensor_tensor(gsq[:], grp[:, 1, :], gsq[:], ALU.subtract))
                nc.vector.tensor_scalar(gsq[:], gsq[:], 1e-5, None, ALU.add).then_inc(var_ready, 1)
                nc.vector.tensor_scalar(k.gn_nmean[:], grp[:, 0, :], -1.0, None, ALU.mult)
                dve.wait_ge(std_ready, 1)
                nc.vector.reciprocal(k.gn_rstd[:], gstd[:])

            @block.tensor
            def _(pe):
                pe.wait_ge(mat_in, 16)
                pe.wait_ge(moments_ready, 1)
                nc.tensor.matmul(ps[:, 0, 0:2 * B], group_mat[:], moments[:].rearrange("p a b -> p (a b)"),
                                 start=True, stop=True).then_inc(grouped, 1)

            @block.scalar
            def _(act):
                act.wait_ge(var_ready, 1)
                nc.scalar.activation(gstd[:], gsq[:], ACT.Sqrt).then_inc(std_ready, 1)


def layer0(k):
    nc, X, ps = k.nc, k.X, k.ps
    with ExitStack() as ctx:
        sb = lambda n, s, dt=F32: k.sb(f"a0_{n}", s, dt, ctx)
        sem = lambda n, credit=0: k.sem(f"a0_{n}", credit)
        wqkv, bqkv = sb("wqkv", [C, 3 * C]), sb("bqkv", [C, 3])
        wproj, bproj = sb("wproj", [C, C]), sb("bproj", [C, 1])
        head_scale = sb("head_scale", [C, NH0])
        bias, wmask = sb("bias", [TILE, NH0, WIN]), sb("wmask", [TILE, WIN])
        xn = sb("xn", [C, CH])
        Q, Kp, Vp = sb("Q", [C, L]), sb("Kp", [C, LP]), sb("Vp", [C, LP])
        vst, V = sb("vst", [C, 2 * PAIR]), sb("V", [PAIR, NPAIR, C])
        qh = sb("qh", [C, NH0, TILE])
        scored, P = sb("scored", [TILE, 2, WIN]), sb("P", [TILE, 2, WIN])
        PT = sb("PT", [PAIR, 2, NWIN * TILE])
        rmax, nmax = sb("rmax", [TILE, NH0]), sb("nmax", [TILE, NH0])
        rsum, rinv = sb("rsum", [TILE, NH0]), sb("rinv", [TILE, NH0])
        o, oT = sb("o", [TILE, C]), sb("oT", [C, TILE])
        junk = sb("junk", [1, 1])
        w_in, own = sem("w_in"), sem("own")
        xn_ready, qkv_done, q_out, kv_out = sem("xn_ready"), sem("qkv_done", 1), sem("q_out", 1), sem("kv_out")
        v_staged, v_turned, v_out = sem("v_staged"), sem("v_turned"), sem("v_out", 1)
        qh_ready, s_done, s_read, mx_ready = sem("qh_ready"), sem("s_done", 1), sem("s_read", 2), sem("mx_ready")
        p_ready, p_turned, pt_ready, pv_done = sem("p_ready", 2), sem("p_turned", 2), sem("pt_ready", 2), sem("pv_done", 2)
        o_ready, o_turned, ot_ready, proj_done, x_done = (
            sem(n) for n in ("o_ready", "o_turned", "ot_ready", "proj_done", "x_done"))
        loads = [(wqkv[:], "w0_qkv"), (bqkv[:], "b0_qkv"), (wproj[:], "w0_proj"), (bproj[:], "b0_proj"),
                 (head_scale[:], "head_scale0"), (bias[:], "rpb_laid"), (wmask[:], "wmask")]
        rows = lambda t: t[:].rearrange("p (r w) -> p r w", w=WP)

        def tiles(eng, tile):
            tile(0, False, True)
            with eng.Fori(1, TPB - 1) as r:
                tile(r, True, True)
            tile(TPB - 1, True, False)

        def pairs(eng, body):
            with eng.Fori(0, NPAIR // 2) as i:
                body(i * 2, i, 2)
            body(NPAIR - 1, NPAIR // 2, 1)

        TURNS = NPAIR // 2 + 1

        with nc.Block() as block:
            @block.sync
            def _(sp):
                for dst, name in loads:
                    sp.dma_start(dst, k.dram[name]).then_inc(w_in.s, 16)

            @block.vector
            def _(dve):
                for q in (s_read, v_out):
                    dve.sem_inc(q.s, q.credit)
                nc.vector.memset(Kp[:], 0.0)
                nc.vector.memset(Vp[:], 0.0)
                dve.wait_ge(w_in.s, 16 * len(loads))
                for h in range(NH0):
                    ins = nc.vector.tensor_tensor(bias[:, h, :], bias[:, h, :], wmask[:], ALU.add)
                ins.then_inc(own.s, 1)
                dve.wait_ge(own.s, 1)
                with dve.Fori(0, B) as b:
                    with dve.Fori(0, CPB) as i:
                        it = b * CPB + i
                        dve.wait_ge(qkv_done.s, qkv_done.at(it * 3))
                        nc.vector.tensor_scalar(xn[:], X[:, ds(b * L + i * CH, CH)], k.gn_nmean[:, ds(b, 1)],
                                                k.gn_rstd[:, ds(b, 1)], ALU.add, ALU.mult).then_inc(xn_ready.s, 1)
                        for j, buf in ((1, Kp), (2, Vp)):
                            dve.wait_ge(qkv_done.s, qkv_done.at(it * 3 + j + 1))
                            nc.vector.tensor_scalar(rows(buf)[:, ds(i * 8 + PAD, 8), PAD:PAD + HW],
                                                    ps[:, j, 0:CH].rearrange("p (r w) -> p r w", w=HW),
                                                    bqkv[:, j:j + 1], None, ALU.add).then_inc(kv_out.s, 1)

                    def values_out(first, i, count):
                        dve.wait_ge(v_turned.s, b * TURNS + i + 1)
                        nc.vector.tensor_copy(V[:, ds(first, count), :].rearrange("p a c -> p (a c)"),
                                              ps[0:PAIR, 3, 0:count * C]).then_inc(v_out.s, 1)

                    pairs(dve, values_out)

                    def scale_queries(r):
                        it = b * TPB + r
                        dve.wait_ge(s_done.s, s_done.at(it * NH0))
                        nc.vector.tensor_tensor(qh[:], Q[:, ds(r * TILE, TILE)].unsqueeze(1).to_broadcast([C, NH0, TILE]),
                                                head_scale[:].unsqueeze(2).to_broadcast([C, NH0, TILE]),
                                                ALU.mult).then_inc(qh_ready.s, 1)

                    def bias_scores(it, h):
                        s, n = h % 2, it * NH0 + h
                        dve.wait_ge(s_done.s, s_done.at(n + 1))
                        dve.wait_ge(p_ready.s, p_ready.at(n - 1))
                        nc.vector.memset(junk[:], 0.0)
                        nc.vector.tensor_tensor_reduce(out=scored[:, s, :], in0=ps[0:TILE, s, 0:WIN], in1=bias[:, h, :],
                                                       scale=1.0, scalar=-3.0e38, op0=ALU.add, op1=ALU.max,
                                                       accum_out=rmax[:, h:h + 1]).then_inc(s_read.s, 1)
                        dve.wait_ge(s_read.s, s_read.at(n + 1))
                        nc.vector.tensor_scalar(nmax[:, h:h + 1], rmax[:, h:h + 1], -1.0, None, ALU.mult).then_inc(mx_ready.s, 1)

                    def invert_sums(it):
                        dve.wait_ge(p_ready.s, p_ready.at(it * NH0 + NH0))
                        nc.vector.reciprocal(rinv[:], rsum[:]).then_inc(own.s, 1)

                    def normalise(it):
                        dve.wait_ge(own.s, it + 2)
                        dve.wait_ge(pv_done.s, pv_done.at(it * NH0 + NH0))
                        nc.vector.tensor_tensor(o[:].rearrange("p (h d) -> p h d", h=NH0),
                                                ps[0:TILE, 4, 0:C].rearrange("p (h d) -> p h d", h=NH0),
                                                rinv[:].unsqueeze(2).to_broadcast([TILE, NH0, HD0]), ALU.mult).then_inc(o_ready.s, 1)

                    def add_to_x(r):
                        dve.wait_ge(proj_done.s, b * TPB + r + 1)
                        xs = X[:, ds(b * L + r * TILE, TILE)]
                        nc.vector.scalar_tensor_tensor(xs, ps[:, 6, 0:TILE], bproj[:, 0:1], xs, ALU.add, ALU.add)

                    def tile(r, before, after):
                        it = b * TPB + r
                        if before:
                            invert_sums(it - 1)
                        bias_scores(it, 0)
                        if before:
                            normalise(it - 1)
                        bias_scores(it, 1)
                        bias_scores(it, 2)
                        if before:
                            add_to_x(r - 1)
                        bias_scores(it, 3)
                        if after:
                            scale_queries(r + 1)

                    dve.wait_ge(q_out.s, q_out.at((b + 1) * CPB))
                    scale_queries(0)
                    tiles(dve, tile)
                    invert_sums(b * TPB + (TPB - 1))
                    normalise(b * TPB + (TPB - 1))
                    add_to_x(TPB - 1)

            @block.scalar
            def _(act):
                for q in (p_ready, pt_ready, q_out):
                    act.sem_inc(q.s, q.credit)
                act.wait_ge(w_in.s, 16 * len(loads))

                def turned_out(n, s):
                    act.wait_ge(p_turned.s, p_turned.at(n + 1))
                    act.wait_ge(pv_done.s, pv_done.at(n - 1))
                    nc.scalar.activation(PT[:, s, :], ps[0:PAIR, 2 + s, 0:NWIN * TILE], ACT.Copy).then_inc(pt_ready.s, 1)

                with act.Fori(0, B) as b:
                    with act.Fori(0, CPB) as i:
                        act.wait_ge(qkv_done.s, qkv_done.at((b * CPB + i) * 3 + 1))
                        nc.scalar.activation(Q[:, ds(i * CH, CH)], ps[:, 0, 0:CH], ACT.Identity, bias=bqkv[:, 0:1]).then_inc(q_out.s, 1)
                    act.wait_ge(kv_out.s, (b + 1) * (2 * CPB))

                    def stage_values(first, i, count):
                        act.wait_ge(v_out.s, v_out.at(b * TURNS + i))
                        nc.scalar.activation(vst[:, 0:count * PAIR], Vp[:, ds(first * PAIR, count * PAIR)], ACT.Copy).then_inc(v_staged.s, 1)

                    pairs(act, stage_values)

                    def exponentials(it, h):
                        s, n = h % 2, it * NH0 + h
                        act.wait_ge(mx_ready.s, n + 1)
                        act.wait_ge(p_turned.s, p_turned.at(n - 1))
                        nc.scalar.activation(P[:, s, :], scored[:, s, :], ACT.Exp, bias=nmax[:, h:h + 1],
                                             accum_out=rsum[:, h:h + 1]).then_inc(p_ready.s, 1)

                    def output_out(it):
                        act.wait_ge(o_turned.s, it + 1)
                        nc.scalar.activation(oT[:], ps[:, 5, 0:TILE], ACT.Copy).then_inc(ot_ready.s, 1)

                    def tile(r, before, after):
                        it = b * TPB + r
                        exponentials(it, 0)
                        if before:
                            turned_out(it * NH0 - 1, 1)
                        exponentials(it, 1)
                        if before:
                            output_out(it - 1)
                        turned_out(it * NH0, 0)
                        for h in range(2, NH0):
                            exponentials(it, h)
                            turned_out(it * NH0 + h - 1, 1 - h % 2)

                    tiles(act, tile)
                    turned_out((b + 1) * (TPB * NH0) - 1, 1)
                    output_out(b * TPB + (TPB - 1))

            @block.tensor
            def _(pe):
                for q in (qkv_done, s_done, p_turned, pv_done):
                    pe.sem_inc(q.s, q.credit)
                pe.wait_ge(w_in.s, 16 * len(loads))

                def scores(it, r, h):
                    n = it * NH0 + h
                    pe.wait_ge(s_read.s, s_read.at(n - 1))
                    nc.tensor.matmul(ps[0:TILE, h % 2, 0:WIN], qh[:, h, :], Kp[:, ds(r * PAIR, WIN)],
                                     start=True, stop=True).then_inc(s_done.s, 1)

                def turn(it, h):
                    s, n = h % 2, it * NH0 + h
                    pe.wait_ge(p_ready.s, p_ready.at(n + 1))
                    pe.wait_ge(pt_ready.s, pt_ready.at(n - 1))
                    for j in range(NWIN):
                        ins = nc.tensor.transpose(ps[0:PAIR, 2 + s, j * TILE:(j + 1) * TILE],
                                                  P[:, s, j * PAIR:(j + 1) * PAIR], k.ident[0:TILE, 0:TILE])
                    ins.then_inc(p_turned.s, 1)

                def weigh(it, r, h):
                    s, n = h % 2, it * NH0 + h
                    pe.wait_ge(pt_ready.s, pt_ready.at(n + 1))
                    for j in range(NWIN):
                        ins = nc.tensor.matmul(ps[0:TILE, 4, h * HD0:(h + 1) * HD0], PT[:, s, j * TILE:(j + 1) * TILE],
                                               V[:, ds(r + j, 1), h * HD0:(h + 1) * HD0].rearrange("p a c -> p (a c)"),
                                               start=(j == 0), stop=(j == NWIN - 1))
                    ins.then_inc(pv_done.s, 1)

                with pe.Fori(0, B) as b:
                    with pe.Fori(0, CPB) as i:
                        it = b * CPB + i
                        pe.wait_ge(xn_ready.s, it + 1)
                        pe.wait_ge(q_out.s, q_out.at(it))
                        for j in range(3):
                            nc.tensor.matmul(ps[:, j, 0:CH], wqkv[:, j * C:(j + 1) * C], xn[:],
                                             start=True, stop=True).then_inc(qkv_done.s, 1)

                    def turn_values(first, i, count):
                        pe.wait_ge(v_staged.s, b * TURNS + i + 1)
                        for t in range(count):
                            ins = nc.tensor.transpose(ps[0:PAIR, 3, t * C:(t + 1) * C], vst[:, t * PAIR:(t + 1) * PAIR], k.ident[:])
                        ins.then_inc(v_turned.s, 1)

                    pairs(pe, turn_values)

                    def turn_output(it):
                        pe.wait_ge(o_ready.s, it + 1)
                        nc.tensor.transpose(ps[:, 5, 0:TILE], o[:], k.ident[0:TILE, 0:TILE]).then_inc(o_turned.s, 1)

                    def project(it):
                        pe.wait_ge(ot_ready.s, it + 1)
                        nc.tensor.matmul(ps[:, 6, 0:TILE], wproj[:], oT[:], start=True, stop=True).then_inc(proj_done.s, 1)

                    def tile(r, before, after):
                        it = b * TPB + r
                        turn(it, 0)
                        scores(it, r, 2)
                        if before:
                            turn_output(it - 1)
                        weigh(it, r, 0)
                        turn(it, 1)
                        scores(it, r, 3)
                        if before:
                            project(it - 1)
                        weigh(it, r, 1)
                        turn(it, 2)
                        if after:
                            pe.wait_ge(qh_ready.s, it + 2)
                            scores(it + 1, r + 1, 0)
                        weigh(it, r, 2)
                        turn(it, 3)
                        if after:
                            scores(it + 1, r + 1, 1)
                        weigh(it, r, 3)

                    pe.wait_ge(v_out.s, v_out.at((b + 1) * TURNS))
                    pe.wait_ge(qh_ready.s, b * TPB + 1)
                    scores(b * TPB, 0, 0)
                    scores(b * TPB, 0, 1)
                    tiles(pe, tile)
                    turn_output(b * TPB + (TPB - 1))
                    project(b * TPB + (TPB - 1))


def layer_norm(k, tag, eps_value):
    nc, X, N, ps = k.nc, k.X, k.normed(), k.ps
    with ExitStack() as ctx:
        sb = lambda n, s, dt=F32: k.sb(f"{tag}_{n}", s, dt, ctx)
        sem = lambda n, credit=0: k.sem(f"{tag}_{n}", credit)
        xc, sq, std = sb("xc", [C, 2, CH]), sb("sq", [C, 2, CH]), sb("std", [C, 2, CH])
        eps = sb("eps", [C, 1])
        two = lambda n, credit=0: [sem(f"{n}{i}", credit) for i in range(2)]
        eps_set, mean_done, centred, squared, var_done, std_ready, inverted, done = (
            sem("eps_set"), two("mean_done"), two("centred", 1), two("squared", 1), two("var_done", 1),
            two("std_ready", 1), two("inverted", 1), two("done", 1))
        with nc.Block() as block:
            @block.tensor
            def _(pe):
                for s in range(2):
                    pe.sem_inc(var_done[s].s, 1)
                with pe.Fori(0, NCH // 2) as i:
                    for s in range(2):
                        pe.wait_ge(centred[s].s, centred[s].at(i))
                        nc.tensor.matmul(ps[:, s, 0:CH], k.mean_mat[:], X[:, ds(i * (2 * CH) + s * CH, CH)],
                                         start=True, stop=True).then_inc(mean_done[s].s, 1)
                    for s in range(2):
                        pe.wait_ge(squared[s].s, squared[s].at(i + 1))
                        pe.wait_ge(std_ready[s].s, std_ready[s].at(i))
                        nc.tensor.matmul(ps[:, 2 + s, 0:CH], k.mean_mat[:], sq[:, s, :],
                                         start=True, stop=True).then_inc(var_done[s].s, 1)

            @block.scalar
            def _(act):
                for s in range(2):
                    act.sem_inc(squared[s].s, 1)
                    act.sem_inc(std_ready[s].s, 1)
                act.wait_ge(eps_set.s, 1)
                with act.Fori(0, NCH // 2) as i:
                    for s in range(2):
                        act.wait_ge(centred[s].s, centred[s].at(i + 1))
                        act.wait_ge(var_done[s].s, var_done[s].at(i))
                        nc.scalar.activation(sq[:, s, :], xc[:, s, :], ACT.Square).then_inc(squared[s].s, 1)
                    for s in range(2):
                        act.wait_ge(var_done[s].s, var_done[s].at(i + 1))
                        act.wait_ge(inverted[s].s, inverted[s].at(i))
                        nc.scalar.activation(std[:, s, :], ps[:, 2 + s, 0:CH], ACT.Sqrt, bias=eps[:]).then_inc(std_ready[s].s, 1)

            @block.vector
            def _(dve):
                nc.vector.memset(eps[:], eps_value).then_inc(eps_set.s, 1)
                for s in range(2):
                    dve.sem_inc(centred[s].s, 1)
                    dve.sem_inc(inverted[s].s, 1)
                    dve.sem_inc(done[s].s, 1)
                with dve.Fori(0, NCH // 2) as i:
                    for s in range(2):
                        dve.wait_ge(mean_done[s].s, i + 1)
                        dve.wait_ge(done[s].s, done[s].at(i))
                        nc.vector.tensor_tensor(xc[:, s, :], X[:, ds(i * (2 * CH) + s * CH, CH)], ps[:, s, 0:CH],
                                                ALU.subtract).then_inc(centred[s].s, 1)
                    for s in range(2):
                        dve.wait_ge(std_ready[s].s, std_ready[s].at(i + 1))
                        dve.wait_ge(done[s].s, done[s].at(i))
                        nc.vector.reciprocal(std[:, s, :], std[:, s, :]).then_inc(inverted[s].s, 1)
                        dve.wait_ge(inverted[s].s, inverted[s].at(i + 1))
                        nc.vector.tensor_tensor(N[:, ds(i * (2 * CH) + s * CH, CH)], xc[:, s, :], std[:, s, :],
                                                ALU.mult).then_inc(done[s].s, 1)


def attention(k, tag):
    nc, X, N, ps = k.nc, k.X, k.normed(), k.ps
    with ExitStack() as ctx:
        sb = lambda n, s, dt=F32: k.sb(f"{tag}_{n}", s, dt, ctx)
        sem = lambda n, credit=0: k.sem(f"{tag}_{n}", credit)
        wqkv, masks = sb("wqkv", [C, 3 * C]), sb("masks", [TILE, TPC, CH])
        Q, K, V = sb("Q", [C, L]), sb("K", [C, L]), sb("V", [TILE, TPB, C])
        ncs = sb("ncs", [C, CH])
        qh, row = sb("qh", [C, 2, TILE]), sb("row", [TILE, 2, L])
        PT = sb("PT", [TILE, 2, CH])
        rmax, nmax, rsum, rinv = (sb(n, [TILE, 2]) for n in ("rmax", "nmax", "rsum", "rinv"))
        o = sb("o", [TILE, 2, C])
        w_in, n_copied, qkv_done, q_out, kv_out = (
            sem("w_in"), sem("n_copied"), sem("qkv_done", 1), sem("q_out", 1), sem("kv_out", 1))
        qh_ready, s_done, s_read, row_max, neg_max = sem("qh_ready"), sem("s_done"), sem("s_read", 2), sem("row_max"), sem("neg_max")
        p_ready, pt_ready, pv_blk, blk_turned = sem("p_ready"), sem("pt_ready", 2), sem("pv_blk", 2), sem("blk_turned")
        inverted, o_ready, o_turned, x_done = sem("inverted"), sem("o_ready"), sem("o_turned"), sem("x_done", 2)
        loads = [(wqkv[:], "w2_qkv"), (masks[:], "causal_masks")]

        def tiles(b):
            for t in range(TPB):
                I, j = t // TPC, t % TPC
                first = b * (TPC * sum(range(1, TPB // TPC + 1))) + (TPC * (I * (I + 1) // 2) + j * (I + 1))
                yield I, j, t % 2, b * TPB + t, first

        with nc.Block() as block:
            @block.sync
            def _(sp):
                for dst, name in loads:
                    sp.dma_start(dst, k.dram[name]).then_inc(w_in.s, 16)

            @block.vector
            def _(dve):
                for q in (s_read, kv_out, x_done):
                    dve.sem_inc(q.s, q.credit)
                dve.wait_ge(w_in.s, 16 * len(loads))
                with dve.Fori(0, B) as b:
                    with dve.Fori(0, CPB) as i:
                        it = b * CPB + i
                        dve.wait_ge(qkv_done.s, qkv_done.at(it * 3))
                        nc.vector.tensor_copy(ncs[:], N[:, ds(b * L + i * CH, CH)]).then_inc(n_copied.s, 1)
                        dve.wait_ge(qkv_done.s, qkv_done.at(it * 3 + 2))
                        nc.vector.tensor_copy(K[:, ds(i * CH, CH)], ps[:, 1, 0:CH]).then_inc(kv_out.s, 1)
                        dve.wait_ge(qkv_done.s, qkv_done.at(it * 3 + 3))
                        nc.vector.tensor_copy(V[:, ds(i * TPC, TPC), :], ps[0:TILE, 2, :].rearrange("p (t c) -> p t c", c=C)).then_inc(kv_out.s, 1)

                    def maxima(I, j, s, n, g):
                        dve.wait_ge(q_out.s, q_out.at((b + 1) * CPB))
                        nc.vector.tensor_scalar(qh[:, s, :], Q[:, (j + I * TPC) * TILE:(j + I * TPC + 1) * TILE],
                                                L ** -0.5, None, ALU.mult).then_inc(qh_ready.s, 1)
                        for c in range(I + 1):
                            dve.wait_ge(s_done.s, g + c + 1)
                            dst, src = row[:, s, c * CH:(c + 1) * CH], ps[0:TILE, 2 * s + c % 2, 0:CH]
                            if c < I:
                                nc.vector.tensor_copy(dst, src).then_inc(s_read.s, 1)
                            else:
                                nc.vector.tensor_tensor(dst, src, masks[:, j, :], ALU.add).then_inc(s_read.s, 1)
                        dve.wait_ge(s_read.s, s_read.at(g + I + 1))
                        nc.vector.tensor_reduce(rmax[:, s:s + 1], row[:, s, 0:(I + 1) * CH], AX.X, ALU.max).then_inc(row_max.s, 1)
                        dve.wait_ge(row_max.s, n + 1)
                        nc.vector.tensor_scalar(nmax[:, s:s + 1], rmax[:, s:s + 1], -1.0, None, ALU.mult).then_inc(neg_max.s, 1)

                    def normalise(I, j, s, n, g):
                        dve.wait_ge(p_ready.s, n + 1)
                        nc.vector.reciprocal(rinv[:, s:s + 1], rsum[:, s:s + 1]).then_inc(inverted.s, 1)
                        dve.wait_ge(inverted.s, n + 1)
                        dve.wait_ge(pv_blk.s, pv_blk.at(g + I + 1))
                        nc.vector.tensor_scalar(o[:, s, :], ps[0:TILE, 6 + s, 0:C], rinv[:, s:s + 1], None, ALU.mult).then_inc(o_ready.s, 1)

                    def add_to_x(I, j, s, n, g):
                        dve.wait_ge(o_turned.s, n + 1)
                        xs = X[:, ds(b * L + (j + I * TPC) * TILE, TILE)]
                        nc.vector.tensor_tensor(xs, xs, ps[:, 6 + s, C:C + TILE], ALU.add).then_inc(x_done.s, 1)

                    todo = list(tiles(b))
                    maxima(*todo[0])
                    for t in range(TPB):
                        if t + 1 < TPB:
                            maxima(*todo[t + 1])
                        if t > 0:
                            add_to_x(*todo[t - 1])
                        normalise(*todo[t])
                    add_to_x(*todo[-1])

            @block.scalar
            def _(act):
                for q in (pt_ready, q_out):
                    act.sem_inc(q.s, q.credit)
                with act.Fori(0, B) as b:
                    with act.Fori(0, CPB) as i:
                        act.wait_ge(qkv_done.s, qkv_done.at((b * CPB + i) * 3 + 1))
                        nc.scalar.activation(Q[:, ds(i * CH, CH)], ps[:, 0, 0:CH], ACT.Copy).then_inc(q_out.s, 1)

                    for I, j, s, n, g in tiles(b):
                        act.wait_ge(neg_max.s, n + 1)
                        p = row[:, s, 0:(I + 1) * CH]
                        nc.scalar.activation(p, p, ACT.Exp, bias=nmax[:, s:s + 1], accum_out=rsum[:, s:s + 1]).then_inc(p_ready.s, 1)
                        for c in range(I + 1):
                            act.wait_ge(blk_turned.s, g + c + 1)
                            act.wait_ge(pv_blk.s, pv_blk.at(g + c - (1 if c else 0)))
                            nc.scalar.activation(PT[:, c % 2, :], ps[0:TILE, 4 + c % 2, 0:CH], ACT.Copy).then_inc(pt_ready.s, 1)

            @block.tensor
            def _(pe):
                for q in (qkv_done, pv_blk):
                    pe.sem_inc(q.s, q.credit)
                pe.wait_ge(w_in.s, 16 * len(loads))
                with pe.Fori(0, B) as b:
                    with pe.Fori(0, CPB) as i:
                        it = b * CPB + i
                        pe.wait_ge(n_copied.s, it + 1)
                        pe.wait_ge(q_out.s, q_out.at(it))
                        for j in range(2):
                            nc.tensor.matmul(ps[:, j, 0:CH], wqkv[:, j * C:(j + 1) * C], ncs[:],
                                             start=True, stop=True).then_inc(qkv_done.s, 1)
                        for t in range(TPC):
                            ins = nc.tensor.matmul(ps[0:TILE, 2, t * C:(t + 1) * C], ncs[:, t * TILE:(t + 1) * TILE],
                                                   wqkv[:, 2 * C:3 * C], start=True, stop=True)
                        ins.then_inc(qkv_done.s, 1)

                    def scores(I, j, s, n, g):
                        pe.wait_ge(kv_out.s, kv_out.at((b + 1) * (2 * CPB)))
                        pe.wait_ge(qh_ready.s, n + 1)
                        for c in range(I + 1):
                            pe.wait_ge(s_read.s, s_read.at(g + c - (1 if c else 0)))
                            nc.tensor.matmul(ps[0:TILE, 2 * s + c % 2, 0:CH], qh[:, s, :], K[:, c * CH:(c + 1) * CH],
                                             start=True, stop=True).then_inc(s_done.s, 1)

                    def weigh(I, c, s, g):
                        pe.wait_ge(pt_ready.s, pt_ready.at(g + c + 1))
                        for t in range(TPC):
                            first, last = c == 0 and t == 0, c == I and t == TPC - 1
                            ins = nc.tensor.matmul(ps[0:TILE, 6 + s, 0:C], PT[:, c % 2, t * TILE:(t + 1) * TILE],
                                                   V[:, c * TPC + t, :], start=first, stop=last)
                        ins.then_inc(pv_blk.s, 1)

                    def use(I, j, s, n, g):
                        pe.wait_ge(p_ready.s, n + 1)
                        pe.wait_ge(x_done.s, x_done.at(n - 1))
                        for c in range(I + 1):
                            pe.wait_ge(pt_ready.s, pt_ready.at(g + c - (1 if c else 0)))
                            for t in range(TPC):
                                ins = nc.tensor.transpose(ps[0:TILE, 4 + c % 2, t * TILE:(t + 1) * TILE],
                                                          row[:, s, c * CH + t * TILE:c * CH + (t + 1) * TILE],
                                                          k.ident[0:TILE, 0:TILE])
                            ins.then_inc(blk_turned.s, 1)
                            if c > 0:
                                weigh(I, c - 1, s, g)
                        weigh(I, I, s, g)

                    def turn_output(I, j, s, n, g):
                        pe.wait_ge(o_ready.s, n + 1)
                        nc.tensor.transpose(ps[:, 6 + s, C:C + TILE], o[:, s, :], k.ident[0:TILE, 0:TILE]).then_inc(o_turned.s, 1)

                    todo = list(tiles(b))
                    scores(*todo[0])
                    for t in range(TPB):
                        if t + 1 < TPB:
                            scores(*todo[t + 1])
                        if t > 0:
                            turn_output(*todo[t - 1])
                        use(*todo[t])
                    turn_output(*todo[-1])


def attention_heads(k, tag):
    nc, X, N, ps = k.nc, k.X, k.normed(), k.ps
    v, g = nc.vector, nc.gpsimd
    H, D = NH3, HD3
    NI = TPB // TPC
    ROWS = 6 * D
    KR = ROWS + 3
    VC = 32
    Q_PARTS, K_PARTS = (0, 0, 1, 1, 0, 2), (0, 1, 0, 1, 2, 0)
    with ExitStack() as ctx:
        sb = lambda n, s, dt=F32: k.sb(f"{tag}_{n}", s, dt, ctx)
        sem = lambda n, credit=0: k.sem(f"{tag}_{n}", credit)
        wqkv, wproj = sb("wqkv", [C, 3 * C]), sb("wproj", [C, C])
        identb = sb("identb", [TILE, TILE], BF16)
        tri, triT, full = (sb(n, [TILE, TILE], BF16) for n in ("tri", "triT", "full"))
        part = [sb(f"part{i}", [TILE, TPC, 2, C], BF16) for i in range(3)]
        stack = [sb(n, [TILE, TPC, H, ROWS], BF16) for n in ("q_stack", "k_stack")]
        KT, QT = sb("KT", [KR, H, L], BF16), sb("QT", [KR, H, CH], BF16)
        V, Vh = sb("V", [TILE, TPB, H, D]), sb("Vh", [TILE, 2, TPB, VC])
        fold = sb("fold", [C, D + 1])
        PT = sb("PT", [TILE, 2, 2, CH])
        rest = PT[:].rearrange("p a b c -> p (a b c)")[:, 0:TPC * 2 * C].rearrange("p (t a c) -> p t a c", t=TPC, a=2)
        maxes, nmax, nrest = sb("maxes", [TILE, TPC, NI]), sb("nmax", [TILE, TPC]), sb("nrest", [TILE, TPC])
        mrow = sb("mrow", [TILE, TPC, KR], BF16)
        rinv, oT = sb("rinv", [TILE, TPC]), sb("oT", [C, CH])
        o = part[0][:].rearrange("p t a c -> p t (a c)").bitcast(F32)
        zero, junk, zero_set = sb("zero", [TILE, 1]), sb("junk", [TILE, 2]), sem("zero_set")
        ncs = oh = oT
        w_in, own, const_ready = sem("w_in"), sem("own"), sem("const_ready")
        ncs_ready, tok_done, v_copied = sem("ncs_ready"), sem("tok_done"), sem("v_copied")
        hi_done, mid_done, lo_done = sem("hi_done"), sem("mid_done"), sem("lo_done")
        qk_read, stacked, inverted = sem("qk_read"), sem("stacked"), sem("inverted")
        vh_ready, oh_ready, folded = sem("vh_ready"), sem("oh_ready", 2), sem("folded")
        turned, q_out, k_out = sem("turned"), sem("q_out", 1), sem("k_out", 4)
        sm_done, sm_read, mrow_ready, mrow_turned, qm_ready = (
            sem("sm_done"), sem("sm_read", 6), sem("mrow_ready"), sem("mrow_turned"), sem("qm_ready"))
        st_done, p_ready, pv_done, o_read = sem("st_done"), sem("p_ready", 2), sem("pv_done", 2), sem("o_read", 2)
        o_turned, ot_ready, proj_done, x_done = sem("o_turned"), sem("ot_ready"), sem("proj_done"), sem("x_done", 1)
        u16 = mybir.dt.uint16
        loads = [(wqkv[:], "w3_qkv"), (wproj[:], "w3_proj"), (identb[:].bitcast(u16), "identb"),
                 (tri[:].bitcast(u16), "tri"), (triT[:].bitcast(u16), "triT"),
                 (full[:].bitcast(u16), "full"), (fold[:], "fold")]
        bank16 = lambda i: ps[:, i, :].bitcast(BF16)

        unit0 = lambda b, I, h: b * (H * 2 * NI * (NI + 1)) + H * 2 * I * (I + 1) + h * (4 * (I + 1))
        pair0 = lambda b, I, h: b * (H * NI * (NI + 1)) + H * I * (I + 1) + h * (2 * (I + 1))

        FREE = (0, 1, 3, 4, 5, 6)

        def m_bank(I, h, u, banks):
            return banks[u % 2] if len(banks) == 2 else banks[(h * 4 * (I + 1) + u) % len(banks)]

        def heads(eng, first, step, last):
            first()
            with eng.Fori(0, (H - 2) // 2) as i:
                step(i * 2, i * 2 + 2, i * 2 + 1, 0)
                step(i * 2 + 1, i * 2 + 3, i * 2 + 2, 1)
            step(H - 2, None, H - 1, 0)
            step(H - 1, None, None, 1)
            last()

        with nc.Block() as block:
            @block.sync
            def _(sp):
                for dst, name in loads:
                    sp.dma_start(dst, k.dram[name]).then_inc(w_in.s, 16)

            @block.gpsimd
            def _(pool):
                g.memset(zero[:], 0.0).then_inc(zero_set.s, 1)
                pool.wait_ge(zero_set.s, 1)
                with pool.Fori(0, B) as b:
                    with pool.Fori(0, NI) as i:
                        it = b * NI + i

                        def stage_values(h, s):
                            pool.wait_ge(v_copied.s, it + 1)
                            pool.wait_ge(oh_ready.s, oh_ready.at(it * H + h - 1))
                            g.tensor_tensor(junk[:, s:s + 1], zero[:], zero[:], ALU.mult)
                            g.tensor_copy(Vh[:, s, :, 0:D], V[:, :, ds(h, 1), :].rearrange("p t a d -> p (t a) d")).then_inc(vh_ready.s, 1)

                        with pool.Fori(0, H // 2) as hh:
                            for s in range(2):
                                stage_values(hh * 2 + s, s)

            @block.vector
            def _(dve):
                for q in (q_out, sm_read, o_read, x_done):
                    dve.sem_inc(q.s, q.credit)
                v.memset(KT[ROWS:KR], 1.0)
                v.memset(V[:], 0.0)
                v.memset(Vh[:, :, :, D + 1:VC], 0.0)
                v.memset(Vh[:, :, :, D:D + 1], 1.0)
                v.memset(mrow[:], 0.0).then_inc(const_ready.s, 1)
                dve.wait_ge(w_in.s, 16 * len(loads))
                with dve.Fori(0, B) as b:
                    for I in range(NI):
                        it = b * NI + I
                        v.tensor_copy(ncs[:], N[:, ds(b * L + I * CH, CH)]).then_inc(ncs_ready.s, 1)
                        dve.wait_ge(tok_done.s, it + 1)
                        flat = lambda t: t[:].rearrange("p t a c -> p t (a c)")
                        v.tensor_copy(flat(part[0]), ps[0:TILE, 0:TPC, 0:2 * C]).then_inc(hi_done.s, 1)
                        dve.wait_ge(hi_done.s, it + 1)
                        restf = rest.rearrange("p t a c -> p t (a c)")
                        v.tensor_tensor(restf, ps[0:TILE, 0:TPC, 0:2 * C], flat(part[0]), ALU.subtract).then_inc(qk_read.s, 1)
                        dve.wait_ge(qk_read.s, it + 1)
                        v.tensor_copy(flat(part[1]), restf).then_inc(mid_done.s, 1)
                        dve.wait_ge(mid_done.s, it + 1)
                        v.tensor_tensor(flat(part[2]), restf, flat(part[1]), ALU.subtract).then_inc(lo_done.s, 1)
                        dve.wait_ge(lo_done.s, it + 1)
                        for a, parts in enumerate((Q_PARTS, K_PARTS)):
                            for r in range(6):
                                for t in range(TPC):
                                    ins = v.tensor_copy(stack[a][:, t, :, r * D:(r + 1) * D],
                                                        part[parts[r]][:, t, a, :].rearrange("p (h d) -> p h d", d=D))
                        ins.then_inc(stacked.s, 1)
                        for h in range(H):
                            dve.wait_ge(turned.s, it * H + h + 1)
                            v.tensor_copy(QT[0:ROWS, h, :], bank16(3 + h % 4)[0:ROWS, 0:CH]).then_inc(q_out.s, 1)

                        def reduces(h, banks=(0, 1)):
                            for u in range(4 * (I + 1)):
                                j, c = u // (I + 1), u % (I + 1)
                                n = unit0(b, I, h) + u
                                dve.wait_ge(sm_done.s, n + 1)
                                w = CH if c < I else (j + 1) * TILE
                                v.tensor_reduce(maxes[:, j, c:c + 1], ps[0:TILE, m_bank(I, h, u, banks), 0:w], AX.X,
                                                ALU.max).then_inc(sm_read.s, 1)

                        def max_parts(h):
                            hn = it * H + h
                            dve.wait_ge(sm_read.s, sm_read.at(unit0(b, I, h) + 4 * (I + 1)))
                            chain = Chain(dve, own.s, hn * 6)
                            link = chain.link
                            link(v.tensor_reduce(nmax[:], maxes[:, :, 0:I + 1], AX.X, ALU.max))
                            link(v.tensor_scalar(nmax[:], nmax[:], -1.0, None, ALU.mult))
                            link(v.tensor_copy(mrow[:, :, ROWS], nmax[:]))
                            link(v.tensor_tensor(nrest[:], nmax[:], mrow[:, :, ROWS], ALU.subtract))
                            link(v.tensor_copy(mrow[:, :, ROWS + 1], nrest[:]))
                            link(v.tensor_tensor(mrow[:, :, ROWS + 2], nrest[:], mrow[:, :, ROWS + 1], ALU.subtract))
                            dve.sem_inc(mrow_ready.s, 1)

                        def first():
                            reduces(0, FREE)
                            max_parts(0)
                            reduces(1, FREE)
                            dve.wait_ge(mrow_turned.s, it * H + 1)
                            max_parts(1)

                        def step(h, hm, ht, s):
                            hn = it * H + h
                            if hm is not None:
                                reduces(hm)
                                dve.wait_ge(mrow_turned.s, hn + 2)
                                max_parts(hm)
                            dve.wait_ge(folded.s, hn + 1)
                            O = ps[0:TILE, 2, 256:256 + TPC * (D + 1)].rearrange("p (t d) -> p t d", d=D + 1)
                            v.reciprocal(rinv[:], O[:, :, D]).then_inc(inverted.s, 1)
                            dve.wait_ge(inverted.s, hn + 1)
                            v.tensor_tensor(o[:, :, ds(h * D, D)], O[:, :, 0:D],
                                            rinv[:].unsqueeze(2).to_broadcast([TILE, TPC, D]), ALU.mult).then_inc(o_read.s, 1)

                        def last():
                            dve.wait_ge(proj_done.s, it + 1)
                            xs = X[:, ds(b * L + I * CH, CH)]
                            v.tensor_tensor(xs, xs, ps[:, 0, 0:CH], ALU.add).then_inc(x_done.s, 1)

                        heads(dve, first, step, last)

            @block.scalar
            def _(act):
                for q in (k_out, p_ready, oh_ready):
                    act.sem_inc(q.s, q.credit)
                with act.Fori(0, B) as b:
                    for I in range(NI):
                        it = b * NI + I
                        for t in range(TPC):
                            act.wait_ge(const_ready.s, 1)
                            act.wait_ge(qk_read.s, it + 1)
                            ins = nc.scalar.activation(V[:, I * TPC + t, :, 0:D],
                                                       ps[0:TILE, t, 2 * C:3 * C].rearrange("p (h d) -> p h d", d=D), ACT.Copy)
                        ins.then_inc(v_copied.s, 1)
                        for h in range(H):
                            act.wait_ge(q_out.s, q_out.at(it * H + h + 1))
                            nc.scalar.activation(KT[0:ROWS, h, I * CH:(I + 1) * CH], bank16(3 + h % 4)[0:ROWS, CH:2 * CH],
                                                 ACT.Copy).then_inc(k_out.s, 1)

                        def max_out(h):
                            act.wait_ge(mrow_turned.s, it * H + h + 1)
                            nc.scalar.activation(QT[ROWS:KR, ds(h, 1), :].rearrange("p a c -> p (a c)"),
                                                 bank16(2)[ROWS:KR, 0:CH], ACT.Copy).then_inc(qm_ready.s, 1)

                        def exponentials(h, e):
                            n = pair0(b, I, h) + e
                            w = CH if e < 2 * I + 1 or I == 0 else CH // 2
                            act.wait_ge(st_done.s, n + 1)
                            act.wait_ge(pv_done.s, pv_done.at(n - 1))
                            bank = 3 + 2 * (e % 2)
                            nc.scalar.activation(PT[:, e % 2, :, 0:w], ps[0:TILE, bank:bank + 2, 0:w], ACT.Exp,
                                                 scale=D ** -0.5).then_inc(p_ready.s, 1)

                        def first():
                            max_out(0)
                            exponentials(0, 0)

                        def step(h, hm, ht, s):
                            for e in range(1, 2 * (I + 1)):
                                exponentials(h, e)
                                if e == min(2, 2 * I + 1) and ht is not None:
                                    max_out(ht)
                            if ht is not None:
                                exponentials(ht, 0)
                            act.wait_ge(pv_done.s, pv_done.at(pair0(b, I, h) + 2 * (I + 1)))
                            nc.scalar.activation(oh[:], ps[:, 7, 0:CH], ACT.Copy).then_inc(oh_ready.s, 1)

                        def last():
                            act.wait_ge(o_turned.s, it + 1)
                            nc.scalar.activation(oT[:], ps[:, 2, 0:CH], ACT.Copy).then_inc(ot_ready.s, 1)

                        heads(act, first, step, last)

            @block.tensor
            def _(pe):
                pe.sem_inc(pv_done.s, pv_done.credit)
                pe.wait_ge(w_in.s, 16 * len(loads))
                with pe.Fori(0, B) as b:
                    for I in range(NI):
                        it = b * NI + I
                        pe.wait_ge(ncs_ready.s, it + 1)
                        pe.wait_ge(x_done.s, x_done.at(it))
                        for t in range(TPC):
                            ins = nc.tensor.matmul(ps[0:TILE, t, 0:3 * C], ncs[:, t * TILE:(t + 1) * TILE], wqkv[:],
                                                   start=True, stop=True)
                        ins.then_inc(tok_done.s, 1)
                        for h in range(H):
                            pe.wait_ge(stacked.s, it + 1)
                            pe.wait_ge(v_copied.s, it + 1)
                            pe.wait_ge(k_out.s, k_out.at(it * H + h - 3))
                            for a in range(2):
                                for t in range(TPC):
                                    ins = nc.tensor.transpose(bank16(3 + h % 4)[0:ROWS, a * CH + t * TILE:a * CH + (t + 1) * TILE],
                                                              stack[a][:, t, h, :], identb[:])
                            ins.then_inc(turned.s, 1)

                        def m_unit(h, u, banks=(0, 1)):
                            j, c = u // (I + 1), u % (I + 1)
                            bank = m_bank(I, h, u, banks)
                            pe.wait_ge(sm_read.s, sm_read.at(unit0(b, I, h) + u + 1 - len(banks)))
                            w = CH if c < I else (j + 1) * TILE
                            q = QT[0:ROWS, ds(h, 1), j * TILE:(j + 1) * TILE].rearrange("p a c -> p (a c)")
                            keys = KT[0:ROWS, ds(h, 1), c * CH:c * CH + w].rearrange("p a c -> p (a c)")
                            ins = nc.tensor.matmul(ps[0:TILE, bank, 0:w], q, keys, start=True, stop=(c < I))
                            if c == I:
                                ins = nc.tensor.matmul(ps[0:TILE, bank, j * TILE:w], identb[:], tri[:], start=False, stop=True)
                            ins.then_inc(sm_done.s, 1)

                        def turn_max(h):
                            hn = it * H + h
                            pe.wait_ge(mrow_ready.s, hn + 1)
                            pe.wait_ge(o_read.s, o_read.at(hn - 1))
                            for t in range(TPC):
                                ins = nc.tensor.transpose(bank16(2)[0:KR, t * TILE:(t + 1) * TILE], mrow[:, t, :], identb[:])
                            ins.then_inc(mrow_turned.s, 1)

                        def e_scores(h, e):
                            pe.wait_ge(p_ready.s, p_ready.at(pair0(b, I, h) + e - 1))
                            diagonal = e - 2 * I
                            q0 = CH // 2 if diagonal == 1 and I > 0 else 0
                            for t in range(2):
                                kt = 2 * e + t
                                bank = 3 + 2 * (e % 2) + t
                                keys = KT[:, ds(h, 1), kt * TILE:(kt + 1) * TILE].rearrange("p a c -> p (a c)")
                                q = QT[:, ds(h, 1), q0:CH].rearrange("p a c -> p (a c)")
                                ins = nc.tensor.matmul(ps[0:TILE, bank, 0:CH - q0], keys, q, start=True, stop=(diagonal < 0))
                                if diagonal >= 0:
                                    own_tile = kt - 4 * I - q0 // TILE
                                    for j in range(own_tile if I == 0 else 0):
                                        nc.tensor.matmul(ps[0:TILE, bank, j * TILE:(j + 1) * TILE], identb[:], full[:],
                                                         start=False, stop=False)
                                    ins = nc.tensor.matmul(ps[0:TILE, bank, own_tile * TILE:(own_tile + 1) * TILE], identb[:], triT[:],
                                                           start=False, stop=True)
                            ins.then_inc(st_done.s, 1)

                        def e_values(h, e, s):
                            pe.wait_ge(p_ready.s, p_ready.at(pair0(b, I, h) + e + 1))
                            if e == 0:
                                pe.wait_ge(vh_ready.s, it * H + h + 1)
                                pe.wait_ge(oh_ready.s, oh_ready.at(it * H + h))
                            q0 = CH // 2 if e == 2 * I + 1 and I > 0 else 0
                            for t in range(2):
                                kt = 2 * e + t
                                c0 = TILE * max(kt - 4 * I, 0) if I > 0 else 0
                                col = VC * (kt % 4)
                                ins = nc.tensor.matmul(ps[col:col + VC, 7, c0:CH], Vh[:, s, kt, :], PT[:, e % 2, t, c0 - q0:CH - q0],
                                                       start=(kt < 4), stop=(kt >= 4 * I), skip_group_check=True)
                            ins.then_inc(pv_done.s, 1)

                        def fold_head(h):
                            pe.wait_ge(oh_ready.s, oh_ready.at(it * H + h + 1))
                            pe.wait_ge(o_read.s, o_read.at(it * H + h))
                            for t in range(TPC):
                                ins = nc.tensor.matmul(ps[0:TILE, 2, 256 + t * (D + 1):256 + (t + 1) * (D + 1)],
                                                       oh[:, t * TILE:(t + 1) * TILE], fold[:], start=True, stop=True)
                            ins.then_inc(folded.s, 1)

                        def first():
                            pe.wait_ge(k_out.s, k_out.at(it * H + H))
                            pe.wait_ge(v_copied.s, it + 1)
                            for u in range(4 * (I + 1)):
                                m_unit(0, u, FREE)
                            for u in range(4 * (I + 1)):
                                m_unit(1, u, FREE)
                                if u == 3:
                                    turn_max(0)
                            pe.wait_ge(sm_read.s, sm_read.at(unit0(b, I, 2)))
                            pe.wait_ge(qm_ready.s, it * H + 1)
                            e_scores(0, 0)
                            e_scores(0, 1)

                        def step(h, hm, ht, s):
                            pairs = 2 * (I + 1)
                            for e in range(1, pairs + 1):
                                if 1 < e < pairs:
                                    e_scores(h, e)
                                if e == pairs and ht is not None:
                                    pe.wait_ge(qm_ready.s, it * H + ht + 1)
                                    e_scores(ht, 0)
                                if hm is not None:
                                    m_unit(hm, 2 * e - 2)
                                if e == min(2, 2 * I + 1) and ht is not None:
                                    turn_max(ht)
                                e_values(h, e - 1, s)
                                if hm is not None:
                                    m_unit(hm, 2 * e - 1)
                            if ht is not None:
                                e_scores(ht, 1)
                            fold_head(h)

                        def last():
                            pe.wait_ge(o_read.s, o_read.at(it * H + H))
                            for t in range(TPC):
                                ins = nc.tensor.transpose(ps[:, 2, t * TILE:(t + 1) * TILE], o[:, t, :], k.ident[0:TILE, 0:TILE])
                            ins.then_inc(o_turned.s, 1)
                            pe.wait_ge(ot_ready.s, it + 1)
                            nc.tensor.matmul(ps[:, 0, 0:CH], wproj[:], oT[:], start=True, stop=True).then_inc(proj_done.s, 1)

                        heads(pe, first, step, last)


def experts(k):
    nc, X, N, ps = k.nc, k.X, k.normed(), k.ps
    NT = T // TILE
    with ExitStack() as ctx:
        sb = lambda n, s, dt=F32: k.sb(f"moe_{n}", s, dt, ctx)
        sem = lambda n, credit=0: k.sem(f"moe_{n}", credit)
        wr, br = sb("wr", [C, NE]), sb("br", [NE, 1])
        we, be, spread = sb("we", [C, NE, C]), sb("be", [NE, C]), sb("spread", [NE, NE, C])
        rank = sb("rank", [TILE, NE])
        lt = sb("lt", [NE, CH])
        logit, prob, left, pick = (sb(n, [TILE, NT, NE]) for n in ("logit", "prob", "left", "pick"))
        best, top1, top2 = (sb(n, [TILE, NT]) for n in ("best", "top1", "top2"))
        gst, gT = sb("gst", [TILE, TPC * NE]), sb("gT", [NE, CH])
        xg = sb("xg", [C, 2, CH])
        w_in, own = sem("w_in"), sem("own")
        logit_done, lt_ready, lt_turned, l_out = sem("logit_done"), sem("lt_ready"), sem("lt_turned"), sem("l_out")
        shifted, exped = sem("shifted"), sem("exped")
        g_staged, g_turned, gt_ready, spread_done, xg_ready, xg_used, y_done, x_done = (
            sem("g_staged"), sem("g_turned"), sem("gt_ready"), sem("spread_done"), sem("xg_ready", 2), sem("xg_used", 2),
            sem("y_done"), sem("x_done", 1))
        loads = [(wr[:], "w2_router"), (br[:], "b2_router"), (we[:], "w2_expert"), (be[:], "b2_expert"),
                 (spread[:], "spread8"), (rank[:], "rank8")]
        over = lambda t: t[:].unsqueeze(2).to_broadcast([TILE, NT, NE])
        with nc.Block() as block:
            @block.sync
            def _(sp):
                for dst, name in loads:
                    sp.dma_start(dst, k.dram[name]).then_inc(w_in.s, 16)

            @block.tensor
            def _(pe):
                pe.sem_inc(xg_used.s, xg_used.credit)
                pe.wait_ge(w_in.s, 16 * len(loads))
                with pe.Fori(0, NCH) as i:
                    nc.tensor.matmul(ps[0:NE, 0, 0:CH], wr[:], N[:, ds(i * CH, CH)], start=True, stop=True).then_inc(logit_done.s, 1)
                    pe.wait_ge(lt_ready.s, i + 1)
                    for t in range(TPC):
                        ins = nc.tensor.matmul(ps[0:TILE, 1, t * NE:(t + 1) * NE], lt[:, t * TILE:(t + 1) * TILE],
                                               k.ident[0:NE, 0:NE], start=True, stop=True)
                    ins.then_inc(lt_turned.s, 1)
                    pe.wait_ge(l_out.s, i + 1)
                with pe.Fori(0, NCH) as i:
                    pe.wait_ge(g_staged.s, i + 1)
                    for t in range(TPC):
                        ins = nc.tensor.transpose(ps[0:NE, 2, t * TILE:(t + 1) * TILE], gst[:, t * NE:(t + 1) * NE],
                                                  k.ident[0:TILE, 0:TILE])
                    ins.then_inc(g_turned.s, 1)
                    pe.wait_ge(gt_ready.s, i + 1)
                    pe.wait_ge(x_done.s, x_done.at(i))
                    nc.tensor.matmul(ps[:, 3, 0:CH], be[:], gT[:], start=True, stop=False)

                    def spread_gate(e):
                        pe.wait_ge(xg_ready.s, xg_ready.at(i * NE + e - 1))
                        nc.tensor.matmul(ps[:, 4 + e % 2, 0:CH], spread[:, e, :], gT[:], start=True, stop=True).then_inc(spread_done.s, 1)

                    spread_gate(0)
                    for e in range(NE):
                        if e + 1 < NE:
                            spread_gate(e + 1)
                        pe.wait_ge(xg_ready.s, xg_ready.at(i * NE + e + 1))
                        ins = nc.tensor.matmul(ps[:, 3, 0:CH], we[:, e, :], xg[:, e % 2, :], start=False, stop=(e == NE - 1))
                        ins.then_inc(xg_used.s, 1)

            @block.scalar
            def _(act):
                act.wait_ge(w_in.s, 16 * len(loads))
                with act.Fori(0, NCH) as i:
                    act.wait_ge(logit_done.s, i + 1)
                    nc.scalar.activation(lt[:], ps[0:NE, 0, 0:CH], ACT.Identity, bias=br[:]).then_inc(lt_ready.s, 1)
                act.wait_ge(shifted.s, 1)
                nc.scalar.activation(prob[:], prob[:], ACT.Exp).then_inc(exped.s, 1)
                with act.Fori(0, NCH) as i:
                    act.wait_ge(g_turned.s, i + 1)
                    nc.scalar.activation(gT[:], ps[0:NE, 2, 0:CH], ACT.Copy).then_inc(gt_ready.s, 1)

            @block.vector
            def _(dve):
                dve.sem_inc(xg_ready.s, xg_ready.credit)
                dve.sem_inc(x_done.s, x_done.credit)
                dve.wait_ge(w_in.s, 16 * len(loads))
                with dve.Fori(0, NCH) as i:
                    dve.wait_ge(lt_turned.s, i + 1)
                    nc.vector.tensor_copy(logit[:, ds(i * TPC, TPC), :], ps[0:TILE, 1, 0:TPC * NE].rearrange("p (t e) -> p t e", e=NE)).then_inc(l_out.s, 1)
                dve.wait_ge(l_out.s, NCH)
                link = Chain(dve, own.s).link
                v = nc.vector
                link(v.tensor_reduce(best[:], logit[:], AX.X, ALU.max))
                v.tensor_tensor(prob[:], logit[:], over(best), ALU.subtract).then_inc(shifted.s, 1)
                dve.wait_ge(exped.s, 1)
                link(v.tensor_reduce(best[:], prob[:], AX.X, ALU.add))
                link(v.reciprocal(best[:], best[:]))
                link(v.tensor_tensor(prob[:], prob[:], over(best), ALU.mult))
                ranks = rank[:].unsqueeze(1).to_broadcast([TILE, NT, NE])

                def choose(chosen, p, top):
                    link(v.tensor_reduce(top[:], p[:], AX.X, ALU.max))
                    link(v.tensor_tensor(chosen[:], p[:], over(top), ALU.is_equal))
                    link(v.tensor_tensor(chosen[:], chosen[:], ranks, ALU.mult))
                    link(v.tensor_reduce(best[:], chosen[:], AX.X, ALU.max))
                    link(v.tensor_tensor(chosen[:], chosen[:], over(best), ALU.is_equal))

                choose(pick, prob, top1)
                link(v.scalar_tensor_tensor(left[:], pick[:], -2.0, prob[:], ALU.mult, ALU.add))
                choose(logit, left, top2)
                link(v.tensor_tensor(pick[:], pick[:], logit[:], ALU.add))
                link(v.tensor_tensor(top1[:], top1[:], top2[:], ALU.add))
                link(v.reciprocal(top1[:], top1[:]))
                link(v.tensor_tensor(prob[:], prob[:], pick[:], ALU.mult))
                link(v.tensor_tensor(prob[:], prob[:], over(top1), ALU.mult))
                with dve.Fori(0, NCH) as i:
                    nc.vector.tensor_copy(gst[:].rearrange("p (t e) -> p t e", e=NE), prob[:, ds(i * TPC, TPC), :]).then_inc(g_staged.s, 1)
                    for e in range(NE):
                        dve.wait_ge(spread_done.s, i * NE + e + 1)
                        dve.wait_ge(xg_used.s, xg_used.at(i * NE + e - 1))
                        nc.vector.tensor_tensor(xg[:, e % 2, :], N[:, ds(i * CH, CH)], ps[:, 4 + e % 2, 0:CH], ALU.mult).then_inc(xg_ready.s, 1)
                    dve.wait_ge(xg_used.s, xg_used.at(i * NE + NE))
                    xs = X[:, ds(i * CH, CH)]
                    nc.vector.tensor_tensor(xs, xs, ps[:, 3, 0:CH], ALU.add).then_inc(x_done.s, 1)


def recurrence(k):
    nc, X, N, ps = k.nc, k.X, k.normed(), k.ps
    G = CH // B
    NG = L // G
    QUARTERS = 4
    with ExitStack() as ctx:
        sb = lambda n, s, dt=F32: k.sb(f"rnn_{n}", s, dt, ctx)
        sem = lambda n, credit=0: k.sem(f"rnn_{n}", credit)
        wx, w, v = sb("wx", [C, T]), sb("w", [C, C]), sb("v", [C, C])
        gamma, beta = sb("gamma", [C, 1]), sb("beta", [C, 1])
        stats, mv, std, a, c = sb("stats", [C, NCH * 6]), sb("mv", [C, 2]), sb("std", [C, 1]), sb("a", [C, 1]), sb("c", [C, 1])
        y = sb("y", [C, 2, CH])
        w_in, own, zeroed = sem("w_in"), sem("own"), sem("zeroed")
        wx_done, wx_out, stat_done, var_ready, std_ready, wn_ready, added, stepped, y_ready, banks = (
            sem(n, cr) for n, cr in (("wx_done", 0), ("wx_out", 2), ("stat_done", 0), ("var_ready", 0), ("std_ready", 0),
                                     ("wn_ready", 0), ("added", 2), ("stepped", 0), ("y_ready", 1), ("banks", 0)))
        loads = [(w[:], "w3_in"), (v[:], "w3_v"), (gamma[:], "gamma3"), (beta[:], "beta3")]
        steps_major = N[:].rearrange("p (t b) -> p t b", b=B)
        with nc.Block() as block:
            @block.sync
            def _(sp):
                for dst, name in loads:
                    sp.dma_start(dst, k.dram[name]).then_inc(w_in.s, 16)

            @block.vector
            def _(dve):
                nc.vector.memset(y[:], 0.0).then_inc(zeroed.s, 1)
                dve.wait_ge(w_in.s, 16 * len(loads))
                with dve.Fori(0, NCH) as i:
                    dve.wait_ge(wx_out.s, wx_out.at(i + 1))
                    nc.vector.bn_stats(stats[:, ds(i * 6, 6)], wx[:, ds(i * CH, CH)]).then_inc(stat_done.s, 1)
                dve.wait_ge(stat_done.s, NCH)
                chain = Chain(dve, own.s)
                link = chain.link
                link(nc.vector.bn_aggr(mv[:], stats[:]))
                nc.vector.tensor_scalar(std[:], mv[:, 1:2], 1e-5, None, ALU.add).then_inc(var_ready.s, 1)
                dve.wait_ge(std_ready.s, 1)
                link(nc.vector.reciprocal(a[:], std[:]))
                link(nc.vector.tensor_tensor(a[:], a[:], gamma[:], ALU.mult))
                link(nc.vector.tensor_tensor(c[:], mv[:, 0:1], a[:], ALU.mult))
                link(nc.vector.tensor_tensor(c[:], beta[:], c[:], ALU.subtract))
                for b in range(B):
                    nc.vector.tensor_scalar(steps_major[:, :, b], wx[:, b * L:(b + 1) * L], a[:, 0:1], c[:, 0:1],
                                            ALU.mult, ALU.add).then_inc(wn_ready.s, 1)

            @block.gpsimd
            def _(pool):
                pool.sem_inc(added.s, added.credit)
                with pool.Fori(0, NG // 2) as i:
                    for s in range(2):
                        pool.wait_ge(y_ready.s, y_ready.at((i * 2 + s + 1) * G))
                        xs = X[:].rearrange("p (b t) -> p b t", b=B)[:, :, ds((i * 2 + s) * G, G)]
                        nc.gpsimd.tensor_tensor(xs, xs, y[:, s, :].rearrange("p (t b) -> p b t", b=B), ALU.add).then_inc(added.s, 1)

            @block.scalar
            def _(act):
                act.sem_inc(wx_out.s, wx_out.credit)
                act.sem_inc(y_ready.s, y_ready.credit)
                with act.Fori(0, NCH // 2) as i:
                    for s in range(2):
                        act.wait_ge(wx_done.s, i * 2 + s + 1)
                        nc.scalar.activation(wx[:, ds(i * (2 * CH) + s * CH, CH)], ps[:, s, 0:CH], ACT.Copy).then_inc(wx_out.s, 1)
                act.wait_ge(var_ready.s, 1)
                nc.scalar.activation(std[:], std[:], ACT.Sqrt).then_inc(std_ready.s, 1)
                with act.Fori(0, NG // 2) as i:
                    for s in range(2):
                        act.wait_ge(added.s, added.at(i * 2 + s - 1))
                        for t in range(G):
                            act.wait_ge(stepped.s, ((i * 2 + s) * G + t + 1) * QUARTERS)
                            nc.scalar.activation(y[:, s, t * B:(t + 1) * B], ps[:, 2 + s, t * B:(t + 1) * B],
                                                 ACT.Sigmoid).then_inc(y_ready.s, 1)

            @block.tensor
            def _(pe):
                pe.wait_ge(w_in.s, 16 * len(loads))
                with pe.Fori(0, NCH // 2) as i:
                    for s in range(2):
                        pe.wait_ge(wx_out.s, wx_out.at(i * 2 + s - 1))
                        nc.tensor.matmul(ps[:, s, 0:CH], w[:], N[:, ds(i * (2 * CH) + s * CH, CH)], start=True, stop=True).then_inc(wx_done.s, 1)
                pe.wait_ge(wn_ready.s, B)
                nc.tensor.matmul(ps[:, 2, 0:CH], k.ident[:], N[:, 0:CH], start=True, stop=True)
                pe.wait_ge(zeroed.s, 1)

                def group(i, s, fill):
                    for t in range(G):
                        pe.wait_ge(y_ready.s, y_ready.at((i * 2 + s) * G + t))
                        prev = y[:, s, (t - 1) * B:t * B] if t else y[:, 1 - s, CH - B:CH]
                        for c in range(QUARTERS):
                            part = slice(c * (C // QUARTERS), (c + 1) * (C // QUARTERS))
                            nc.tensor.matmul(ps[part, 2 + s, t * B:(t + 1) * B], v[:, part], prev, start=False, stop=True,
                                             skip_group_check=True).then_inc(stepped.s, 1)
                        if t == G // 2 and fill:
                            nc.tensor.matmul(ps[:, 3 - s, 0:CH], k.ident[:], N[:, ds((i * 2 + s + 1) * CH, CH)], start=True, stop=True)

                with pe.Fori(0, NG // 2 - 1) as i:
                    group(i, 0, True)
                    group(i, 1, True)
                group(NG // 2 - 1, 0, True)
                group(NG // 2 - 1, 1, False)


def layer1(k):
    nc, X, ps = k.nc, k.X, k.ps
    WPD = HW + 2
    v = nc.vector
    with ExitStack() as ctx:
        sb = lambda n, s, dt=F32: k.sb(f"l1_{n}", s, dt, ctx)
        sem = lambda n, credit=0: k.sem(f"l1_{n}", credit)
        w_in_proj = sb("w_in_proj", [C, 2 * DI])
        w_taps, b_conv = sb("w_taps", [C, CT, 9]), sb("b_conv", [C, CT])
        w_bc, w_dt_in, w_dt = sb("w_bc", [C, ND, CT, 96]), sb("w_dt_in", [C, ND, CT, DTR]), sb("w_dt", [DTR + 1, ND, DI])
        A, D = sb("A", [C, ND, CT, NS]), sb("D", [C, ND, CT])
        ln_w, ln_b, w_out = sb("ln_w", [C, CT]), sb("ln_b", [C, CT]), sb("w_out", [C, CT, C])
        mean256, eps = sb("mean256", [C, C]), sb("eps", [C, 1])
        spread = sb("spread", [96, 2 * NS, C], BF16)
        d_mat = sb("d_mat", [C, ND, CT, C])
        xn, u, Y = sb("xn", [C, L]), sb("u", [C, CT, L]), sb("Y", [C, CT, L])
        xpad = sb("xpad", [C, WPD, WPD])
        bc, rest = sb("bc", [96, 2, CS], BF16), sb("rest", [96, CS])
        dtr, relu, e, w = sb("dtr", [DTR + 1, CS]), sb("relu", [C, CT, CS]), sb("e", [C, CT, CS]), sb("w", [C, CT, CS])
        dt, dtu = sb("dt", [C, 2, CT, CS]), sb("dtu", [C, 2, CT, CS])
        dA, dBu, h, hC = (sb(n, [C, 2, CT, CS]) for n in ("dA", "dBu", "h", "hC"))
        Cs, mid, state = sb("Cs", [C, 2, CS]), sb("mid", [96, CS], BF16), sb("state", [C, 2, CT, NS])
        one, minus_one = sb("one", [C, 1]), sb("minus_one", [C, 1])
        flat = lambda t, n, w: t[:].rearrange("p a b c -> p (a b c)")[:, 0:n * w].rearrange("p (a c) -> p a c", a=n)
        yc, sq, std, sz = flat(dA, CT, CH), flat(dBu, CT, CH), flat(h, 1, CH), flat(hC, CT, CH)

        const_ready = sem("const_ready")
        w_loaded, conv_own, end_own, a_negated, d_ready = (
            sem(n) for n in ("w_loaded", "conv_own", "end_own", "a_negated", "d_ready"))
        xn_ready, xc_done, xc_out, conv_done, sg_ready, u_ready = (
            sem("xn_ready"), sem("xc_done"), sem("xc_out", 1), sem("conv_done", 1), sem("sg_ready"), sem("u_ready"))
        proj_done, dtr_ready, abs_ready, less_one, hi_ready, rest_ready, mid_ready, split_done, delta_done = (
            sem(n) for n in ("proj_done", "dtr_ready", "abs_ready", "less_one", "hi_ready", "rest_ready", "mid_ready", "split_done", "delta_done"))
        delta_out, e_ready, w_ready, ln_ready, pool_own, dt_ready, dtu_ready = (
            sem(n, int(n == "delta_out")) for n in ("delta_out", "e_ready", "w_ready", "ln_ready", "pool_own", "dt_ready", "dtu_ready"))
        bc_done, dbu_ready, a_ready, c_copied, scan_done, hc_ready, y_done, y_out, state_zeroed = (
            sem("bc_done"), sem("dbu_ready", 2 * CT), sem("a_ready"), sem("c_copied", 2), sem("scan_done", 2 * CT),
            sem("hc_ready", 2), sem("y_done", 2), sem("y_out", 1), sem("state_zeroed"))
        m_done, yc_ready, sq_ready, var_done, std_ready, z_done, sz_ready, g_ready, out_done, x_done = (
            sem("m_done"), sem("yc_ready"), sem("sq_ready"), sem("var_done"), sem("std_ready"), sem("z_done"),
            sem("sz_ready"), sem("g_ready"), sem("out_done"), sem("x_done", 1))
        loads = [(w_in_proj[:], "w1_in"), (w_taps[:], "w1_taps"), (b_conv[:], "b1_conv"), (w_bc[:], "w1_bc"),
                 (w_dt_in[:], "w1_dt_in"), (w_dt[:], "w1_dt"), (A[:], "A_logs"), (D[:], "D1"),
                 (ln_w[:], "ln1_w"), (ln_b[:], "ln1_b"), (w_out[:], "w1_out"), (mean256[:], "mean256"),
                 (spread[:].bitcast(mybir.dt.uint16), "spread_bc")]

        def forward(kk, o, more=0):
            return o + more if kk < 2 else o * -1 + (NCS // 2 - 1 - more)

        def chunks(eng, b, body):
            for kk in range(ND):
                place = lambda o: forward(kk, o)
                start = (b * ND + kk) * NCS
                first = (kk, place(0), start, 0)
                last = (kk, place(NCS // 2 - 1), start + (NCS - 1), 1)
                before = (kk - 1, forward(kk - 1, NCS // 2 - 1), start - 1, 1) if kk > 0 else None
                after = (kk + 1, forward(kk + 1, 0), start + NCS, 0) if kk + 1 < ND else None
                body(first, before, (kk, place(0), start + 1, 1))
                with eng.Fori(0, NCS // 2 - 1) as o:
                    here, there, q = place(o), forward(kk, o, 1), start + o * 2
                    body((kk, here, q + 1, 1), (kk, here, q, 0), (kk, there, q + 2, 0))
                    body((kk, there, q + 2, 0), (kk, here, q + 1, 1), (kk, there, q + 3, 1))
                body(last, (kk, place(NCS // 2 - 1), start + (NCS - 2), 0), after)

        def u_view(ct, kk, o, p):
            p = p if kk < 2 else 1 - p
            win = u[:, ct, :].rearrange("p (hg wh wg ww) -> p hg wh wg ww", hg=4, wh=WS, wg=4)
            if kk % 2 == 0:
                return win[:, ds(o, 1), :, 2 * p:2 * p + 2, :].rearrange("p a wh wg ww -> p (a wg) wh ww")
            return win[:, 2 * p:2 * p + 2, :, ds(o, 1), :].rearrange("p hg wh a ww -> p (a hg) ww wh")

        def y_view(ct, kk, o, p):
            p = p if kk < 2 else 1 - p
            pos = "p (i j) -> p i j" if kk % 2 == 0 else "p (i j) -> p j i"
            return Y[:, ct, :].rearrange(pos, i=HW)[:, ds((o * 2 + p) * RC, RC), :]

        windows = lambda t: t.rearrange("p (g a b) -> p g a b", g=2, a=WS)
        lines = lambda t: t.rearrange("p (r c) -> p r c", c=HW)
        order = lambda t, kk: t if kk < 2 else t[:, ::-1]

        with nc.Block() as block:
            @block.sync
            def _(sp):
                for dst, name in loads:
                    sp.dma_start(dst, k.dram[name]).then_inc(w_loaded.s, 16)

            @block.tensor
            def _(pe):
                for q in (y_done,):
                    pe.sem_inc(q.s, q.credit)
                pe.wait_ge(w_loaded.s, 16 * len(loads))
                with pe.Fori(0, B) as b:
                    for ct in range(CT):
                        with pe.Fori(0, CPB) as i:
                            pe.wait_ge(xn_ready.s, b + 1)
                            pe.wait_ge(xc_out.s, xc_out.at((b * CT + ct) * CPB + i))
                            nc.tensor.matmul(ps[:, 0, 0:CH], w_in_proj[:, ct * C:(ct + 1) * C], xn[:, ds(i * CH, CH)],
                                             start=True, stop=True).then_inc(xc_done.s, 1)

                    def project(chunk, n):
                        kk, f, q, p = chunk
                        if n == 0:
                            pe.wait_ge(u_ready.s, (b + 1) * CT)
                            pe.wait_ge(delta_out.s, delta_out.at(q))
                            for ct in range(CT):
                                nc.tensor.matmul(ps[0:96, 6, 0:CS], w_bc[:, kk, ct, :], u_view(ct, kk, f, p),
                                                 start=(ct == 0), stop=(ct == CT - 1))
                        if n == 1:
                            for ct in range(CT):
                                ins = nc.tensor.matmul(ps[0:DTR, 7, 0:CS], w_dt_in[:, kk, ct, :], u_view(ct, kk, f, p),
                                                       start=(ct == 0), stop=(ct == CT - 1))
                            ins.then_inc(proj_done.s, 1)
                        if n == 4:
                            pe.wait_ge(rest_ready.s, q + 1)
                            pe.wait_ge(dtr_ready.s, q + 1)
                            for ct in range(CT):
                                ins = nc.tensor.matmul(ps[:, 6 + ct, 0:CS], w_dt[:, kk, ct * C:(ct + 1) * C], dtr[:],
                                                       start=True, stop=True)
                            ins.then_inc(delta_done.s, 1)

                    AHEAD = 3

                    def spread_bc(chunk, n):
                        kk, f, q, p = chunk
                        m = q * NS + n
                        pe.wait_ge(split_done.s, q + 1)
                        pe.wait_ge(dbu_ready.s, dbu_ready.at((m - 1) * CT))
                        pe.wait_ge(c_copied.s, c_copied.at(m - 1))
                        nc.tensor.matmul(ps[:, n % 2, 0:CS], spread[:, n, :], bc[:, p, :], start=True, stop=True)
                        nc.tensor.matmul(ps[:, 2 + n % 2, 0:CS], spread[:, NS + n, :], bc[:, p, :],
                                         start=True, stop=True).then_inc(bc_done.s, 1)

                    def scan_chunk(chunk, before, after):
                        kk, f, q, p = chunk
                        if kk == 0 and before is None:
                            for n in range(NS):
                                project(chunk, n)
                            for n in range(AHEAD):
                                spread_bc(chunk, n)
                        for n in range(NS):
                            if n + AHEAD < NS:
                                spread_bc(chunk, n + AHEAD)
                            elif after is not None:
                                spread_bc(after, n + AHEAD - NS)
                            if after is not None:
                                project(after, n)
                            if n == 0:
                                pe.wait_ge(y_out.s, y_out.at(q))
                            if n >= NS - CT - 2 and n < NS - 2:
                                ct = n - (NS - CT - 2)
                                pe.wait_ge(d_ready.s, 1)
                                nc.tensor.matmul(ps[:, 4 + ct, 0:CS], d_mat[:, kk, ct, :], u_view(ct, kk, f, p),
                                                 start=False, stop=False)
                            pe.wait_ge(hc_ready.s, hc_ready.at(q * NS + n + 1))
                            for ct in range(CT):
                                ins = nc.tensor.matmul(ps[:, 4 + ct, 0:CS], k.ident[:], hC[:, n % 2, ct, :],
                                                       start=(n == 0), stop=(n == NS - 1))
                            ins.then_inc(y_done.s, 1)

                    chunks(pe, b, scan_chunk)
                    with pe.Fori(0, CPB) as i:
                        it = b * CPB + i
                        pe.wait_ge(y_out.s, y_out.at((b + 1) * (ND * NCS)))
                        pe.wait_ge(x_done.s, x_done.at(it))
                        for ct in range(CT):
                            ins = nc.tensor.matmul(ps[:, 0, 0:CH], mean256[:], Y[:, ct, ds(i * CH, CH)],
                                                   start=(ct == 0), stop=(ct == CT - 1))
                        ins.then_inc(m_done.s, 1)
                        for ct in range(CT):
                            ins = nc.tensor.matmul(ps[:, 2 + ct, 0:CH], w_in_proj[:, DI + ct * C:DI + (ct + 1) * C],
                                                   xn[:, ds(i * CH, CH)], start=True, stop=True)
                        ins.then_inc(z_done.s, 1)
                        pe.wait_ge(sq_ready.s, it + 1)
                        for ct in range(CT):
                            ins = nc.tensor.matmul(ps[:, 1, 0:CH], mean256[:], sq[:, ct, :], start=(ct == 0), stop=(ct == CT - 1))
                        ins.then_inc(var_done.s, 1)
                        pe.wait_ge(g_ready.s, it + 1)
                        for ct in range(CT):
                            ins = nc.tensor.matmul(ps[:, 4, 0:CH], w_out[:, ct, :], sz[:, ct, :], start=(ct == 0), stop=(ct == CT - 1))
                        ins.then_inc(out_done.s, 1)

            @block.scalar
            def _(act):
                for q in (xc_out, c_copied, delta_out):
                    act.sem_inc(q.s, q.credit)
                act.wait_ge(w_loaded.s, 16 * len(loads))
                nc.scalar.activation(A[:], A[:], ACT.Exp).then_inc(a_negated.s, 1)
                with act.Fori(0, B) as b:
                    for ct in range(CT):
                        with act.Fori(0, CPB) as i:
                            act.wait_ge(xc_done.s, (b * CT + ct) * CPB + i + 1)
                            act.wait_ge(conv_done.s, conv_done.at(b * CT + ct))
                            nc.scalar.activation(xpad[:, ds(i * 8 + 1, 8), 1:1 + HW], ps[:, 0, 0:CH].rearrange("p (r w) -> p r w", w=HW),
                                                 ACT.Copy).then_inc(xc_out.s, 1)
                        act.wait_ge(conv_done.s, conv_done.at(b * CT + ct + 1))
                        nc.scalar.activation(Y[:, ct, :], u[:, ct, :], ACT.Sigmoid, bias=b_conv[:, ct:ct + 1]).then_inc(sg_ready.s, 1)

                    def set_up(chunk, n):
                        kk, f, q, p = chunk
                        if n == 2:
                            act.wait_ge(proj_done.s, q + 1)
                            nc.scalar.activation(bc[:, p, :], ps[0:96, 6, 0:CS], ACT.Copy).then_inc(hi_ready.s, 1)
                        if n == 3:
                            nc.scalar.activation(dtr[0:DTR, :], ps[0:DTR, 7, 0:CS], ACT.Copy).then_inc(dtr_ready.s, 1)
                        if n == 4:
                            act.wait_ge(rest_ready.s, q + 1)
                            nc.scalar.activation(mid[:], rest[:], ACT.Copy)
                            nc.scalar.activation(bc[32:64, p, :], rest[32:64, :], ACT.Copy).then_inc(mid_ready.s, 1)
                        if n == 6:
                            act.wait_ge(delta_done.s, q + 1)
                            nc.scalar.activation(e[:], ps[:, 6:6 + CT, 0:CS], ACT.Abs).then_inc(abs_ready.s, 1)
                        if n == 7:
                            act.wait_ge(abs_ready.s, q + 1)
                            nc.scalar.activation(e[:], e[:], ACT.Exp, scale=-1.0).then_inc(e_ready.s, 1)
                        if n == 8:
                            act.wait_ge(e_ready.s, q + 1)
                            nc.scalar.activation(w[:], e[:], ACT.Identity, bias=one[:]).then_inc(w_ready.s, 1)
                        if n == 9:
                            act.wait_ge(w_ready.s, q + 1)
                            nc.scalar.activation(dtu[:, p], w[:], ACT.Identity, bias=minus_one[:]).then_inc(less_one.s, 1)
                        if n == 10:
                            nc.scalar.activation(relu[:], ps[:, 6:6 + CT, 0:CS], ACT.Relu).then_inc(delta_out.s, 1)
                        if n == 11:
                            nc.scalar.activation(dt[:, p], w[:], ACT.Ln).then_inc(ln_ready.s, 1)

                    def scan_chunk(chunk, before, after):
                        kk, f, q, p = chunk
                        if kk == 0 and before is None:
                            act.wait_ge(const_ready.s, 1)
                            for n in range(NS):
                                set_up(chunk, n)
                        for n in range(NS):
                            m = q * NS + n
                            act.wait_ge(a_negated.s, 2)
                            act.wait_ge(dt_ready.s, q + 1)
                            act.wait_ge(scan_done.s, scan_done.at((m - 1) * CT))
                            for ct in range(CT):
                                ins = nc.scalar.activation(dA[:, n % 2, ct, :], dt[:, p, ct, :], ACT.Exp,
                                                           scale=A[:, kk, ct, n:n + 1])
                            ins.then_inc(a_ready.s, 1)
                            act.wait_ge(bc_done.s, m + 1)
                            act.wait_ge(hc_ready.s, hc_ready.at(m - 1))
                            nc.scalar.activation(Cs[:, n % 2, :], ps[:, 2 + n % 2, 0:CS], ACT.Copy).then_inc(c_copied.s, 1)
                            if after is not None:
                                set_up(after, n)

                    chunks(act, b, scan_chunk)
                    with act.Fori(0, CPB) as i:
                        it = b * CPB + i
                        act.wait_ge(z_done.s, it + 1)
                        act.wait_ge(x_done.s, x_done.at(it))
                        nc.scalar.activation(sz, ps[:, 2:4, 0:CH], ACT.Sigmoid).then_inc(sz_ready.s, 1)
                        act.wait_ge(yc_ready.s, it + 1)
                        nc.scalar.activation(sq, yc, ACT.Square).then_inc(sq_ready.s, 1)
                        act.wait_ge(var_done.s, it + 1)
                        nc.scalar.activation(std[:, 0, :], ps[:, 1, 0:CH], ACT.Sqrt, bias=eps[:]).then_inc(std_ready.s, 1)

            @block.gpsimd
            def _(pool):
                pool.sem_inc(hc_ready.s, hc_ready.credit)
                with pool.Fori(0, B) as b:

                    def set_up(chunk, n):
                        kk, f, q, p = chunk
                        if n == 9:
                            pool.wait_ge(less_one.s, q + 1)
                            nc.gpsimd.tensor_tensor(e[:], dtu[:, p], e[:], ALU.subtract).then_inc(pool_own.s, 1)
                        if n == 10:
                            pool.wait_ge(delta_out.s, delta_out.at(q + 1))
                            pool.wait_ge(pool_own.s, q * 2 + 1)
                            nc.gpsimd.tensor_tensor(e[:], relu[:], e[:], ALU.subtract).then_inc(pool_own.s, 1)
                        if n == 12:
                            pool.wait_ge(ln_ready.s, q + 1)
                            pool.wait_ge(pool_own.s, q * 2 + 2)
                            nc.gpsimd.tensor_tensor(dt[:, p], dt[:, p], e[:], ALU.add).then_inc(dt_ready.s, 1)

                    def scan_chunk(chunk, before, after):
                        kk, f, q, p = chunk
                        if kk == 0 and before is None:
                            for n in range(NS):
                                set_up(chunk, n)
                        last = CS - 1 if kk < 2 else 0
                        for n in range(NS):
                            m = q * NS + n
                            pool.wait_ge(scan_done.s, scan_done.at((m + 1) * CT))
                            pool.wait_ge(c_copied.s, c_copied.at(m + 1))
                            pool.wait_ge(y_done.s, y_done.at(m - 1))
                            nc.gpsimd.tensor_tensor(hC[:, n % 2], h[:, n % 2], Cs[:, n % 2, :].unsqueeze(1).to_broadcast([C, CT, CS]),
                                                    ALU.mult)
                            nc.gpsimd.tensor_copy(state[:, kk % 2, :, n:n + 1], h[:, n % 2, :, last:last + 1]).then_inc(hc_ready.s, 1)
                            if after is not None:
                                set_up(after, n)

                    chunks(pool, b, scan_chunk)

            @block.vector
            def _(dve):
                for q in (conv_done, dbu_ready, scan_done, y_out, x_done):
                    dve.sem_inc(q.s, q.credit)
                v.memset(xpad[:], 0.0)
                v.memset(eps[:], 1e-5)
                v.memset(one[:], 1.0)
                v.memset(dtr[:], 1.0)
                v.memset(minus_one[:], -1.0).then_inc(const_ready.s, 1)
                dve.wait_ge(a_negated.s, 1)
                v.tensor_scalar(A[:], A[:], -1.0, None, ALU.mult).then_inc(a_negated.s, 1)
                for kk in range(ND):
                    for ct in range(CT):
                        ins = v.tensor_scalar(d_mat[:, kk, ct, :], k.ident[:], D[:, kk, ct:ct + 1], None, ALU.mult)
                ins.then_inc(d_ready.s, 1)
                PER_B = 1 + CT * 10
                with dve.Fori(0, B) as b:
                    chain = Chain(dve, conv_own.s, b * PER_B)
                    chain.link(v.tensor_scalar(xn[:], X[:, ds(b * L, L)], k.gn_nmean[:, ds(b, 1)], k.gn_rstd[:, ds(b, 1)],
                                               ALU.add, ALU.mult))
                    dve.sem_inc(xn_ready.s, 1)
                    for ct in range(CT):
                        dve.wait_ge(xc_out.s, xc_out.at((b * CT + ct + 1) * CPB))
                        image = u[:, ct, :].rearrange("p (r c) -> p r c", c=HW)
                        for tap in range(9):
                            src = xpad[:, tap // 3:tap // 3 + HW, tap % 3:tap % 3 + HW]
                            if tap == 0:
                                ins = v.tensor_scalar(image, src, w_taps[:, ct, 0:1], None, ALU.mult)
                            else:
                                ins = v.scalar_tensor_tensor(image, src, w_taps[:, ct, tap:tap + 1], image, ALU.mult, ALU.add)
                            chain.link(ins)
                        dve.sem_inc(conv_done.s, 1)
                        dve.wait_ge(sg_ready.s, b * CT + ct + 1)
                        chain.link(v.scalar_tensor_tensor(u[:, ct, :], u[:, ct, :], b_conv[:, ct:ct + 1], Y[:, ct, :],
                                                          ALU.add, ALU.mult))
                        dve.sem_inc(u_ready.s, 1)
                    assert chain.n == PER_B

                    def zero_states(kk, done):
                        dve.wait_ge(hc_ready.s, hc_ready.at(done))
                        v.memset(state[:, kk % 2], 0.0).then_inc(state_zeroed.s, 1)

                    def set_up(chunk, n):
                        kk, f, q, p = chunk
                        if n == 3:
                            dve.wait_ge(hi_ready.s, q + 1)
                            v.tensor_tensor(rest[:], ps[0:96, 6, 0:CS], bc[:, p, :], ALU.subtract).then_inc(rest_ready.s, 1)
                        if n == 6:
                            dve.wait_ge(mid_ready.s, q + 1)
                            v.tensor_tensor(bc[64:96, p, :], rest[64:96, :], mid[64:96, :], ALU.subtract).then_inc(split_done.s, 1)
                        if n == NS - 2:
                            dve.wait_ge(dt_ready.s, q + 1)
                            for ct in range(CT):
                                ins = v.tensor_tensor(windows(dtu[:, p, ct, :]), windows(dt[:, p, ct, :]), u_view(ct, kk, f, p), ALU.mult)
                            ins.then_inc(dtu_ready.s, 1)

                    def add_output(chunk):
                        kk, f, q, p = chunk
                        dve.wait_ge(y_done.s, y_done.at((q + 1) * NS))
                        dve.wait_ge(y_out.s, y_out.at(q))
                        for ct in range(CT):
                            dst, src = y_view(ct, kk, f, p), lines(ps[:, 4 + ct, 0:CS])
                            if kk == 0:
                                ins = v.tensor_copy(dst, src)
                            else:
                                ins = v.tensor_tensor(dst, dst, src, ALU.add)
                        ins.then_inc(y_out.s, 1)

                    def weigh_b(chunk, n, ct):
                        kk, f, q, p = chunk
                        m = q * NS + n
                        dve.wait_ge(dtu_ready.s, q + 1)
                        dve.wait_ge(bc_done.s, m + 1)
                        dve.wait_ge(scan_done.s, scan_done.at((m - 2) * CT + ct + 1))
                        v.tensor_tensor(dBu[:, n % 2, ct, :], dtu[:, p, ct, :], ps[:, n % 2, 0:CS], ALU.mult).then_inc(dbu_ready.s, 1)

                    def scan_chunk(chunk, before, after):
                        kk, f, q, p = chunk
                        if kk == 0 and before is None:
                            zero_states(0, q * NS)
                            for n in range(NS):
                                set_up(chunk, n)
                            for ct in range(CT):
                                weigh_b(chunk, 0, ct)
                        for n in range(NS):
                            m, s = q * NS + n, n % 2
                            for ct in range(CT):
                                dve.wait_ge(dbu_ready.s, dbu_ready.at(m * CT + ct + 1))
                                dve.wait_ge(a_ready.s, m + 1)
                                dve.wait_ge(hc_ready.s, hc_ready.at(m - 1))
                                dve.wait_ge(state_zeroed.s, b * ND + kk + 1)
                                v.tensor_tensor_scan(order(h[:, s, ct, :], kk), order(dA[:, s, ct, :], kk),
                                                     order(dBu[:, s, ct, :], kk), state[:, kk % 2, ct, n:n + 1],
                                                     ALU.mult, ALU.add).then_inc(scan_done.s, 1)
                                if n + 1 < NS:
                                    weigh_b(chunk, n + 1, ct)
                                elif after is not None:
                                    weigh_b(after, 0, ct)
                            if n == 1 and before is not None:
                                add_output(before)
                            if after is not None:
                                set_up(after, n)
                                if n == 8 and after[0] != kk:
                                    zero_states(kk + 1, q * NS)
                        if after is None:
                            add_output(chunk)

                    chunks(dve, b, scan_chunk)
                    PER_I = 5
                    with dve.Fori(0, CPB) as i:
                        it = b * CPB + i
                        chain = Chain(dve, end_own.s, it * PER_I)
                        over = lambda t: t.unsqueeze(1).to_broadcast([C, CT, CH])
                        dve.wait_ge(m_done.s, it + 1)
                        v.tensor_tensor(yc, Y[:, :, ds(i * CH, CH)], over(ps[:, 0, 0:CH]), ALU.subtract).then_inc(yc_ready.s, 1)
                        dve.wait_ge(std_ready.s, it + 1)
                        chain.link(v.reciprocal(std[:, 0, :], std[:, 0, :]))
                        chain.link(v.tensor_tensor(yc, yc, over(std[:, 0, :]), ALU.mult))
                        for ct in range(CT):
                            chain.link(v.tensor_scalar(yc[:, ct, :], yc[:, ct, :], ln_w[:, ct:ct + 1], ln_b[:, ct:ct + 1], ALU.mult, ALU.add))
                        dve.wait_ge(sz_ready.s, it + 1)
                        chain.link(v.tensor_tensor(sz, sz, ps[:, 2:4, 0:CH], ALU.mult))
                        v.tensor_tensor(sz, sz, yc, ALU.mult).then_inc(g_ready.s, 1)
                        assert chain.n == PER_I
                        dve.wait_ge(out_done.s, it + 1)
                        xs = X[:, ds(b * L + i * CH, CH)]
                        v.tensor_tensor(xs, xs, ps[:, 4, 0:CH], ALU.add).then_inc(x_done.s, 1)


PHASES = {"load": load_x, "store": store_x, "gn0": lambda k: gn_stats(k, "gn0"), "l0": layer0,
          "ln2a": lambda k: layer_norm(k, "ln2a", 1e-5), "a2": lambda k: attention(k, "a2"),
          "gn1": lambda k: gn_stats(k, "gn1"), "l1": layer1,
          "ln2f": lambda k: layer_norm(k, "ln2f", 1e-5), "moe": experts,
          "ln3f": lambda k: layer_norm(k, "ln3f", 1e-5), "rnn": recurrence,
          "ln3a": lambda k: layer_norm(k, "ln3a", 1e-5), "a3": lambda k: attention_heads(k, "a3")}
ORDER = ["load", "gn0", "l0", "gn1", "l1", "ln2a", "a2", "ln2f", "moe", "ln3a", "a3", "ln3f", "rnn", "store"]


def build(nc, dram):
    with ExitStack() as ctx:
        k = Core(nc, ctx, dram)
        for name in ORDER:
            PHASES[name](k)
            k.end_phase()


def arrange(inputs):
    import numpy as np
    f = {n: np.ascontiguousarray(v) for n, v in inputs.items()}
    t = np.ascontiguousarray
    a = {"x": f["x"].reshape(T, C)}
    a["ident"] = np.eye(C, dtype=np.float32)
    a["mean_mat"] = np.full((C, C), 1.0 / C, np.float32)
    a["group_mat"] = np.kron(np.eye(C // 4), np.full((4, 4), 0.25)).astype(np.float32)
    a["w0_qkv"], a["b0_qkv"] = t(f["L0_conv_qkv_w"].T), t(f["L0_conv_qkv_b"].reshape(3, C).T)
    a["w0_proj"], a["b0_proj"] = t(f["L0_conv_proj_w"].T), f["L0_conv_proj_b"].reshape(C, 1)
    a["head_scale0"] = np.kron(np.eye(NH0), np.full((HD0, 1), HD0 ** -0.5)).astype(np.float32)
    ki = np.arange(8)[None, None, :, None] - np.arange(2)[:, None, None, None]
    kj = np.arange(WP)[None, None, None, :] - np.arange(HW)[None, :, None, None]
    ki, kj = (np.broadcast_to(v, (2, HW, 8, WP)).reshape(TILE, WIN) for v in (ki, kj))
    inside = (ki >= 0) & (ki < KS) & (kj >= 0) & (kj < KS)
    a["wmask"] = np.where(inside, 0.0, NEG).astype(np.float32)
    laid = f["L0_conv_rpb"][:, np.clip(ki, 0, KS - 1) + PAD, np.clip(kj, 0, KS - 1) + PAD]
    a["rpb_laid"] = t(laid.transpose(1, 0, 2))
    a["w1_in"] = t(f["L1_conv_W_in"].T)
    a["w1_taps"] = t(f["L1_conv_conv_w"].reshape(CT, C, 9).transpose(1, 0, 2))
    a["b1_conv"] = t(f["L1_conv_conv_b"].reshape(CT, C).T)
    xp = f["L1_conv_x_proj_w"].reshape(ND, DTR + 2 * NS, CT, C).transpose(3, 0, 2, 1)
    a["w1_dt_in"] = t(xp[..., :DTR])
    a["w1_bc"] = t(np.concatenate([xp[..., DTR:]] * 3, axis=-1))
    a["w1_dt"] = t(np.concatenate([f["L1_conv_dt_proj_w"].transpose(2, 0, 1), f["L1_conv_dt_proj_b"].reshape(1, ND, DI)]))
    a["A_logs"] = t(f["L1_conv_A_logs"].reshape(ND, CT, C, NS).transpose(2, 0, 1, 3))
    a["D1"] = t(f["L1_conv_Ds"].reshape(ND, CT, C).transpose(2, 0, 1))
    a["ln1_w"], a["ln1_b"] = t(f["L1_conv_ln_w"].reshape(CT, C).T), t(f["L1_conv_ln_b"].reshape(CT, C).T)
    a["w1_out"] = t(f["L1_conv_W_out"].reshape(C, CT, C).transpose(2, 1, 0))
    a["mean256"] = np.full((C, C), 1.0 / DI, np.float32)
    one = np.tile(np.eye(2 * NS, dtype=np.float32), (3, 1))
    a["spread_bc"] = np.repeat(one[:, :, None], C, axis=2).astype(np.uint16) * np.uint16(0x3F80)
    key = np.arange(CH)[None, None, :]
    query = np.arange(TILE)[:, None, None] + TILE * np.arange(TPC)[None, :, None]
    a["causal_masks"] = np.where(key <= query, 0.0, NEG).astype(np.float32)
    a["w2_qkv"] = np.concatenate([f["L2_attn_Wq"], f["L2_attn_Wk"], f["L2_attn_Wv"]], axis=1)
    a["w3_qkv"], a["w3_proj"] = f["L3_attn_w_attn"], f["L3_attn_w_proj"]
    BNEG, ONE = np.uint16(0xF149), np.uint16(0x3F80)
    a["identb"] = np.eye(TILE, dtype=np.uint16) * ONE
    later = np.triu(np.ones((TILE, TILE), np.uint16), 1)
    a["tri"], a["triT"] = later * BNEG, t(later.T * BNEG)
    a["full"] = np.full((TILE, TILE), BNEG, np.uint16)
    a["fold"] = np.tile(np.eye(32, HD3 + 1, dtype=np.float32), (4, 1))
    a["w2_router"], a["b2_router"] = f["L2_ffn_router_w"], f["L2_ffn_router_b"].reshape(NE, 1)
    a["w2_expert"], a["b2_expert"] = t(f["L2_ffn_expert_w"].transpose(1, 0, 2)), f["L2_ffn_expert_b"]
    a["spread8"] = np.repeat(np.eye(NE, dtype=np.float32)[:, :, None], C, axis=2)
    a["rank8"] = np.broadcast_to(np.arange(NE, 0, -1).astype(np.float32), (TILE, NE)).copy()
    a["w3_in"], a["w3_v"] = t(f["L3_ffn_W"].T), t(f["L3_ffn_V"].T)
    a["gamma3"], a["beta3"] = f["L3_ffn_gamma"].reshape(C, 1), f["L3_ffn_beta"].reshape(C, 1)
    return a


def kernel(**inputs):
    import concourse.bacc as _bacc
    from concourse import mybir as _mybir
    from concourse.bass_utils import run_bass_kernel_spmd as _run

    nc = _bacc.Bacc("TRN2", target_bir_lowering=False, num_devices=1)
    arrays, dram = {}, {}
    for name, a in arrange(inputs).items():
        arrays[f"in_{name}_dram"] = a
        dram[name] = nc.dram_tensor(f"in_{name}_dram", a.shape, _mybir.dt.from_np(a.dtype), kind="ExternalInput").ap()
    dram["out"] = nc.dram_tensor("out_0_dram", (T, C), _mybir.dt.float32, kind="ExternalOutput").ap()
    build(nc, dram)
    r = _run(nc, [arrays], core_ids=[0])
    return r.results[0]["out_0_dram"].reshape(B, HW, HW, C)
```
